# Optimizing a Trainium2 kernel written in Bass

```python
import numpy as np
import jax
import jax.numpy as jnp

def _softmax(x, axis=-1):
    return jax.nn.softmax(x, axis=axis)

def _gelu(x):
    return jax.nn.gelu(x, approximate=True)

def _silu(x):
    return jax.nn.silu(x)

def _sigmoid(x):
    return jax.nn.sigmoid(x)

def _layernorm(x, axis=-1, eps=1e-05):
    m = jnp.mean(x, axis=axis, keepdims=True)
    v = jnp.var(x, axis=axis, keepdims=True)
    return (x - m) / jnp.sqrt(v + eps)

def _scatter_add(tgt, idx, src, axis=0):
    return tgt.at[idx].add(src)

def _segment_sum(src, seg, n):
    return jax.ops.segment_sum(src, seg, n)
kernel_name = 'mk_vit_tower_d1_tok_img1024_r4_da5a25'

def setup_inputs(seed: int=0):
    np.random.seed(seed)
    _w = jnp.asarray

    def _rec_inputs():
        import jax
        import jax.numpy as jnp
        _rk = jax.random.key(seed)
        x = -0.00016672 + 0.999947 * jax.random.normal(jax.random.fold_in(_rk, 1), (16, 3, 96, 96), jnp.float32)
        return x
    x = _rec_inputs()

    def _L0_tok_setup():
        import jax, jax.numpy as jnp
        import numpy as np
        P = 16
        Q_EPS = 1e-05

        def _rms_norm(x):
            return x * jax.lax.rsqrt(jnp.mean(x * x, axis=-1, keepdims=True) + 1e-06)

        def _act_quant(x):
            scale = 127.0 / jnp.clip(jnp.max(jnp.abs(x), axis=-1, keepdims=True), Q_EPS, None)
            return jnp.clip(jnp.round(x * scale), -128.0, 127.0) / scale

        def _weight_quant(w):
            scale = 1.0 / jnp.clip(jnp.mean(jnp.abs(w)), Q_EPS, None)
            return jnp.clip(jnp.round(w * scale), -1.0, 1.0) / scale
        key = jax.random.key(seed)
        k1, k2, k3, k4 = jax.random.split(key, 4)
        B, C, H, W = (64, 3, 96, 96)
        D = 256
        Din = P * P * C
        return {'x': jax.random.normal(k1, (B, C, H, W), jnp.float32), 'weight': jax.random.normal(k2, (D, Din), jnp.float32) * 0.02, 'class_token': jax.random.normal(k3, (1, 1, D), jnp.float32), 'pos_embedding': jax.random.normal(k4, (1, 1, D), jnp.float32)}
    _L0_tok_all = _L0_tok_setup()
    _L0_tok_in = {k: v for k, v in _L0_tok_all.items() if k in ('weight', 'class_token', 'pos_embedding')}
    del _L0_tok_all

    def _L0_attn_setup():
        import jax, jax.numpy as jnp
        import numpy as np
        B, S, D = (2, 512, 256)
        H, DH = (16, 64)
        DQL, DKVL = (128, 128)
        DR = 64
        TOPK = 64
        LN_EPS = 1e-05
        ROPE_BASE = 10000.0

        def _rope_tables(seq_len, dim):
            inv_freq = 1.0 / ROPE_BASE ** (np.arange(0, dim, 2, dtype=np.float32) / dim)
            t = np.arange(seq_len, dtype=np.float32)
            freqs = np.outer(t, inv_freq)
            cos = np.concatenate([np.cos(freqs), np.cos(freqs)], -1)[:, ::2]
            sin = np.concatenate([np.sin(freqs), np.sin(freqs)], -1)[:, ::2]
            return (jnp.asarray(cos), jnp.asarray(sin))

        def _apply_rope_subspace(x, d_rope):
            s = x.shape[-2]
            cos, sin = _rope_tables(s, d_rope)
            xr, xp = (x[..., :d_rope], x[..., d_rope:])
            e, o = (xr[..., 0::2], xr[..., 1::2])
            rot = jnp.stack([e * cos - o * sin, e * sin + o * cos], axis=-1).reshape(xr.shape)
            return jnp.concatenate([rot, xp], axis=-1)

        def _reference_tuple_inner(x, w_down_q, w_down_kv, w_up_q, w_up_k, w_up_v, w_out, ln_scale, ln_bias):
            b, s, d = x.shape
            residual = x
            mu = jnp.mean(x, axis=-1, keepdims=True)
            var = jnp.mean((x - mu) ** 2, axis=-1, keepdims=True)
            h = (x - mu) * jax.lax.rsqrt(var + LN_EPS) * ln_scale + ln_bias
            c_q = h @ w_down_q.T
            c_kv = h @ w_down_kv.T
            q = (c_q @ w_up_q.T).reshape(b, s, H, DH).transpose(0, 2, 1, 3)
            k = (c_kv @ w_up_k.T).reshape(b, s, H, DH).transpose(0, 2, 1, 3)
            v = (c_kv @ w_up_v.T).reshape(b, s, H, DH).transpose(0, 2, 1, 3)
            q = _apply_rope_subspace(q, DR)
            k = _apply_rope_subspace(k, DR)
            scale = 1.0 / np.sqrt(DH).astype(np.float32)
            scores = jnp.einsum('bhqd,bhkd->bhqk', q, k) * scale
            _, indices = jax.lax.top_k(scores, min(TOPK, s))
            attn = jax.nn.softmax(scores, axis=-1)
            out = jnp.einsum('bhqk,bhkd->bhqd', attn, v)
            out = out.transpose(0, 2, 1, 3).reshape(b, s, H * DH)
            out = out @ w_out.T + residual
            return (out, indices.astype(jnp.int64))
        key = jax.random.key(seed)
        ks = jax.random.split(key, 7)
        init = lambda k, shape: jax.random.normal(k, shape, jnp.float32) * 0.02
        return {'x': jax.random.normal(ks[0], (B, S, D), jnp.float32), 'w_down_q': init(ks[1], (DQL, D)), 'w_down_kv': init(ks[2], (DKVL, D)), 'w_up_q': init(ks[3], (H * DH, DQL)), 'w_up_k': init(ks[4], (H * DH, DKVL)), 'w_up_v': init(ks[5], (H * DH, DKVL)), 'w_out': init(ks[6], (D, H * DH)), 'ln_scale': jnp.ones((D,), jnp.float32), 'ln_bias': jnp.zeros((D,), jnp.float32)}
    _L0_attn_all = _L0_attn_setup()
    _L0_attn_in = {k: v for k, v in _L0_attn_all.items() if k in ('w_down_q', 'w_down_kv', 'w_up_q', 'w_up_k', 'w_up_v', 'w_out', 'ln_scale', 'ln_bias')}
    del _L0_attn_all

    def _L0_ffn_setup():
        import jax, jax.numpy as jnp
        import numpy as np
        B, S, D, E, H, K = (64, 512, 256, 32, 1024, 8)
        key = jax.random.key(seed)
        k0, k1, k2, k3 = jax.random.split(key, 4)
        x = jax.random.normal(k0, (B, S, D), jnp.float32)
        gate_w = jax.random.normal(k1, (E, D), jnp.float32) * (1.0 / np.sqrt(D))
        gate_b = jnp.zeros((E,), jnp.float32)
        w1 = jax.random.normal(k2, (E, D + 1, H), jnp.float32) * (1.0 / np.sqrt(D + 1))
        w2 = jax.random.normal(k3, (E, H + 1, D), jnp.float32) * (1.0 / np.sqrt(H + 1))
        return {'x': x, 'gate_w': gate_w, 'gate_b': gate_b, 'w1': w1, 'w2': w2}
    _L0_ffn_all = _L0_ffn_setup()
    _L0_ffn_in = {k: v for k, v in _L0_ffn_all.items() if k in ('gate_w', 'gate_b', 'w1', 'w2')}
    del _L0_ffn_all
    return {'x': x, 'L0_tok_weight': _L0_tok_in['weight'], 'L0_tok_class_token': _L0_tok_in['class_token'], 'L0_tok_pos_embedding': _L0_tok_in['pos_embedding'], 'L0_attn_w_down_q': _L0_attn_in['w_down_q'], 'L0_attn_w_down_kv': _L0_attn_in['w_down_kv'], 'L0_attn_w_up_q': _L0_attn_in['w_up_q'], 'L0_attn_w_up_k': _L0_attn_in['w_up_k'], 'L0_attn_w_up_v': _L0_attn_in['w_up_v'], 'L0_attn_w_out': _L0_attn_in['w_out'], 'L0_attn_ln_scale': _L0_attn_in['ln_scale'], 'L0_attn_ln_bias': _L0_attn_in['ln_bias'], 'L0_ffn_gate_w': _L0_ffn_in['gate_w'], 'L0_ffn_gate_b': _L0_ffn_in['gate_b'], 'L0_ffn_w1': _L0_ffn_in['w1'], 'L0_ffn_w2': _L0_ffn_in['w2']}

def reference(x, L0_tok_weight, L0_tok_class_token, L0_tok_pos_embedding, L0_attn_w_down_q, L0_attn_w_down_kv, L0_attn_w_up_q, L0_attn_w_up_k, L0_attn_w_up_v, L0_attn_w_out, L0_attn_ln_scale, L0_attn_ln_bias, L0_ffn_gate_w, L0_ffn_gate_b, L0_ffn_w1, L0_ffn_w2):
    import jax
    import jax.numpy as jnp

    def _L0_tok_ref(x, weight, class_token, pos_embedding):
        import jax, jax.numpy as jnp
        import numpy as np
        P = 16
        Q_EPS = 1e-05

        def _rms_norm(x):
            return x * jax.lax.rsqrt(jnp.mean(x * x, axis=-1, keepdims=True) + 1e-06)

        def _act_quant(x):
            scale = 127.0 / jnp.clip(jnp.max(jnp.abs(x), axis=-1, keepdims=True), Q_EPS, None)
            return jnp.clip(jnp.round(x * scale), -128.0, 127.0) / scale

        def _weight_quant(w):
            scale = 1.0 / jnp.clip(jnp.mean(jnp.abs(w)), Q_EPS, None)
            return jnp.clip(jnp.round(w * scale), -1.0, 1.0) / scale
        B, C, H, W = x.shape
        h, w = (H // P, W // P)
        patches = x.reshape(B, C, h, P, w, P).transpose(0, 2, 4, 3, 5, 1).reshape(B, h * w, P * P * C)
        xn = _rms_norm(patches)
        xq = xn + jax.lax.stop_gradient(_act_quant(xn) - xn)
        wq = weight + jax.lax.stop_gradient(_weight_quant(weight) - weight)
        proj = jnp.einsum('bnd,od->bno', xq, wq)
        cls = jnp.broadcast_to(class_token, (B, 1, proj.shape[-1]))
        out = jnp.concatenate([cls, proj], axis=1) + pos_embedding
        return out

    def _L0_attn_ref(x, w_down_q, w_down_kv, w_up_q, w_up_k, w_up_v, w_out, ln_scale, ln_bias):
        import jax, jax.numpy as jnp
        import numpy as np
        B, S, D = (2, 512, 256)
        H, DH = (16, 64)
        DQL, DKVL = (128, 128)
        DR = 64
        TOPK = 64
        LN_EPS = 1e-05
        ROPE_BASE = 10000.0

        def _rope_tables(seq_len, dim):
            inv_freq = 1.0 / ROPE_BASE ** (np.arange(0, dim, 2, dtype=np.float32) / dim)
            t = np.arange(seq_len, dtype=np.float32)
            freqs = np.outer(t, inv_freq)
            cos = np.concatenate([np.cos(freqs), np.cos(freqs)], -1)[:, ::2]
            sin = np.concatenate([np.sin(freqs), np.sin(freqs)], -1)[:, ::2]
            return (jnp.asarray(cos), jnp.asarray(sin))

        def _apply_rope_subspace(x, d_rope):
            s = x.shape[-2]
            cos, sin = _rope_tables(s, d_rope)
            xr, xp = (x[..., :d_rope], x[..., d_rope:])
            e, o = (xr[..., 0::2], xr[..., 1::2])
            rot = jnp.stack([e * cos - o * sin, e * sin + o * cos], axis=-1).reshape(xr.shape)
            return jnp.concatenate([rot, xp], axis=-1)

        def _reference_tuple_inner(x, w_down_q, w_down_kv, w_up_q, w_up_k, w_up_v, w_out, ln_scale, ln_bias):
            b, s, d = x.shape
            residual = x
            mu = jnp.mean(x, axis=-1, keepdims=True)
            var = jnp.mean((x - mu) ** 2, axis=-1, keepdims=True)
            h = (x - mu) * jax.lax.rsqrt(var + LN_EPS) * ln_scale + ln_bias
            c_q = h @ w_down_q.T
            c_kv = h @ w_down_kv.T
            q = (c_q @ w_up_q.T).reshape(b, s, H, DH).transpose(0, 2, 1, 3)
            k = (c_kv @ w_up_k.T).reshape(b, s, H, DH).transpose(0, 2, 1, 3)
            v = (c_kv @ w_up_v.T).reshape(b, s, H, DH).transpose(0, 2, 1, 3)
            q = _apply_rope_subspace(q, DR)
            k = _apply_rope_subspace(k, DR)
            scale = 1.0 / np.sqrt(DH).astype(np.float32)
            scores = jnp.einsum('bhqd,bhkd->bhqk', q, k) * scale
            _, indices = jax.lax.top_k(scores, min(TOPK, s))
            attn = jax.nn.softmax(scores, axis=-1)
            out = jnp.einsum('bhqk,bhkd->bhqd', attn, v)
            out = out.transpose(0, 2, 1, 3).reshape(b, s, H * DH)
            out = out @ w_out.T + residual
            return (out, indices.astype(jnp.int64))
        return _reference_tuple_inner(x, w_down_q, w_down_kv, w_up_q, w_up_k, w_up_v, w_out, ln_scale, ln_bias)[0]

    def _L0_ffn_ref(x, gate_w, gate_b, w1, w2):
        import jax, jax.numpy as jnp
        import numpy as np
        B, S, D, E, H, K = (64, 512, 256, 32, 1024, 8)
        b, s, d = x.shape
        logits = jnp.einsum('bsd,ed->bse', x, gate_w) + gate_b
        probs = jax.nn.softmax(logits, axis=-2)
        vals_t, idx_t = jax.lax.top_k(probs.transpose(0, 2, 1), K)
        vals = vals_t.transpose(0, 2, 1)
        idx = idx_t.transpose(0, 2, 1)
        flat_idx = idx.reshape(b, K * E)
        tok = jnp.take_along_axis(x, flat_idx[:, :, None], axis=1)
        tok = tok.reshape(b, K, E, d)
        merged = jnp.einsum('bked,bke->bed', tok, vals)
        ones = jnp.ones(merged.shape[:-1] + (1,), merged.dtype)
        h = jnp.einsum('bei,eih->beh', jnp.concatenate([merged, ones], -1), w1)
        h = jax.nn.gelu(h, approximate=False)
        o = jnp.einsum('bej,ejo->beo', jnp.concatenate([h, ones], -1), w2)
        out_tok = jnp.einsum('beo,bke->bkeo', o, vals).reshape(b, K * E, d)
        out = jnp.zeros_like(x).at[jnp.arange(b)[:, None], flat_idx].add(out_tok)
        return out
    h = _L0_tok_ref(x, L0_tok_weight, L0_tok_class_token, L0_tok_pos_embedding)
    h = h + _L0_attn_ref(_layernorm(h, axis=-1), L0_attn_w_down_q, L0_attn_w_down_kv, L0_attn_w_up_q, L0_attn_w_up_k, L0_attn_w_up_v, L0_attn_w_out, L0_attn_ln_scale, L0_attn_ln_bias)
    h = h + _L0_ffn_ref(_layernorm(h, axis=-1), L0_ffn_gate_w, L0_ffn_gate_b, L0_ffn_w1, L0_ffn_w2)
    return h

_drawn_inputs = setup_inputs


def setup_inputs(seed=0):
    import zlib

    import numpy as np

    out = dict(_drawn_inputs(seed))
    spreads = {'L0_attn_ln_scale': (1.0, 0.6), 'L0_attn_ln_bias': (0.0, 0.8), 'L0_ffn_gate_b': (0.0, 0.8)}
    factors = {'L0_attn_w_down_q': 8.0,
     'L0_attn_w_down_kv': 2.686,
     'L0_attn_w_up_q': 8.0,
     'L0_attn_w_up_k': 8.0,
     'L0_ffn_gate_w': 6.053,
     'L0_ffn_w1': 5.679,
     'L0_ffn_w2': 5.436}
    for name, (base, spread) in spreads.items():
        noise = np.random.default_rng([zlib.crc32(name.encode()), seed]).standard_normal(out[name].shape)
        drawn = base * np.exp(spread * noise) if base else spread * noise
        out[name] = jnp.asarray(drawn.astype(out[name].dtype))
    for name, factor in factors.items():
        out[name] = (out[name] * factor).astype(out[name].dtype)
    return out
```

```python
from contextlib import ExitStack

import numpy as np
import concourse.bass as bass
from concourse import mybir

fp32 = mybir.dt.float32
bf16 = mybir.dt.bfloat16
int32 = mybir.dt.int32
ALU = mybir.AluOpType
ACT = mybir.ActivationFunctionType
AX = mybir.AxisListType

B, C, IMG, P = 16, 3, 96, 16
GRID = IMG // P
NPATCH = GRID * GRID
S = NPATCH + 1
D = 256
DIN = P * P * C
KC = DIN // 128
NT = B // 2
ROWS = 64 + S
QROWS = ROWS + 1
HB = B // 2
HN = HB * S
H, DH = 16, 64
NM = H // 2
DL = 128
E, HID, K = 32, 1024, 8
GE = 4
NG = E // GE
SLOTS = 2 * GE
W1N, W2N = 2 * HID, 8 * D
SCRATCH = 5
MAGIC = 12582912.0
SEED = 1597463007.0
LN_EPS = 1e-5
HID0, GELU0, THE0, O0, OE0, MOVED0 = 3, 2, 2, 1, 1, 16


def vit_tower(nc, xr, tokw, clsr, posr, wd, lnsb, wuq, wuk, wuv, wo, gw, gb, w1, w2,
              rope, eye, rowmask, sel, out):
    ctx = ExitStack()
    with ctx:
        def sb(name, shape, dt=fp32):
            return ctx.enter_context(nc.sbuf_tensor(name, shape, dt))

        def sem(name):
            return ctx.enter_context(nc.semaphore(name))

        def sems(name, n):
            return [sem(f"{name}{i}") for i in range(n)]

        w1_ring = sb("w1_ring", [128, SLOTS, W1N])
        w2_ring = sb("w2_ring", [128, SLOTS, W2N])
        scr1 = w1_ring[:, SCRATCH:SLOTS, :].rearrange("p a n -> p (a n)")
        scr2 = w2_ring[:, SCRATCH:SLOTS, :].rearrange("p a n -> p (a n)")
        r_av = sb("r_av", [128, 1024 + 2048])
        resid = sb("resid", [128, NT, D])
        ckv_dup = sb("ckv_dup", [128, B * ROWS])
        ckv_lo = sb("ckv_lo", [128, HB, 128])
        ckv_hi = sb("ckv_hi", [128, HB, 128])
        r_p = sb("r_p", [128, 2048])
        r_pt = sb("r_pt", [128, NM * HN])
        r_z = sb("r_z", [128, 2 * NM * HN])
        r_ot = sb("r_ot", [128, 2 * HN])
        r_ao = sb("r_ao", [128, 2, HB * 64])
        ident = sb("ident", [128, 128])
        ident_b = sb("ident_b", [128, 128], bf16)
        small = sb("small", [128, 256])
        gwc = sb("gwc", [128, 2, E])
        lnc = sb("lnc", [128, 4])
        gbc = sb("gbc", [128, 1])
        maskc = sb("maskc", [128, 1])

        x_sb = scr1[:, :].rearrange("p (t n) -> p t n", t=NT)
        k_bd = scr1[:, 0:2 * NM * HN].rearrange("p (m i n) -> p m i n", m=NM, i=2)
        rope_a = scr1[:, 4736:4736 + 2 * HN].rearrange("p (i n) -> p i n", i=2)
        rope_b = scr1[:, 5328:5328 + 2 * HN].rearrange("p (i n) -> p i n", i=2)
        wuq_sb = scr2[:, 0:H * 96].rearrange("p (m i n) -> p m i n", m=NM, i=2)
        wuk_sb = scr2[:, 1536:1536 + H * 96].rearrange("p (m i n) -> p m i n", m=NM, i=2)
        q_rot = scr2[:, 3072:3072 + NM * HN].rearrange("p (m n) -> p m n", m=NM)
        tokw_sb = scr2[:, 3072:3072 + KC * D]
        tokw_q = scr2[:, 4608:4608 + KC * D // 2].bitcast(bf16).rearrange("p (c n) -> p c n", c=KC)
        cq = scr2[:, 5440:5440 + B * S]
        rope_sb = scr2[:, 6032:6032 + 2 * S]
        wuv_sb = r_av[:, 0:H * DH]
        wo_sb = r_av[:, 1024:3072].rearrange("p (m n) -> p m n", m=NM)
        base = r_p[:, 0:D]
        cls_sb = r_p[:, D:2 * D]
        ones = r_p[:, 2 * D:2 * D + 128]
        junk = r_p[:, 1024:1024 + DIN]
        prob = r_p[:, :].rearrange("p (i m n) -> p i m n", i=2, m=NM)
        xq = r_pt[:, 0:DIN].bitcast(bf16).rearrange("p (i n) -> p i n", i=2)
        zT = r_pt[:, 768:768 + 2 * B * S].rearrange("p (c n) -> p c n", c=2)
        pT = r_pt[:, :].rearrange("p (m n) -> p m n", m=NM)
        h0 = r_z[:, 0:2048].rearrange("p (t n) -> p t n", t=NT)
        z = r_z[:, 2048:4096].rearrange("p (t n) -> p t n", t=NT)
        xqT = r_z[:, 4096:4096 + KC * QROWS].bitcast(bf16).rearrange("p (i c n) -> p i c n", i=2, c=KC)
        wjunk = r_z[:, 0:KC * D]
        ZT = r_z[:, :].rearrange("p (i m n) -> p i m n", i=2, m=NM)
        dup = ckv_dup[:, :].rearrange("p (b n) -> p b n", b=B)
        oT = r_ot[:, :].rearrange("p (i n) -> p i n", i=2)
        wd_sb = r_ao[:, :, 0:256]
        aoT = r_ao
        hn2 = r_z[:, 0:2048].rearrange("p (t n) -> p t n", t=NT)
        hn2T = r_z[:, 2048:2048 + 2 * B * S].rearrange("p (c b s) -> p c b s", c=2, b=B)
        r_soft = r_z[:, 3232:3232 + 4 * 4 * S].rearrange("p (k q s) -> p k q s", k=4, q=4)
        pm_pad = ckv_dup[:, 0:512].rearrange("p (q n) -> p q n", q=4)
        pmT = ckv_dup[:, 512:1024].rearrange("p (q n) -> p q n", q=4)
        merged = ckv_lo[:, :, :].rearrange("p a n -> p (a n)").rearrange("p (q n) -> p q n", q=4)
        mT = r_pt[:, 0:2048].rearrange("p (c e b) -> p c e b", c=2, e=E)
        hi_flat = ckv_hi[:, :, :].rearrange("p a n -> p (a n)")
        pm_e = hi_flat[0:72, 0:B * S].rearrange("p (b s) -> p b s", b=B)
        sel_sb = hi_flat[0:GE, 640:640 + 128]
        bias1 = r_av[0:GE, 0:2 * HID].rearrange("p (g n) -> p g n", g=2)
        bias2 = r_av[0:GE, 2048:2048 + 2 * D].rearrange("p (g n) -> p g n", g=2)
        stage = r_av[:, 2560:3072].rearrange("p (g c e b) -> p g c e b", g=2, c=2, e=GE)
        hg = r_p[:, 0:HID]
        hT = r_p[:, 1024:2048].rearrange("p (k n) -> p k n", k=8)
        o_sb = r_ot[:, 0:2 * D].rearrange("p (g n) -> p g n", g=2)
        o_all = r_z[0:72, 0:B * D].rearrange("p (b n) -> p b n", b=B)

        at = [0]

        def few(n):
            at[0] += n
            assert at[0] <= 256
            return small[:, at[0] - n:at[0]]

        wsum, wmean, wscale, wdq = few(1), few(1), few(1), few(1)
        ssq, amax, xr_s, xscale, dq = few(NT), few(NT), few(NT), few(NT), few(NT)
        nv, ny, na, nb = few(NT), few(NT), few(NT), few(NT)
        r1, r2 = few(NT), few(NT)
        mv = few(2 * NT).rearrange("p (t k) -> p t k", k=2)
        bst = few(6)
        smax = few(2 * H).rearrange("p (i h) -> p i h", i=2)
        ssum = few(2 * H).rearrange("p (i h) -> p i h", i=2)
        top8 = few(32).rearrange("p (q k) -> p q k", q=4)
        rq = few(4)

        bank = [ctx.enter_context(nc.psum_tensor(f"bank{i}", [128, 512], fp32)) for i in range(8)]

        s_x = sems("x_in", NT)
        s_tokw, s_base, s_wd, s_eye, s_wup, s_av, s_gate, s_sel = (
            sem(n) for n in ("tokw_in", "base_in", "wd_in", "eye_in", "wup_in", "av_in", "gate_in", "sel_in"))
        s_w1 = sems("w1_in", SLOTS)
        s_w2 = sems("w2_in", SLOTS)
        s_b1 = sems("b1_in", 2)
        s_b2 = sems("b2_in", 2)
        s_bank = sem("banks_zeroed")
        s_pool0 = sem("pool_constants")
        s_dve, s_actc = sem("dve_chain"), sem("act_chain")
        s_wabs, s_wsum, s_wm, s_wq = (sem(n) for n in ("w_abs", "w_sum", "w_mean", "w_ternary"))
        s_ssq, s_xs, s_xq, s_xt, s_xte, s_proj, s_h0, s_hn, s_z, s_res = (sem(n) for n in (
            "sum_sq", "x_scaled", "x_rounded", "x_turned", "x_turned_out", "projected", "h0_ready",
            "hn_ready", "z_ready", "resid_ready"))
        s_zt, s_zte, s_c, s_ce, s_ct, s_cte = (sem(n) for n in (
            "z_turned", "z_turned_out", "latents", "latents_out", "ckv_turned", "ckv_turned_out"))
        s_up, s_prod, s_rot, s_kbz = (sem(n) for n in ("up_done", "rope_products", "rotated", "k_bd_zeroed"))
        s_sc, s_sub, s_exp, s_rs, s_pn, s_pt, s_pte = (sem(n) for n in (
            "scores", "shifted", "exps", "row_sums", "probs", "probs_turned", "probs_turned_out"))
        s_gap = sem("gaps_zeroed")
        s_zz, s_ze0, s_ze1, s_oo, s_ooe, s_ote, s_bk, s_h1 = (sem(n) for n in (
            "z_done", "z_out_even", "z_out_odd", "heads_done", "heads_out", "attn_out",
            "attn_turned", "h1_ready"))
        s_hn2, s_ht, s_hte, s_lg, s_rsub, s_rexp, s_pm, s_pmt, s_pmte, s_mg, s_mge, s_mt, s_mte, s_pme = (
            sem(n) for n in (
                "hn2_ready", "hn2_turned", "hn2_turned_out", "logits", "logits_shifted", "router_exps",
                "pm_ready", "pm_turned", "pm_turned_out", "merged_done", "merged_out", "merged_turned",
                "merged_turned_out", "pm_e_in"))
        s_pool1 = sem("expert_zeros")
        s_stage, s_hid, s_gelu, s_th, s_the, s_o, s_oe, s_fin, s_fout, s_out = (sem(n) for n in (
            "staged", "hidden", "gelus", "hidden_turned", "hidden_turned_out", "expert_out",
            "expert_out_kept", "scattered", "result", "stored"))
        s_ob = sems("expert_out_moved", 2)
        s_idb = sem("ident_b_ready")
        s_otm = sem("attn_sums")

        block = ctx.enter_context(nc.Block())

        @block.sync
        def _(sp):
            sp.dma_start(tokw_sb, tokw).then_inc(s_tokw, 16)
            for t in range(NT):
                sp.dma_start(x_sb[0:64, t, :], xr[72 * t:72 * t + 64, :]).then_inc(s_x[t], 16)
                sp.dma_start(x_sb[64:112, t, :], xr[72 * t + 36:72 * t + 84, :]).then_inc(s_x[t], 16)
            sp.dma_start(wd_sb, wd).then_inc(s_wd, 16)
            sp.dma_start(scr2[:, 0:1536], wuq).then_inc(s_wup, 16)
            sp.dma_start(scr2[:, 1536:3072], wuk).then_inc(s_wup, 16)
            sp.dma_start(wuv_sb, wuv).then_inc(s_av, 16)
            sp.dma_start(wo_sb, wo).then_inc(s_av, 16)

            def load_w1(e, slot):
                sp.dma_start(w1_ring[:, slot, :],
                             w1[bass.ds(e, 1), 0:D, :].rearrange("a (p c) h -> p (a c h)", c=2)).then_inc(s_w1[slot], 16)

            def load_w2(e, slot):
                sp.dma_start(w2_ring[:, slot, :],
                             w2[bass.ds(e, 1), 0:HID, :].rearrange("a (p c) h -> p (a c h)", c=8)).then_inc(s_w2[slot], 16)

            def load_b1(e, g):
                sp.dma_start(bias1[:, g, :], w1[bass.ds(e, GE), D:D + 1, :].rearrange("e a h -> e (a h)")).then_inc(s_b1[g], 16)

            def load_b2(e, g):
                sp.dma_start(bias2[:, g, :], w2[bass.ds(e, GE), HID:HID + 1, :].rearrange("e a h -> e (a h)")).then_inc(s_b2[g], 16)

            for e in range(GE):
                load_w1(e, e)
            for e in range(GE):
                load_w2(e, e)
            for e in range(GE, SCRATCH):
                load_w1(e, e)
                load_w2(e, e)
            sp.wait_ge(s_sc, 2 * NT)
            for e in range(SCRATCH, SLOTS):
                load_w1(e, e)
            for e in range(SCRATCH, SLOTS):
                load_w2(e, e)
            sp.wait_ge(s_otm, 2 * NM)
            for g in range(2):
                load_b1(GE * g, g)
                load_b2(GE * g, g)
            with sp.Fori(1, NG // 2) as it:
                for g in range(2):
                    sp.wait_ge(s_hid, 4 * it + 2 * g - 2 + HID0)
                    load_b1(it * SLOTS + GE * g, g)
                    for j in range(GE):
                        load_w1(it * SLOTS + GE * g + j, GE * g + j)
                    sp.wait_ge(s_o, 2 * it + g - 1 + O0)
                    load_b2(it * SLOTS + GE * g, g)
                    for j in range(GE):
                        load_w2(it * SLOTS + GE * g + j, GE * g + j)
            for p in range(NT // 2):
                sp.wait_ge(s_fout, p + 1)
                for i in range(2):
                    o_v = out.rearrange("(t i) s d -> i s t d", i=2)
                    sp.dma_start(o_v[i, 1:S, 2 * p:2 * p + 2, :],
                                 resid[64 * i:64 * i + NPATCH, 2 * p:2 * p + 2, :]).then_inc(s_out, 16)
                    sp.dma_start(o_v[i, 0:1, 2 * p:2 * p + 2, :],
                                 resid[64 * i + NPATCH:64 * i + S, 2 * p:2 * p + 2, :]).then_inc(s_out, 16)
            sp.wait_ge(s_out, 16 * 2 * NT)

        @block.gpsimd
        def _(pool):
            pool.memset(ones, 1.0).then_inc(s_pool0, 1)
            pool.memset(ckv_dup[:, :], 0.0).then_inc(s_pool0, 1)
            pool.memset(ckv_lo[:, :, :], 0.0).then_inc(s_pool0, 1)
            pool.memset(ckv_hi[:, :, :], 0.0).then_inc(s_pool0, 1)
            for t in range(NT):
                pool.wait_ge(s_xs, t + 1)
                if t >= 2:
                    pool.wait_ge(s_xt, t - 1)
                pool.tensor_scalar(xq[0:QROWS, t % 2, :], x_sb[0:QROWS, t, :], MAGIC, -MAGIC,
                                   ALU.add, ALU.add).then_inc(s_xq, 1)
            for t in range(NT):
                pool.wait_ge(s_z, t + 1)
                if t == 0:
                    pool.wait_ge(s_xq, NT)
                    pool.memset(k_bd[0:64, :, 1, :], 0.0).then_inc(s_kbz, 1)
                    pool.wait_ge(s_kbz, 1)
                    pool.memset(k_bd[64:128, :, 0, :], 0.0).then_inc(s_kbz, 1)
                    pool.wait_ge(s_kbz, 2)
                pool.tensor_tensor(resid[0:ROWS, t, :], h0[0:ROWS, t, :], resid[0:ROWS, t, :], ALU.add).then_inc(s_res, 1)
            pool.wait_ge(s_h0, NT)
            pool.wait_ge(s_wm, 1)
            pool.memset(prob[:, :, :, 37:64], 0.0).then_inc(s_gap, 1)
            pool.wait_ge(s_c, 4)
            pool.memset(aoT[:, :, :], 0.0).then_inc(s_gap, 1)

            def rotate(half):
                for m in range(NM):
                    for u in range(2):
                        n = (half * NM + m) * 2 + u
                        pool.wait_ge(s_prod, 2 * n + 2)
                        if n == 0:
                            pool.wait_ge(s_wq, 1)
                        if half and m == 0 and u == 0:
                            pool.wait_ge(s_sc, NT)
                        if u == 0:
                            if n:
                                pool.wait_ge(s_rot, 3 * (n // 2))
                            pool.tensor_tensor(q_rot[:, m, :], rope_a[:, 0, :], rope_b[:, 0, :], ALU.add).then_inc(s_rot, 1)
                        else:
                            for i in range(2):
                                pool.wait_ge(s_rot, 3 * (n // 2) + 1 + i)
                                pool.tensor_tensor(k_bd[64 * i:64 * i + 64, m, i, :], rope_a[64 * i:64 * i + 64, 1, :],
                                                   rope_b[64 * i:64 * i + 64, 1, :], ALU.add).then_inc(s_rot, 1)

            def normalise(t):
                pool.wait_ge(s_rs, t + 1)
                p = prob[0:ROWS, t % 2, :, :].rearrange("p m (i k) -> p (m i) k", i=2)[:, :, 0:S]
                pool.tensor_tensor(p, p, ssum[0:ROWS, t % 2, :].unsqueeze(2).broadcast_to([ROWS, H, S]),
                                   ALU.mult).then_inc(s_pn, 1)

            rotate(0)
            pool.wait_ge(s_rot, 3 * NM)
            for t in range(NT // 2):
                normalise(t)
            rotate(1)
            pool.wait_ge(s_rot, 6 * NM)
            for t in range(NT // 2, NT):
                normalise(t)
            pool.wait_ge(s_ct, 4)
            pool.memset(pm_pad, 0.0).then_inc(s_pool1, 1)
            pool.wait_ge(s_zz, 2 * B)
            pool.memset(hi_flat[:, 0:B * S], 0.0).then_inc(s_pool1, 1)
            pool.memset(mT[:, :, :, :], 0.0).then_inc(s_pool1, 1)
            pool.wait_ge(s_mg, 2)
            pool.wait_ge(s_pm, 1)
            pool.memset(r_z[0:72, 0:B * D], 0.0).then_inc(s_pool1, 1)

        @block.scalar
        def _(act):
            for dst, src, s in ((ident[:, :], eye, s_eye), (base[0:ROWS, :], posr, s_base), (cls_sb[0:ROWS, :], clsr, s_base),
                                (maskc[:, :], rowmask, s_base), (rope_sb, rope, s_wup), (lnc[:, :], lnsb, s_wd),
                                (gwc[:, :, :], gw, s_gate), (gbc[:, :], gb, s_gate)):
                act.dma_start(dst, src).then_inc(s, 16)

            act.wait_ge(s_tokw, 16)
            act.activation(wjunk, tokw_sb, ACT.Abs, accum_out=wsum).then_inc(s_wabs, 1)

            def square_sum(t):
                act.wait_ge(s_x[t], 32)
                if t == 0:
                    act.wait_ge(s_wabs, 1)
                else:
                    act.wait_ge(s_ssq, t)
                act.activation(junk[0:QROWS, :], x_sb[0:QROWS, t, :], ACT.Square,
                               accum_out=ssq[0:QROWS, t:t + 1]).then_inc(s_ssq, 1)

            def xq_out(t):
                act.wait_ge(s_xt, t + 1)
                if t >= 2:
                    act.wait_ge(s_proj, t - 1)
                act.activation(xqT[:, t % 2, :, :].rearrange("p c n -> p (c n)"),
                               bank[t % 2][:, :].bitcast(bf16)[:, 0:KC * QROWS], ACT.Copy).then_inc(s_xte, 1)

            for t in range(5):
                square_sum(t)
            xq_out(0)
            for t in range(5, NT):
                square_sum(t)
                xq_out(t - 4)
            for t in range(NT - 4, NT):
                xq_out(t)

            def z_out(t):
                act.wait_ge(s_zt, t + 1)
                if t == 0:
                    act.wait_ge(s_wd, 32)
                for c in range(2):
                    act.activation(zT[:, c, 2 * t * S:2 * t * S + 2 * S].rearrange("p (i s) -> p i s", i=2),
                                   bank[6 + t % 2][:, c * 128:(c + 1) * 128].rearrange("p (i s) -> p i s", i=2)[:, :, 0:S],
                                   ACT.Identity, bias=lnc[:, 2 + c:3 + c], scale=lnc[:, c:c + 1]).then_inc(s_zte, 1)

            def latents_out(half):
                act.wait_ge(s_c, 2 * half + 1)
                act.activation(cq[:, half * HN:(half + 1) * HN], bank[2 * half][:, 0:HN], ACT.Copy).then_inc(s_ce, 1)
                act.wait_ge(s_c, 2 * half + 2)
                act.wait_ge(s_pool0, 2)
                for i in range(2):
                    act.activation(dup[:, half * HB:(half + 1) * HB, 64 * i:64 * i + S],
                                   bank[2 * half + 1][:, 0:HN].rearrange("p (b s) -> p b s", b=HB),
                                   ACT.Copy).then_inc(s_ce, 1)

            def ckv_out(half):
                act.wait_ge(s_pool0, 4)
                if half:
                    act.wait_ge(s_zz, B)
                for g in range(2):
                    act.wait_ge(s_ct, 2 * half + g + 1)
                    src = bank[6 + g][:, :].rearrange("p (b n) -> p b n", b=4)
                    act.activation(ckv_lo[0:S, 4 * g:4 * g + 4, :], src[0:S, :, :], ACT.Copy).then_inc(s_cte, 1)
                    act.activation(ckv_hi[64:64 + S, 4 * g:4 * g + 4, :], src[64:64 + S, :, :], ACT.Copy).then_inc(s_cte, 1)

            def exps(t):
                act.wait_ge(s_sub, 2 * t + 2)
                p = prob[0:ROWS, t % 2, :, :].rearrange("p m (i k) -> p (m i) k", i=2)[:, :, 0:S]
                act.activation(p, p, ACT.Exp, scale=DH ** -0.5).then_inc(s_exp, 1)

            def probs_out(t):
                half = t // 4
                if half == 0 and t == 0:
                    act.wait_ge(s_ce, 6)
                if half:
                    act.wait_ge(s_zz, B)
                for g in range(2):
                    act.wait_ge(s_pt, 2 * t + g + 1)
                    act.activation(
                        pT[0:ROWS, 4 * g:4 * g + 4, 2 * (t % 4) * S:2 * (t % 4) * S + 2 * S].rearrange("p m (i q) -> p m i q", i=2),
                        bank[2 * (t % 2) + g][0:ROWS, :].rearrange("p (m i q) -> p m i q", m=4, i=2)[:, :, :, 0:S],
                        ACT.Copy).then_inc(s_pte, 1)

            def z_even_out(half):
                if half:
                    act.wait_ge(s_oo, NM)
                else:
                    act.wait_ge(s_res, NT)
                for b in range(HB):
                    act.wait_ge(s_zz, half * B + 2 * b + 1)
                    act.activation(ZT[:, 0, :, b * S:(b + 1) * S],
                                   bank[0][:, 0:HN].rearrange("p (m s) -> p m s", m=NM), ACT.Copy).then_inc(s_ze0, 1)

            def heads_out(half):
                for m in range(NM):
                    n = half * NM + m
                    act.wait_ge(s_oo, n + 1)
                    if n >= 2:
                        act.wait_ge(s_otm, n - 1)
                    act.activation(oT[:, m % 2, :], bank[2 + m % 2][:, 0:HN], ACT.Copy).then_inc(s_ooe, 1)

            for t in range(4):
                z_out(t)
            latents_out(0)
            for t in range(4, NT):
                z_out(t)
            latents_out(1)
            ckv_out(0)
            exps(0)
            exps(1)
            probs_out(0)
            exps(2)
            probs_out(1)
            exps(3)
            probs_out(2)
            probs_out(3)
            exps(4)
            exps(5)
            z_even_out(0)
            probs_out(4)
            probs_out(5)
            exps(6)
            exps(7)
            heads_out(0)
            probs_out(6)
            probs_out(7)
            ckv_out(1)
            z_even_out(1)
            heads_out(1)

            for t in range(NT):
                act.wait_ge(s_ht, t + 1)
                src = bank[t % 4][:, 0:256].rearrange("p (c i s) -> p c i s", c=2, i=2)
                dst = hn2T[:, :, 2 * t:2 * t + 2, :]
                act.activation(dst[:, :, :, 1:S], src[:, :, :, 0:NPATCH], ACT.Copy).then_inc(s_hte, 1)
                act.activation(dst[:, :, :, 0:1], src[:, :, :, NPATCH:S], ACT.Copy).then_inc(s_hte, 1)
            act.wait_ge(s_rsub, 1)
            act.activation(r_soft[:, 1, :, :], r_soft[:, 1, :, :], ACT.Exp).then_inc(s_rexp, 1)
            act.wait_ge(s_pmt, 1)
            act.activation(pmT[0:ROWS, :, :].rearrange("p q n -> p (q n)"), bank[5][0:ROWS, :], ACT.Copy).then_inc(s_pmte, 1)
            act.wait_ge(s_zz, 2 * B)
            act.wait_ge(s_mg, 2)
            act.activation(merged[:, 2:4, :].rearrange("p q n -> p (q n)"), bank[7][:, :], ACT.Copy).then_inc(s_mge, 1)
            act.wait_ge(s_zz, 2 * B)
            act.dma_start(sel_sb, sel).then_inc(s_sel, 16)
            act.wait_ge(s_pool1, 2)
            act.wait_ge(s_pm, 1)
            for i in range(4):
                act.dma_start(pm_e[0:E, :, :].rearrange("p (q i) s -> p i q s", i=4)[:, i, :, :],
                              pm_pad[32 * i:32 * i + 32, :, 0:S]).then_inc(s_pme, 16)
            act.wait_ge(s_mt, 2)
            act.wait_ge(s_pool1, 3)
            act.activation(mT[:, 1, :, 0:B].rearrange("p e b -> p b e"),
                           bank[1][:, :].rearrange("p (b e) -> p b e", b=B), ACT.Copy).then_inc(s_mte, 1)
            act.sem_inc(s_gelu, GELU0)
            for g in range(2):
                act.sem_inc(s_ob[g], MOVED0)
            act.wait_ge(s_mte, 2)
            act.wait_ge(s_pool1, 4)
            for gr in range(NG):
                for n in range(2):
                    act.wait_ge(s_hid, 2 * gr + n + 1 + HID0)
                    if gr >= 1 and n == 0:
                        act.wait_ge(s_th, 2 * gr)
                    act.activation(hg[:, n * 512:(n + 1) * 512], bank[n][:, :], ACT.Gelu).then_inc(s_gelu, 1)
                if gr >= 1:
                    move_out(act, gr - 1, s_oe, o_all, o_sb, s_ob)
            move_out(act, NG - 1, s_oe, o_all, o_sb, s_ob)

        @block.tensor
        def _(pe):
            mm, tr = nc.tensor.matmul, nc.tensor.transpose
            pe.wait_ge(s_bank, 8)
            pe.wait_ge(s_pool0, 1)
            pe.wait_ge(s_wabs, 1)
            mm(bank[7][:, 0:1], ones, wsum, start=True, stop=True).then_inc(s_wsum, 1)

            def project(t):
                pe.wait_ge(s_xte, t + 1)
                if t == 0:
                    pe.wait_ge(s_wq, 1)
                if t >= 4:
                    pe.wait_ge(s_h0, t - 3)
                for c in range(KC):
                    last = mm(bank[2 + t % 4][0:ROWS, 0:D], xqT[:, t % 2, c, 0:ROWS], tokw_q[:, c, :],
                              start=(c == 0), stop=(c == KC - 1))
                last.then_inc(s_proj, 1)

            for t in range(NT):
                pe.wait_ge(s_xq, t + 1)
                if t == 0:
                    pe.wait_ge(s_idb, 1)
                if t >= 2:
                    pe.wait_ge(s_xte, t - 1)
                for c in range(KC):
                    last = tr(bank[t % 2][:, :].bitcast(bf16)[:, c * QROWS:(c + 1) * QROWS],
                              xq[0:QROWS, t % 2, c * 128:(c + 1) * 128], ident_b[0:QROWS, 0:QROWS])
                last.then_inc(s_xt, 1)
                if t >= 1:
                    project(t - 1)
            project(NT - 1)

            def turn_z(t):
                pe.wait_ge(s_z, t + 1)
                if t == 0:
                    pe.wait_ge(s_wm, 1)
                    pe.wait_ge(s_eye, 16)
                if t >= 2:
                    pe.wait_ge(s_zte, 2 * (t - 1))
                for c in range(2):
                    last = tr(bank[6 + t % 2][:, c * 128:c * 128 + ROWS], z[0:ROWS, t, c * 128:(c + 1) * 128],
                              ident[0:ROWS, 0:ROWS])
                last.then_inc(s_zt, 1)

            def latents(half):
                if half == 0:
                    pe.wait_ge(s_xte, NT)
                    pe.wait_ge(s_wd, 32)
                else:
                    pe.wait_ge(s_h0, NT)
                pe.wait_ge(s_zte, NT * (half + 1))
                for u in range(2):
                    for c in range(2):
                        last = mm(bank[2 * half + u][:, 0:HN], wd_sb[:, c, u * DL:(u + 1) * DL],
                                  zT[:, c, half * HN:(half + 1) * HN], start=(c == 0), stop=(c == 1))
                    last.then_inc(s_c, 1)

            def turn_ckv(half):
                pe.wait_ge(s_ce, 3 * half + 3)
                if half == 0:
                    pe.wait_ge(s_zte, 2 * NT)
                else:
                    pe.wait_ge(s_h1, 4)
                for g in range(2):
                    for b in range(4):
                        last = tr(bank[6 + g][0:ROWS, b * 128:(b + 1) * 128], dup[:, half * HB + 4 * g + b, :], ident[:, :])
                    last.then_inc(s_ct, 1)

            def up(half):
                for m in range(NM):
                    for u, w in enumerate((wuq_sb, wuk_sb)):
                        n = (half * NM + m) * 2 + u
                        if n == 0:
                            pe.wait_ge(s_wup, 48)
                            pe.wait_ge(s_ce, 6)
                        if n >= 2:
                            pe.wait_ge(s_prod, 2 * (n - 2) + 2)
                        if n == 16:
                            pe.wait_ge(s_pte, 8)
                        rhs = cq[:, half * HN:(half + 1) * HN] if u == 0 else dup[:, half * HB:(half + 1) * HB, 0:S]
                        for j in range(2):
                            for i in range(2):
                                last = mm(bank[2 * u + j][64 * i:64 * i + 64, 0:HN], w[:, m, i, 32 * j:32 * j + 64], rhs,
                                          start=True, stop=True)
                        last.then_inc(s_up, 1)

            def scores(t):
                half = t // 4
                pe.wait_ge(s_rot, 3 * NM * (half + 1))
                if t == 0:
                    pe.wait_ge(s_kbz, 2)
                    pe.wait_ge(s_h0, NT)
                if t == 1:
                    pe.wait_ge(s_cte, 4)
                if t >= 2:
                    pe.wait_ge(s_sub, 2 * (t - 2) + 2)
                for g in range(2):
                    for mq in range(4):
                        for i in range(2):
                            b = 2 * (t % 4) + i
                            m = 4 * g + mq
                            last = mm(bank[4 + 2 * (t % 2) + g][64 * i:64 * i + S, mq * 2 * S:(mq + 1) * 2 * S],
                                      q_rot[:, m, b * S:(b + 1) * S], k_bd[:, m, :, b * S:(b + 1) * S],
                                      start=True, stop=True)
                    last.then_inc(s_sc, 1)

            def turn_probs(t):
                pe.wait_ge(s_pn, t + 1)
                if t == 0:
                    pe.wait_ge(s_gap, 1)
                    pe.wait_ge(s_prod, 4 * NM)
                if t == 4:
                    pe.wait_ge(s_ze0, HB)
                    pe.wait_ge(s_ze1, HB)
                if t == 5:
                    pe.wait_ge(s_prod, 8 * NM)
                if t == 7:
                    pe.wait_ge(s_ooe, NM)
                if t not in (0, 1, 4, 5):
                    pe.wait_ge(s_pte, 2 * (t - 2) + 2)
                for g in range(2):
                    for mq in range(4):
                        last = tr(bank[2 * (t % 2) + g][0:ROWS, mq * 128:mq * 128 + ROWS],
                                  prob[0:ROWS, t % 2, 4 * g + mq, 0:ROWS], ident[0:ROWS, 0:ROWS])
                    last.then_inc(s_pt, 1)

            def values(half):
                pe.wait_ge(s_pte, 8 * (half + 1))
                pe.wait_ge(s_cte, 4 * (half + 1))
                if half == 0:
                    pe.wait_ge(s_prod, 8 * NM)
                for b in range(HB):
                    for par, ck in enumerate((ckv_lo, ckv_hi)):
                        if b >= 1:
                            pe.wait_ge((s_ze0, s_ze1)[par], half * HB + b)
                        mm(bank[par][:, 0:HN], ck[0:ROWS, b, :], pT[0:ROWS, :, b * S:(b + 1) * S],
                           start=True, stop=True).then_inc(s_zz, 1)

            def heads(half):
                pe.wait_ge(s_ze0, HB * (half + 1))
                pe.wait_ge(s_ze1, HB * (half + 1))
                pe.wait_ge(s_av, 32)

                def combine(m):
                    pe.wait_ge(s_ooe, half * NM + m + 1)
                    if m == 0:
                        if half == 0:
                            pe.wait_ge(s_sub, 14)
                        else:
                            pe.wait_ge(s_ote, 2)
                    for c in range(2):
                        last = mm(bank[4 + c][:, 0:HN], wo_sb[:, m, c * 128:(c + 1) * 128], oT[:, m % 2, :],
                                  start=(m == 0), stop=(m == NM - 1))
                    last.then_inc(s_otm, 1)

                for m in range(NM):
                    n = half * NM + m
                    if half == 0 and m == 0:
                        pe.wait_ge(s_pte, 12)
                    if half == 1 and m == 0:
                        pe.wait_ge(s_pte, 16)
                    if n >= 2:
                        pe.wait_ge(s_ooe, n - 1)
                    for par in range(2):
                        h = 2 * m + par
                        last = mm(bank[2 + m % 2][64 * par:64 * par + 64, 0:HN], wuv_sb[:, h * DH:(h + 1) * DH],
                                  ZT[:, par, m, :], start=True, stop=True)
                    last.then_inc(s_oo, 1)
                    if m >= 1:
                        combine(m - 1)
                combine(NM - 1)

            def turn_back(half):
                for t in range(4):
                    n = 4 * half + t
                    if t == 0:
                        pe.wait_ge(s_ote, 2 * half + 2)
                        if half == 0:
                            pe.wait_ge(s_sub, 16)
                        else:
                            pe.wait_ge(s_cte, 8)
                    if t >= 2:
                        pe.wait_ge(s_h1, n - 1)
                    for c in range(2):
                        last = tr(bank[6 + t % 2][0:ROWS, c * 128:(c + 1) * 128], aoT[:, c, t * 128:t * 128 + ROWS], ident[:, :])
                    last.then_inc(s_bk, 1)

            for t in range(4):
                turn_z(t)
            latents(0)
            for t in range(4, NT):
                turn_z(t)
            latents(1)
            turn_ckv(0)
            up(0)
            scores(0)
            scores(1)
            turn_probs(0)
            scores(2)
            turn_probs(1)
            scores(3)
            turn_probs(2)
            turn_probs(3)
            up(1)
            scores(4)
            scores(5)
            values(0)
            turn_probs(4)
            turn_probs(5)
            scores(6)
            scores(7)
            heads(0)
            turn_probs(6)
            turn_probs(7)
            turn_back(0)
            turn_ckv(1)
            values(1)
            heads(1)
            turn_back(1)

            for t in range(NT):
                pe.wait_ge(s_hn2, t + 1)
                if t == 0:
                    pe.wait_ge(s_ze0, B)
                    pe.wait_ge(s_ooe, 2 * NM)
                if t >= 4:
                    pe.wait_ge(s_hte, 2 * (t - 3))
                for c in range(2):
                    last = tr(bank[t % 4][:, c * 128:c * 128 + ROWS], hn2[0:ROWS, t, c * 128:(c + 1) * 128],
                              ident[0:ROWS, 0:ROWS])
                last.then_inc(s_ht, 1)
            pe.wait_ge(s_gate, 32)
            pe.wait_ge(s_ote, 4)
            for q in range(4):
                for i in range(4):
                    b = 4 * q + i
                    if i % 2 == 0:
                        pe.wait_ge(s_hte, 2 * (b // 2 + 1))
                    for c in range(2):
                        last = mm(bank[4][32 * i:32 * i + 32, q * S:(q + 1) * S], gwc[:, c, :], hn2T[:, c, b, :],
                                  start=(c == 0), stop=(c == 1))
            last.then_inc(s_lg, 1)
            pe.wait_ge(s_pm, 1)
            for q in range(4):
                last = tr(bank[5][0:ROWS, q * 128:(q + 1) * 128], pm_pad[:, q, 0:ROWS], ident[:, :])
            last.then_inc(s_pmt, 1)
            pe.wait_ge(s_pmte, 1)
            pe.wait_ge(s_h1, NT)
            for q in range(4):
                for i in range(4):
                    b, lo = 4 * q + i, 64 * (i % 2)
                    last = mm(bank[6 + q // 2][32 * i:32 * i + 32, (q % 2) * D:(q % 2 + 1) * D],
                              pmT[lo:lo + S, q, 32 * i:32 * i + 32], hn2[lo:lo + S, b // 2, :], start=True, stop=True)
                if q % 2:
                    last.then_inc(s_mg, 1)
            pe.wait_ge(s_mge, 2)
            for c in range(2):
                for q in range(4):
                    last = tr(bank[c][:, q * 128:(q + 1) * 128], merged[:, q, c:D:2], ident[:, :])
                last.then_inc(s_mt, 1)
            pe.wait_ge(s_sel, 16)
            pe.wait_ge(s_mte, 2)
            pe.sem_inc(s_hid, HID0)
            pe.sem_inc(s_o, O0)

            with pe.Fori(0, NG // 2) as it:
                for g in range(2):
                    for n in range(2):
                        if n == 0:
                            pe.wait_ge(s_b1[g], 16 * it + 16)
                            pe.wait_ge(s_stage, 2 * it + g + 1)
                        pe.wait_ge(s_gelu, 4 * it + 2 * g + n - 1 + GELU0)
                        for c in range(2):
                            for j in range(GE):
                                if n == 0 and c == 0:
                                    pe.wait_ge(s_w1[GE * g + j], 16 * it + 16)
                                last = mm(bank[n][32 * j:32 * j + 32, :], stage[:, g, c, j, :],
                                          w1_ring[:, GE * g + j, c * HID + n * 512:c * HID + (n + 1) * 512],
                                          start=(c == 0), stop=False, skip_group_check=True)
                        mm(bank[n][:, :], sel_sb[:, :], bias1[:, g, n * 512:(n + 1) * 512], start=False, stop=True,
                           skip_group_check=True).then_inc(s_hid, 1)
                    pe.wait_ge(s_gelu, 4 * it + 2 * g + 2 + GELU0)
                    pe.wait_ge(s_the, 4 * it + 2 * g + THE0)
                    for k in range(8):
                        last = tr(bank[2 + k // 4][:, (k % 4) * 128:(k % 4 + 1) * 128], hg[:, k:HID:8], ident[:, :])
                        if k % 4 == 3:
                            last.then_inc(s_th, 1)
                    pe.wait_ge(s_oe, 2 * it + g + OE0)
                    pe.wait_ge(s_b2[g], 16 * it + 16)
                    pe.wait_ge(s_the, 4 * it + 2 * g + 2 + THE0)
                    for k in range(8):
                        for j in range(GE):
                            if k == 0:
                                pe.wait_ge(s_w2[GE * g + j], 16 * it + 16)
                            last = mm(bank[4][32 * j:32 * j + 32, 0:D], hT[:, k, 32 * j:32 * j + 32],
                                      w2_ring[:, GE * g + j, k * D:(k + 1) * D], start=(k == 0), stop=False,
                                      skip_group_check=True)
                    mm(bank[4][:, 0:D], sel_sb[:, :], bias2[:, g, :], start=False, stop=True,
                       skip_group_check=True).then_inc(s_o, 1)

            pe.wait_ge(s_pme, 64)
            for g in range(2):
                pe.wait_ge(s_ob[g], 16 * GE * NG // 2 + MOVED0)
            pe.wait_ge(s_oe, NG + OE0)
            for b in range(B):
                t, i = b // 2, b % 2
                last = mm(bank[4 + t // 2][64 * i:64 * i + S, (t % 2) * D:(t % 2 + 1) * D], pm_e[:, b, :], o_all[:, b, :],
                          start=True, stop=True)
                if b % 4 == 3:
                    last.then_inc(s_fin, 1)

        @block.vector
        def _(dve):
            v = nc.vector
            count = [0]

            def link(ins):
                count[0] += 1
                ins.then_inc(s_dve, 1)
                dve.wait_ge(s_dve, count[0])

            def rsqrt(dst, src, tmp_y, tmp_a, tmp_b):
                link(v.tensor_scalar(tmp_y.bitcast(int32), src.bitcast(int32), -0.5, SEED, ALU.mult, ALU.add))
                y = tmp_y
                for step in range(3):
                    link(v.tensor_tensor(tmp_a, y, y, ALU.mult))
                    link(v.scalar_tensor_tensor(out=tmp_b, in0=tmp_a, scalar=-0.5, in1=src, op0=ALU.mult, op1=ALU.mult))
                    new = dst if step == 2 else tmp_y
                    link(v.scalar_tensor_tensor(out=new, in0=tmp_b, scalar=1.5, in1=y, op0=ALU.add, op1=ALU.mult))

            for i in range(8):
                v.memset(bank[i][:, :], 0.0).then_inc(s_bank, 1)
            dve.wait_ge(s_eye, 16)
            v.tensor_copy(ident_b[:, :], ident[:, :]).then_inc(s_idb, 1)

            dve.wait_ge(s_wsum, 1)
            v.tensor_scalar(wmean, bank[7][:, 0:1], 1.0 / (DIN * D), 1e-5, ALU.mult, ALU.max).then_inc(s_wm, 1)
            dve.wait_ge(s_wm, 1)
            link(v.reciprocal(wscale, wmean))
            link(v.reciprocal(wdq, wscale))
            link(v.tensor_scalar(tokw_sb, tokw_sb, wscale, MAGIC, ALU.mult, ALU.add))
            link(v.tensor_scalar(tokw_sb, tokw_sb, -MAGIC, 1.0, ALU.add, ALU.min))
            v.tensor_scalar(tokw_q.rearrange("p c n -> p (c n)"), tokw_sb, -1.0, None, ALU.max).then_inc(s_wq, 1)

            for lo, hi in ((0, 2), (2, 5), (5, NT)):
                for t in range(lo, hi):
                    dve.wait_ge(s_x[t], 32)
                    link(v.tensor_reduce(amax[0:QROWS, t:t + 1], x_sb[0:QROWS, t, :], AX.X, ALU.max, apply_absolute_value=True))
                dve.wait_ge(s_ssq, hi)
                c = lambda a: a[0:QROWS, lo:hi]
                link(v.tensor_scalar(c(nv), c(ssq), 1.0 / DIN, 1e-6, ALU.mult, ALU.add))
                rsqrt(c(xr_s), c(nv), c(ny), c(na), c(nb))
                link(v.tensor_tensor(c(na), c(amax), c(xr_s), ALU.mult))
                link(v.tensor_scalar(c(na), c(na), 1e-5, None, ALU.max))
                link(v.reciprocal(c(nb), c(na)))
                link(v.tensor_scalar(c(xscale), c(nb), 127.0, None, ALU.mult))
                for t in range(lo, hi):
                    link(v.tensor_scalar(x_sb[0:QROWS, t, :], x_sb[0:QROWS, t, :], xr_s[0:QROWS, t:t + 1],
                                         xscale[0:QROWS, t:t + 1], ALU.mult, ALU.mult))
                    v.tensor_scalar(x_sb[0:QROWS, t, :], x_sb[0:QROWS, t, :], 127.0, -128.0,
                                    ALU.min, ALU.max).then_inc(s_xs, 1)
                link(v.reciprocal(c(nb), c(xscale)))
                dve.wait_ge(s_base, 48)
                link(v.tensor_scalar(c(dq), c(nb), wdq[0:QROWS, :], maskc[0:QROWS, :], ALU.mult, ALU.mult))
            link(v.tensor_tensor(base[0:ROWS, :], base[0:ROWS, :], cls_sb[0:ROWS, :], ALU.add))

            for half in range(2):
                for t in range(4 * half, 4 * half + 4):
                    dve.wait_ge(s_proj, t + 1)
                    if t == 0:
                        dve.wait_ge(s_wabs, 1)
                    link(v.scalar_tensor_tensor(out=h0[0:ROWS, t, :], in0=bank[2 + t % 4][0:ROWS, 0:D],
                                                scalar=dq[0:ROWS, t:t + 1], in1=base[0:ROWS, :], op0=ALU.mult, op1=ALU.add))
                    link(v.bn_stats(bst[0:ROWS, :], h0[0:ROWS, t, :]))
                    v.bn_aggr(mv[0:ROWS, t, :], bst[0:ROWS, :]).then_inc(s_h0, 1)
                dve.wait_ge(s_h0, 4 * half + 4)
                c = lambda a: a[0:ROWS, 4 * half:4 * half + 4]
                var = mv[0:ROWS, 4 * half:4 * half + 4, 1]
                link(v.tensor_scalar(c(nv), var, LN_EPS, None, ALU.add))
                rsqrt(c(r1), c(nv), c(ny), c(na), c(nb))
                link(v.tensor_tensor(c(na), c(r1), c(r1), ALU.mult))
                link(v.tensor_tensor(c(na), c(na), var, ALU.mult))
                link(v.tensor_scalar(c(nv), c(na), LN_EPS, None, ALU.add))
                rsqrt(c(r2), c(nv), c(ny), c(na), c(nb))
                for t in range(4 * half, 4 * half + 4):
                    v.tensor_scalar(resid[0:ROWS, t, :], h0[0:ROWS, t, :], mv[0:ROWS, t, 0:1], r1[0:ROWS, t:t + 1],
                                    ALU.subtract, ALU.mult).then_inc(s_hn, 1)
                    dve.wait_ge(s_hn, t + 1)
                    v.tensor_scalar(z[0:ROWS, t, :], resid[0:ROWS, t, :], r2[0:ROWS, t:t + 1], None,
                                    ALU.mult).then_inc(s_z, 1)

            cos_v = rope_sb[:, 0:S].unsqueeze(1).broadcast_to([128, HB, S])
            sin_v = rope_sb[:, S:2 * S].unsqueeze(1).broadcast_to([128, HB, S])

            def rope_products(half):
                for n in range(16 * half, 16 * half + 16):
                    u = n % 2
                    dve.wait_ge(s_up, n + 1)
                    if n == 0:
                        dve.wait_ge(s_wup, 48)
                        dve.wait_ge(s_xq, NT)
                    if n >= 2:
                        done = 3 * ((n - 2) // 2) + (1 if u == 0 else 3)
                        dve.wait_ge(s_rot, done)
                    for j, (dst, tab) in enumerate(((rope_a, cos_v), (rope_b, sin_v))):
                        v.tensor_tensor(dst[:, u, :].rearrange("p (b s) -> p b s", b=HB),
                                        bank[2 * u + j][:, 0:HN].rearrange("p (b s) -> p b s", b=HB), tab,
                                        ALU.mult).then_inc(s_prod, 1)

            def shift(t):
                for g in range(2):
                    dve.wait_ge(s_sc, 2 * t + g + 1)
                    src = bank[4 + 2 * (t % 2) + g][0:ROWS, 0:4 * 2 * S].rearrange("p (h k) -> p h k", k=S)
                    link(v.tensor_reduce(smax[0:ROWS, t % 2, 8 * g:8 * g + 8], src, AX.X, ALU.max))
                    if g == 0 and t == 0:
                        dve.wait_ge(s_h0, NT)
                    if g == 0 and t >= 2:
                        dve.wait_ge(s_pt, 2 * (t - 2) + 2)
                    p = prob[0:ROWS, t % 2, 4 * g:4 * g + 4, :].rearrange("p m (i k) -> p (m i) k", i=2)[:, :, 0:S]
                    v.tensor_tensor(p, src, smax[0:ROWS, t % 2, 8 * g:8 * g + 8].unsqueeze(2).broadcast_to([ROWS, 8, S]),
                                    ALU.subtract).then_inc(s_sub, 1)

            def row_sums(t):
                dve.wait_ge(s_exp, t + 1)
                if t >= 2:
                    dve.wait_ge(s_pn, t - 1)
                p = prob[0:ROWS, t % 2, :, :].rearrange("p m (i k) -> p (m i) k", i=2)[:, :, 0:S]
                link(v.tensor_reduce(ssum[0:ROWS, t % 2, :], p, AX.X, ALU.add))
                v.reciprocal(ssum[0:ROWS, t % 2, :], ssum[0:ROWS, t % 2, :]).then_inc(s_rs, 1)

            def z_odd_out(half):
                if half:
                    dve.wait_ge(s_oo, NM)
                else:
                    dve.wait_ge(s_res, NT)
                for b in range(HB):
                    dve.wait_ge(s_zz, half * B + 2 * b + 2)
                    v.tensor_copy(ZT[:, 1, :, b * S:(b + 1) * S],
                                  bank[1][:, 0:HN].rearrange("p (m s) -> p m s", m=NM)).then_inc(s_ze1, 1)

            def attn_out(half):
                dve.wait_ge(s_otm, NM * (half + 1))
                dve.wait_ge(s_gap, 2)
                if half:
                    dve.wait_ge(s_bk, 4)
                for c in range(2):
                    v.tensor_copy(aoT[:, c, :].rearrange("p (b s) -> p b s", b=HB)[:, :, 0:S],
                                  bank[4 + c][:, 0:HN].rearrange("p (b s) -> p b s", b=HB)).then_inc(s_ote, 1)

            def h1_and_norm(half):
                for t in range(4 * half, 4 * half + 4):
                    dve.wait_ge(s_bk, t + 1)
                    dve.wait_ge(s_res, NT)
                    v.tensor_tensor(resid[0:ROWS, t, :], bank[6 + t % 2][0:ROWS, 0:D], resid[0:ROWS, t, :],
                                    ALU.add).then_inc(s_h1, 1)
                    dve.wait_ge(s_h1, t + 1)
                    link(v.bn_stats(bst[0:ROWS, :], resid[0:ROWS, t, :]))
                    link(v.bn_aggr(mv[0:ROWS, t, :], bst[0:ROWS, :]))
                c = lambda a: a[0:ROWS, 4 * half:4 * half + 4]
                link(v.tensor_scalar(c(nv), mv[0:ROWS, 4 * half:4 * half + 4, 1], LN_EPS, None, ALU.add))
                rsqrt(c(r1), c(nv), c(ny), c(na), c(nb))

            def hn2_out(t):
                v.tensor_scalar(hn2[0:ROWS, t, :], resid[0:ROWS, t, :], mv[0:ROWS, t, 0:1], r1[0:ROWS, t:t + 1],
                                ALU.subtract, ALU.mult).then_inc(s_hn2, 1)

            rope_products(0)
            shift(0)
            shift(1)
            row_sums(0)
            shift(2)
            row_sums(1)
            shift(3)
            row_sums(2)
            row_sums(3)
            rope_products(1)
            shift(4)
            shift(5)
            row_sums(4)
            row_sums(5)
            z_odd_out(0)
            shift(6)
            shift(7)
            row_sums(6)
            row_sums(7)
            attn_out(0)
            h1_and_norm(0)
            z_odd_out(1)
            attn_out(1)
            h1_and_norm(1)
            for t in range(NT):
                hn2_out(t)

            lg, ex, keep = (r_soft[:, k, :, :] for k in range(3))
            dve.wait_ge(s_lg, 1)
            dve.wait_ge(s_gate, 32)
            link(v.tensor_scalar(lg, bank[4][:, 0:4 * S].rearrange("p (q s) -> p q s", q=4), gbc[:, :], None, ALU.add))
            link(v.tensor_reduce(rq, lg, AX.X, ALU.max))
            v.tensor_tensor(ex, lg, rq.unsqueeze(2).broadcast_to([128, 4, S]), ALU.subtract).then_inc(s_rsub, 1)
            dve.wait_ge(s_rexp, 1)
            link(v.tensor_reduce(rq, ex, AX.X, ALU.add))
            link(v.reciprocal(rq, rq))
            link(v.tensor_tensor(ex, ex, rq.unsqueeze(2).broadcast_to([128, 4, S]), ALU.mult))
            for q in range(4):
                link(v.max(top8[:, q, :], ex[:, q, :]))
            for q in range(4):
                link(v.match_replace(keep[:, q, :], in_to_replace=top8[:, q, :], in_values=ex[:, q, :], imm_value=0.0))
            dve.wait_ge(s_pool1, 1)
            for i in range(2):
                v.tensor_tensor(pm_pad[:, :, 64 * i:64 * i + NPATCH], ex[:, :, 1:S], keep[:, :, 1:S], ALU.subtract)
                last = v.tensor_tensor(pm_pad[:, :, 64 * i + NPATCH:64 * i + S], ex[:, :, 0:1], keep[:, :, 0:1], ALU.subtract)
            last.then_inc(s_pm, 1)
            dve.wait_ge(s_mg, 1)
            v.tensor_copy(merged[:, 0:2, :].rearrange("p q n -> p (q n)"), bank[6][:, :]).then_inc(s_mge, 1)
            dve.wait_ge(s_mt, 1)
            dve.wait_ge(s_pool1, 3)
            v.tensor_copy(mT[:, 0, :, 0:B].rearrange("p e b -> p b e"),
                          bank[0][:, :].rearrange("p (b e) -> p b e", b=B)).then_inc(s_mte, 1)
            dve.wait_ge(s_mte, 2)
            dve.sem_inc(s_the, THE0)
            dve.sem_inc(s_oe, OE0)

            with dve.Fori(0, NG // 2) as it:
                for g in range(2):
                    dve.wait_ge(s_hid, 4 * it + 2 * g - 2 + HID0)
                    v.tensor_copy(stage[:, g, :, :, :], mT[:, :, bass.ds(it * SLOTS + GE * g, GE), :]).then_inc(s_stage, 1)
                    for k in range(2):
                        if k == 0:
                            dve.wait_ge(s_o, 2 * it + g + O0)
                        dve.wait_ge(s_th, 4 * it + 2 * g + k + 1)
                        v.tensor_copy(hT[:, 4 * k:4 * k + 4, :].rearrange("p k n -> p (k n)"),
                                      bank[2 + k][:, :]).then_inc(s_the, 1)
                    dve.wait_ge(s_ob[g], 16 * GE * it + MOVED0)
                    dve.wait_ge(s_o, 2 * it + g + 1 + O0)
                    v.tensor_copy(o_sb[:, g, :], bank[4][:, 0:D]).then_inc(s_oe, 1)

            for p in range(NT // 2):
                dve.wait_ge(s_fin, p + 1)
                r = resid[0:ROWS, 2 * p:2 * p + 2, :].rearrange("p t n -> p (t n)")
                v.tensor_tensor(r, bank[4 + p][0:ROWS, :], r, ALU.add).then_inc(s_fout, 1)


def move_out(act, gr, s_oe, o_all, o_sb, s_ob):
    g = gr % 2
    act.wait_ge(s_oe, gr + 1 + OE0)
    for j in range(GE):
        e = GE * gr + j
        act.dma_start(o_all[e:e + 1, :, :].rearrange("a b n -> a b n"), o_sb[32 * j:32 * j + B, g, :]).then_inc(s_ob[g], 16)


def rope_table():
    inv_freq = 1.0 / 10000.0 ** (np.arange(0, DH, 2, dtype=np.float32) / DH)
    freqs = np.outer(np.arange(S, dtype=np.float32), inv_freq)
    cos = np.concatenate([np.cos(freqs), np.cos(freqs)], -1)[:, ::2]
    sin = np.concatenate([np.sin(freqs), np.sin(freqs)], -1)[:, ::2]
    order = np.r_[1:S, 0]
    cos, sin = cos[order].T, sin[order].T
    return np.concatenate([np.tile(cos, (4, 1)), np.tile(np.concatenate([-sin, sin]), (2, 1))], 1).astype(np.float32)


def head_order():
    even, odd = np.arange(0, DH, 2), np.arange(1, DH, 2)
    one = np.concatenate([even, odd, even])
    return (np.arange(H)[:, None] * DH + one).ravel()


def kernel(**inputs):
    from concourse import bacc
    from concourse.bass_utils import run_bass_kernel_spmd

    a = {k: np.asarray(v) for k, v in inputs.items()}
    x = a["x"].reshape(B, C, GRID, P, GRID, P).transpose(0, 2, 4, 3, 5, 1).reshape(B * NPATCH, DIN)
    x = np.concatenate([x, np.zeros((12, DIN), x.dtype)])
    tokw = a["L0_tok_weight"].T.reshape(KC, 128, D).transpose(1, 0, 2).reshape(128, KC * D)
    pos = np.repeat(a["L0_tok_pos_embedding"].reshape(1, D), ROWS, 0)
    cls = np.zeros((ROWS, D), np.float32)
    cls[NPATCH] = cls[64 + NPATCH] = a["L0_tok_class_token"].reshape(D)
    wd = np.concatenate([a["L0_attn_w_down_q"], a["L0_attn_w_down_kv"]]).T.reshape(2, 128, 2 * DL).transpose(1, 0, 2)
    lnsb = np.concatenate([a["L0_attn_ln_scale"].reshape(2, 128), a["L0_attn_ln_bias"].reshape(2, 128)]).T
    order = head_order()
    mask = np.zeros((128, 1), np.float32)
    mask[0:NPATCH] = mask[64:64 + NPATCH] = 1.0
    sel = np.zeros((GE, GE, 32), np.float32)
    sel[np.arange(GE), np.arange(GE), 0:B] = 1.0
    arrays = dict(
        xr=x, tokw=tokw, clsr=cls, posr=pos, wd=wd, lnsb=lnsb,
        wuq=a["L0_attn_w_up_q"][order].T, wuk=a["L0_attn_w_up_k"][order].T, wuv=a["L0_attn_w_up_v"].T,
        wo=a["L0_attn_w_out"].T.reshape(NM, 128, D).transpose(1, 0, 2),
        gw=a["L0_ffn_gate_w"].T.reshape(2, 128, E).transpose(1, 0, 2),
        gb=np.tile(a["L0_ffn_gate_b"], 4).reshape(128, 1),
        w1=a["L0_ffn_w1"], w2=a["L0_ffn_w2"],
        rope=rope_table(), eye=np.eye(128, dtype=np.float32), rowmask=mask, sel=sel.reshape(GE, 128),
    )
    arrays = {k: np.ascontiguousarray(v) for k, v in arrays.items()}
    nc = bacc.Bacc("TRN2", target_bir_lowering=False, num_devices=1)
    args = {k: nc.dram_tensor(f"in_{k}", v.shape, mybir.dt.from_np(v.dtype), kind="ExternalInput").ap() for k, v in arrays.items()}
    out = nc.dram_tensor("out_0", (B, S, D), fp32, kind="ExternalOutput").ap()
    vit_tower(nc, out=out, **args)
    r = run_bass_kernel_spmd(nc, [{f"in_{k}": v for k, v in arrays.items()}], core_ids=[0])
    return r.results[0]["out_0"]
```

```python
from contextlib import ExitStack

import numpy as np
import concourse.bass as bass
from concourse import mybir

fp32 = mybir.dt.float32
bf16 = mybir.dt.bfloat16
int32 = mybir.dt.int32
ALU = mybir.AluOpType
ACT = mybir.ActivationFunctionType
AX = mybir.AxisListType

B, C, IMG, P = 16, 3, 96, 16
GRID = IMG // P
NPATCH = GRID * GRID
S = NPATCH + 1
D = 256
DIN = P * P * C
KC = DIN // 128
NT = B // 2
ROWS = 64 + S
QROWS = ROWS + 1
HB = B // 2
HN = HB * S
H, DH = 16, 64
NM = H // 2
DL = 128
E, HID, K = 32, 1024, 8
GE = 4
NG = E // GE
SLOTS = 2 * GE
W1N, W2N = 2 * HID, 8 * D
TABLES = 128 + 2 * E + 2 * S + 6
XROWS = 112
SCRATCH = 3
MAGIC = 12582912.0
SEED = 1597463007.0
LN_EPS = 1e-5
HID0, GELU0, THE0, O0, OE0, MOVED0 = 3, 2, 2, 1, 1, 16


def vit_tower(nc, x, tokw, tables, posr, wd, wup, wvo, w1, w2, sel, out):
    ctx = ExitStack()
    with ctx:
        def sb(name, shape, dt=fp32):
            return ctx.enter_context(nc.sbuf_tensor(name, shape, dt))

        def sem(name):
            return ctx.enter_context(nc.semaphore(name))

        def sems(name, n):
            return [sem(f"{name}{i}") for i in range(n)]

        w1_ring = sb("w1_ring", [128, SLOTS, W1N])
        w2_ring = sb("w2_ring", [128, SLOTS, W2N])
        scr1 = w1_ring[:, SCRATCH:SLOTS, :].rearrange("p a n -> p (a n)")
        scr2 = w2_ring[:, SCRATCH:SLOTS, :].rearrange("p a n -> p (a n)")
        r_av = sb("r_av", [128, 1024 + 2048])
        resid = sb("resid", [128, NT, D])
        ckv_dup = sb("ckv_dup", [128, B * ROWS])
        ckv_lo = sb("ckv_lo", [128, HB, 128])
        ckv_hi = sb("ckv_hi", [128, HB, 128])
        r_p = sb("r_p", [128, 2048])
        r_pt = sb("r_pt", [128, NM * HN])
        r_z = sb("r_z", [128, 2 * NM * HN])
        r_ot = sb("r_ot", [128, 2 * HN])
        r_ao = sb("r_ao", [128, 2, HB * 64])
        tab = sb("tab", [128, TABLES])
        ident = tab[:, 0:128]
        gwc = tab[:, 128:128 + 2 * E].rearrange("p (c e) -> p c e", c=2)
        rope_sb = tab[:, 192:192 + 2 * S]
        lnc = tab[:, 192 + 2 * S:196 + 2 * S]
        gbc = tab[:, 196 + 2 * S:197 + 2 * S]
        maskc = tab[:, 197 + 2 * S:198 + 2 * S]
        ident_b = sb("ident_b", [128, 128], bf16)
        small = sb("small", [128, 256])

        k_bd = [scr1[:, 4736 * h:4736 * (h + 1)].rearrange("p (m i n) -> p m i n", m=NM, i=2) for h in range(2)]
        x_sb = scr1[:, 4096:4096 + NT * DIN].rearrange("p (t n) -> p t n", t=NT)
        wuq_sb = scr2[:, 0:H * 96].rearrange("p (m i n) -> p m i n", m=NM, i=2)
        wuk_sb = scr2[:, 1536:1536 + H * 96].rearrange("p (m i n) -> p m i n", m=NM, i=2)
        q_rot = [scr2[:, 3072 + 2368 * h:3072 + 2368 * (h + 1)].rearrange("p (m n) -> p m n", m=NM) for h in range(2)]
        tokw_sb = scr2[:, 5440:5440 + KC * D]
        tokw_q = scr2[:, 6976:6976 + KC * D // 2].bitcast(bf16).rearrange("p (c n) -> p c n", c=KC)
        products = [scr2[:, 7808:7808 + 2 * HN], scr2[:, 8400:8400 + 2 * HN], scr2[:, 9584:9584 + 2 * HN], r_ot[:, :]]
        products = [a.rearrange("p (i n) -> p i n", i=2) for a in products]
        rope_a, rope_b = products[0:2], products[2:4]
        cq = scr2[:, 8992:8992 + B * S]
        wuv_sb = r_av[:, 0:H * DH]
        wo_sb = r_av[:, 1024:3072].rearrange("p (m n) -> p m n", m=NM)
        base = r_p[:, 0:D]
        cls_sb = r_p[:, D:2 * D]
        ones = r_p[:, 2 * D:2 * D + 128]
        junk = r_p[:, 1024:1024 + DIN]
        prob = r_p[:, :].rearrange("p (i m n) -> p i m n", i=2, m=NM)
        xq = r_pt[:, 0:DIN].bitcast(bf16).rearrange("p (i n) -> p i n", i=2)
        zT = r_pt[:, 768:768 + 2 * B * S].rearrange("p (c n) -> p c n", c=2)
        pT = r_pt[:, :].rearrange("p (m n) -> p m n", m=NM)
        h0 = r_z[:, 0:2048].rearrange("p (t n) -> p t n", t=NT)
        z = r_z[:, 2048:4096].rearrange("p (t n) -> p t n", t=NT)
        xqT = r_z[:, 4096:4096 + KC * QROWS].bitcast(bf16).rearrange("p (i c n) -> p i c n", i=2, c=KC)
        wjunk = r_z[:, 0:KC * D]
        ZT = r_z[:, :].rearrange("p (i m n) -> p i m n", i=2, m=NM)
        dup = ckv_dup[:, :].rearrange("p (b n) -> p b n", b=B)
        oT = r_ot[:, :].rearrange("p (i n) -> p i n", i=2)
        wd_sb = r_ao[:, :, 0:256]
        aoT = r_ao
        hn2 = r_p[:, :].rearrange("p (t n) -> p t n", t=NT)
        hn2T = ckv_dup[:, 0:2 * B * S].rearrange("p (c b s) -> p c b s", c=2, b=B)
        r_ex = ckv_dup[:, 1184:1184 + 4 * S].rearrange("p (q s) -> p q s", q=4)
        r_keep = ckv_dup[:, 1332:1332 + 4 * S].rearrange("p (q s) -> p q s", q=4)
        pm_pad = r_ao[:, 0, :].rearrange("p (q n) -> p q n", q=4)
        pmT = r_ao[:, 1, :].rearrange("p (q n) -> p q n", q=4)
        merged = ckv_lo[:, :, :].rearrange("p a n -> p (a n)").rearrange("p (q n) -> p q n", q=4)
        mT = r_pt[:, 0:2048].rearrange("p (c e b) -> p c e b", c=2, e=E)
        hi_flat = ckv_hi[:, :, :].rearrange("p a n -> p (a n)")
        pm_e = hi_flat[0:72, 0:B * S].rearrange("p (b s) -> p b s", b=B)
        sel_sb = hi_flat[0:GE, 640:640 + 128]
        bias1 = r_av[0:GE, 0:2 * HID].rearrange("p (g n) -> p g n", g=2)
        bias2 = r_av[0:GE, 2048:2048 + 2 * D].rearrange("p (g n) -> p g n", g=2)
        stage = r_av[:, 2560:3072].rearrange("p (g c e b) -> p g c e b", g=2, c=2, e=GE)
        hg = r_p[:, 0:HID]
        hT = r_p[:, 1024:2048].rearrange("p (k n) -> p k n", k=8)
        o_sb = r_ot[:, 0:2 * D].rearrange("p (g n) -> p g n", g=2)
        o_all = r_z[0:72, 0:B * D].rearrange("p (b n) -> p b n", b=B)

        at = [0]

        def few(n):
            at[0] += n
            assert at[0] <= 256
            return small[:, at[0] - n:at[0]]

        wsum, wmean, wscale, wdq = few(1), few(1), few(1), few(1)
        ssq, amax, xr_s, xscale, dq = few(NT), few(NT), few(NT), few(NT), few(NT)
        nv, ny, na, nb = few(NT), few(NT), few(NT), few(NT)
        r1, rr = few(NT), few(NT)
        nvv = nv.rearrange("p (k t) -> p k t", k=2)
        mv = few(2 * NT).rearrange("p (t k) -> p t k", k=2)
        bst = few(6)
        smax = few(2 * H).rearrange("p (i h) -> p i h", i=2)
        ssum = few(2 * H).rearrange("p (i h) -> p i h", i=2)
        top8 = few(32).rearrange("p (q k) -> p q k", q=4)
        rq = few(4)

        bank = [ctx.enter_context(nc.psum_tensor(f"bank{i}", [128, 512], fp32)) for i in range(8)]

        s_x = sems("x_in", NT // 2)
        s_tokw, s_base, s_wd, s_tab, s_wup, s_av, s_sel = (
            sem(n) for n in ("tokw_in", "base_in", "wd_in", "tables_in", "wup_in", "av_in", "sel_in"))
        s_w1 = sems("w1_in", SLOTS)
        s_w2 = sems("w2_in", SLOTS)
        s_b1 = sems("b1_in", 2)
        s_b2 = sems("b2_in", 2)
        s_bank = sem("banks_zeroed")
        s_pool0 = sem("pool_constants")
        s_dve, s_actc = sem("dve_chain"), sem("act_chain")
        s_wabs, s_wsum, s_wm, s_wq = (sem(n) for n in ("w_abs", "w_sum", "w_mean", "w_ternary"))
        s_ssq, s_xq, s_xt, s_xte, s_proj, s_h0, s_hn, s_z, s_res = (sem(n) for n in (
            "sum_sq", "x_rounded", "x_turned", "x_turned_out", "projected", "h0_ready",
            "hn_ready", "z_ready", "resid_ready"))
        s_zt, s_zte, s_c, s_ce, s_ct, s_cte = (sem(n) for n in (
            "z_turned", "z_turned_out", "latents", "latents_out", "ckv_turned", "ckv_turned_out"))
        s_up, s_prod, s_rot, s_rotd, s_kbz = (sem(n) for n in (
            "up_done", "rope_products", "rotated", "rotated_second", "k_bd_zeroed"))
        s_sc, s_sub, s_exp, s_rs, s_pn, s_pt, s_pte = (sem(n) for n in (
            "scores", "shifted", "exps", "row_sums", "probs", "probs_turned", "probs_turned_out"))
        s_gap = sem("gaps_zeroed")
        s_zz, s_ze0, s_ze1, s_oo, s_ooe, s_ote, s_bk, s_h1 = (sem(n) for n in (
            "z_done", "z_out_even", "z_out_odd", "heads_done", "heads_out", "attn_out",
            "attn_turned", "h1_ready"))
        s_hn2, s_ht, s_hte, s_lg, s_rsub, s_rexp, s_pm, s_pmt, s_pmte, s_mg, s_mge, s_mt, s_mte, s_pme = (
            sem(n) for n in (
                "hn2_ready", "hn2_turned", "hn2_turned_out", "logits", "logits_shifted", "router_exps",
                "pm_ready", "pm_turned", "pm_turned_out", "merged_done", "merged_out", "merged_turned",
                "merged_turned_out", "pm_e_in"))
        s_pool1 = sem("expert_zeros")
        s_stage, s_hid, s_gelu, s_th, s_the, s_o, s_oe, s_fin, s_fout, s_out = (sem(n) for n in (
            "staged", "hidden", "gelus", "hidden_turned", "hidden_turned_out", "expert_out",
            "expert_out_kept", "scattered", "result", "stored"))
        s_ob = sems("expert_out_moved", 2)
        s_idb = sem("ident_b_ready")
        s_otm = sem("attn_sums")

        block = ctx.enter_context(nc.Block())

        @block.sync
        def _(sp):
            def load_x(p):
                sp.dma_start(x_sb[0:XROWS, 2 * p:2 * p + 2, :], x[:, 2 * p:2 * p + 2, :]).then_inc(s_x[p], 16)

            load_x(0)
            sp.dma_start(tokw_sb, tokw).then_inc(s_tokw, 16)
            load_x(1)
            sp.dma_start(tab[:, :], tables).then_inc(s_tab, 16)
            sp.dma_start(r_p[:, 0:2 * D], posr).then_inc(s_base, 16)
            sp.dma_start(wd_sb, wd).then_inc(s_wd, 16)
            sp.dma_start(scr2[:, 0:3072], wup).then_inc(s_wup, 16)
            load_x(2)
            load_x(3)
            sp.dma_start(r_av[:, :], wvo).then_inc(s_av, 16)

            def load_w1(e, slot):
                sp.dma_start(w1_ring[:, slot, :],
                             w1[bass.ds(e, 1), 0:D, :].rearrange("a (p c) h -> p (a c h)", c=2)).then_inc(s_w1[slot], 16)

            def load_w2(e, slot):
                sp.dma_start(w2_ring[:, slot, :],
                             w2[bass.ds(e, 1), 0:HID, :].rearrange("a (p c) h -> p (a c h)", c=8)).then_inc(s_w2[slot], 16)

            def load_b1(e, g):
                sp.dma_start(bias1[:, g, :], w1[bass.ds(e, GE), D:D + 1, :].rearrange("e a h -> e (a h)")).then_inc(s_b1[g], 16)

            def load_b2(e, g):
                sp.dma_start(bias2[:, g, :], w2[bass.ds(e, GE), HID:HID + 1, :].rearrange("e a h -> e (a h)")).then_inc(s_b2[g], 16)

            for e in range(SCRATCH):
                load_w1(e, e)
            for e in range(SCRATCH):
                load_w2(e, e)
            sp.wait_ge(s_sc, 2 * NT)
            for e in range(SCRATCH, SLOTS):
                load_w1(e, e)
            for e in range(SCRATCH, SLOTS):
                load_w2(e, e)
            sp.wait_ge(s_otm, 2 * NM)
            for g in range(2):
                load_b1(GE * g, g)
                load_b2(GE * g, g)
            with sp.Fori(1, NG // 2) as it:
                for g in range(2):
                    sp.wait_ge(s_hid, 4 * it + 2 * g - 2 + HID0)
                    load_b1(it * SLOTS + GE * g, g)
                    for j in range(GE):
                        load_w1(it * SLOTS + GE * g + j, GE * g + j)
                    sp.wait_ge(s_o, 2 * it + g - 1 + O0)
                    load_b2(it * SLOTS + GE * g, g)
                    for j in range(GE):
                        load_w2(it * SLOTS + GE * g + j, GE * g + j)
            for p in range(NT // 2):
                sp.wait_ge(s_fout, p + 1)
                for i in range(2):
                    o_v = out.rearrange("(t i) s d -> i s t d", i=2)
                    sp.dma_start(o_v[i, 1:S, 2 * p:2 * p + 2, :],
                                 resid[64 * i:64 * i + NPATCH, 2 * p:2 * p + 2, :]).then_inc(s_out, 16)
                    sp.dma_start(o_v[i, 0:1, 2 * p:2 * p + 2, :],
                                 resid[64 * i + NPATCH:64 * i + S, 2 * p:2 * p + 2, :]).then_inc(s_out, 16)
            sp.wait_ge(s_out, 16 * 2 * NT)

        @block.gpsimd
        def _(pool):
            pool.memset(ones, 1.0).then_inc(s_pool0, 1)
            pool.memset(ckv_dup[:, :], 0.0).then_inc(s_pool0, 1)
            pool.memset(ckv_lo[:, :, :], 0.0).then_inc(s_pool0, 1)
            pool.memset(ckv_hi[:, :, :], 0.0).then_inc(s_pool0, 1)
            def zero_k(half):
                pool.wait_ge(s_xq, NT if half else 1)
                pool.memset(k_bd[half][0:64, :, 1, :], 0.0).then_inc(s_kbz, 1)
                pool.wait_ge(s_kbz, 2 * half + 1)
                pool.memset(k_bd[half][64:128, :, 0, :], 0.0).then_inc(s_kbz, 1)
                pool.wait_ge(s_kbz, 2 * half + 2)

            def residual(t):
                pool.wait_ge(s_hn, t + 1)
                pool.tensor_tensor(resid[0:ROWS, t, :], h0[0:ROWS, t, :], resid[0:ROWS, t, :], ALU.add).then_inc(s_res, 1)

            def rotate(half, m):
                n = half * NM + m
                if n == NM:
                    pool.wait_ge(s_proj, NT)
                pool.wait_ge(s_prod, 4 * n + 2)
                pool.tensor_tensor(q_rot[half][:, m, :], rope_a[n % 2][:, 0, :], rope_b[n % 2][:, 0, :], ALU.add).then_inc(s_rot, 1)
                pool.wait_ge(s_prod, 4 * n + 4)
                pool.tensor_tensor(k_bd[half][0:64, m, 0, :], rope_a[n % 2][0:64, 1, :],
                                   rope_b[n % 2][0:64, 1, :], ALU.add).then_inc(s_rot, 1)

            def normalise(t):
                pool.wait_ge(s_rs, t + 1)
                p = prob[0:ROWS, t % 2, :, :].rearrange("p m (i k) -> p (m i) k", i=2)[:, :, 0:S]
                pool.tensor_tensor(p, p, ssum[0:ROWS, t % 2, :].unsqueeze(2).broadcast_to([ROWS, H, S]),
                                   ALU.mult).then_inc(s_pn, 1)
                pool.wait_ge(s_pn, t + 1)

            zero_k(0)
            for t in range(4):
                residual(t)
            for m in range(NM):
                rotate(0, m)
            for t in range(4, NT):
                residual(t)
            pool.wait_ge(s_h0, NT)
            pool.wait_ge(s_wm, 1)
            pool.memset(prob[:, :, :, 37:64], 0.0).then_inc(s_gap, 1)
            pool.wait_ge(s_c, 4)
            pool.memset(aoT[:, :, :], 0.0).then_inc(s_gap, 1)
            pool.wait_ge(s_gap, 2)
            zero_k(1)
            for t in range(4):
                rotate(1, 2 * t)
                rotate(1, 2 * t + 1)
                normalise(t)
            for t in range(4, NT):
                normalise(t)
            pool.wait_ge(s_zz, 2 * B)
            pool.memset(hi_flat[:, 0:B * S], 0.0).then_inc(s_pool1, 1)
            pool.memset(mT[:, :, :, :], 0.0).then_inc(s_pool1, 1)
            pool.wait_ge(s_oo, 2 * NM)
            pool.memset(r_z[0:72, 0:B * D], 0.0).then_inc(s_pool1, 1)
            pool.wait_ge(s_bk, NT)
            pool.memset(pm_pad, 0.0).then_inc(s_pool1, 1)

        @block.scalar
        def _(act):
            def square_sum(t):
                act.wait_ge(s_x[t // 2], 16)
                if t >= 1:
                    act.wait_ge(s_ssq, t)
                act.activation(junk[0:QROWS, :], x_sb[0:QROWS, t, :], ACT.Square,
                               accum_out=ssq[0:QROWS, t:t + 1]).then_inc(s_ssq, 1)

            def xq_out(t):
                act.wait_ge(s_xt, t + 1)
                if t >= 2:
                    act.wait_ge(s_proj, t - 1)
                act.activation(xqT[:, t % 2, :, :].rearrange("p c n -> p (c n)"),
                               bank[4 + t % 2][:, :].bitcast(bf16)[:, 0:KC * QROWS], ACT.Copy).then_inc(s_xte, 1)

            square_sum(0)
            square_sum(1)
            act.wait_ge(s_tokw, 16)
            act.activation(wjunk, tokw_sb, ACT.Abs, accum_out=wsum).then_inc(s_wabs, 1)
            for t in range(2, NT):
                square_sum(t)
            for t in range(4):
                xq_out(t)

            def z_out(t):
                act.wait_ge(s_zt, t + 1)
                if t == 0:
                    act.wait_ge(s_tab, 16)
                for c in range(2):
                    act.activation(zT[:, c, 2 * t * S:2 * t * S + 2 * S].rearrange("p (i s) -> p i s", i=2),
                                   bank[4 + t % 2][:, c * 128:(c + 1) * 128].rearrange("p (i s) -> p i s", i=2)[:, :, 0:S],
                                   ACT.Identity, bias=lnc[:, 2 + c:3 + c], scale=lnc[:, c:c + 1]).then_inc(s_zte, 1)

            def latents_out(half):
                act.wait_ge(s_c, 2 * half + 1)
                act.activation(cq[:, half * HN:(half + 1) * HN], bank[6][:, 0:HN], ACT.Copy).then_inc(s_ce, 1)
                act.wait_ge(s_c, 2 * half + 2)
                act.wait_ge(s_pool0, 2)
                for i in range(2):
                    act.activation(dup[:, half * HB:(half + 1) * HB, 64 * i:64 * i + S],
                                   bank[7][:, 0:HN].rearrange("p (b s) -> p b s", b=HB),
                                   ACT.Copy).then_inc(s_ce, 1)

            def ckv_out(half):
                act.wait_ge(s_pool0, 4)
                if half:
                    act.wait_ge(s_zz, B)
                for g in range(2):
                    act.wait_ge(s_ct, 2 * half + g + 1)
                    src = bank[4 + g][:, :].rearrange("p (b n) -> p b n", b=4)
                    act.activation(ckv_lo[0:S, 4 * g:4 * g + 4, :], src[0:S, :, :], ACT.Copy).then_inc(s_cte, 1)
                    act.activation(ckv_hi[64:64 + S, 4 * g:4 * g + 4, :], src[64:64 + S, :, :], ACT.Copy).then_inc(s_cte, 1)

            def exps(t):
                act.wait_ge(s_sub, 2 * t + 2)
                p = prob[0:ROWS, t % 2, :, :].rearrange("p m (i k) -> p (m i) k", i=2)[:, :, 0:S]
                act.activation(p, p, ACT.Exp, scale=DH ** -0.5).then_inc(s_exp, 1)

            def probs_out(t):
                if t == 0:
                    act.wait_ge(s_ce, 6)
                if t >= 4:
                    act.wait_ge(s_zz, 4 * (t - 4) + 4)
                for g in range(2):
                    act.wait_ge(s_pt, 2 * t + g + 1)
                    act.activation(
                        pT[0:ROWS, 4 * g:4 * g + 4, 2 * (t % 4) * S:2 * (t % 4) * S + 2 * S].rearrange("p m (i q) -> p m i q", i=2),
                        bank[6 + g][0:ROWS, :].rearrange("p (m i q) -> p m i q", m=4, i=2)[:, :, :, 0:S],
                        ACT.Copy).then_inc(s_pte, 1)

            def z_even_out(half, b):
                if b == 0:
                    if half:
                        act.wait_ge(s_oo, NM)
                    else:
                        act.wait_ge(s_res, NT)
                act.wait_ge(s_zz, half * B + 2 * b + 1)
                act.activation(ZT[:, 0, :, b * S:(b + 1) * S],
                               bank[0][:, 0:HN].rearrange("p (m s) -> p m s", m=NM), ACT.Copy).then_inc(s_ze0, 1)

            def heads_out(half, m):
                n = half * NM + m
                act.wait_ge(s_oo, n + 1)
                if n >= 2:
                    act.wait_ge(s_otm, n - 1)
                act.activation(oT[:, m % 2, :], bank[m % 2][:, 0:HN], ACT.Copy).then_inc(s_ooe, 1)

            def hn2_turned_out(t):
                if t == 0:
                    act.wait_ge(s_ct, 4)
                act.wait_ge(s_ht, t + 1)
                src = bank[4 + t % 2][:, 0:256].rearrange("p (c i s) -> p c i s", c=2, i=2)
                dst = hn2T[:, :, 2 * t:2 * t + 2, :]
                act.activation(dst[:, :, :, 1:S], src[:, :, :, 0:NPATCH], ACT.Copy).then_inc(s_hte, 1)
                act.activation(dst[:, :, :, 0:1], src[:, :, :, NPATCH:S], ACT.Copy).then_inc(s_hte, 1)

            def router_exps(half):
                act.wait_ge(s_rsub, half + 1)
                ex = r_ex[:, 2 * half:2 * half + 2, :]
                act.activation(ex, ex, ACT.Exp).then_inc(s_rexp, 1)

            for t in range(4):
                z_out(t)
            latents_out(0)
            ckv_out(0)
            for t in range(4, NT):
                xq_out(t)
            for t in range(4, NT):
                z_out(t)
            latents_out(1)
            exps(0)
            exps(1)
            probs_out(0)
            exps(2)
            probs_out(1)
            exps(3)
            probs_out(2)
            probs_out(3)
            z_even_out(0, 0)
            exps(4)
            z_even_out(0, 1)
            z_even_out(0, 2)
            exps(5)
            for b in range(3, 6):
                z_even_out(0, b)
            probs_out(4)
            exps(6)
            z_even_out(0, 6)
            z_even_out(0, 7)
            probs_out(5)
            exps(7)
            heads_out(0, 0)
            heads_out(0, 1)
            probs_out(6)
            for m in range(2, 5):
                heads_out(0, m)
            probs_out(7)
            for m in range(5, NM):
                heads_out(0, m)
            ckv_out(1)
            for b in range(HB):
                z_even_out(1, b)
            for t in range(4):
                hn2_turned_out(t)
            for m in range(NM):
                heads_out(1, m)
                if m == 2:
                    router_exps(0)
            for t in range(4, NT):
                hn2_turned_out(t)
            router_exps(1)

            act.wait_ge(s_pmt, 1)
            act.activation(pmT[0:ROWS, :, :].rearrange("p q n -> p (q n)"), bank[7][0:ROWS, :], ACT.Copy).then_inc(s_pmte, 1)
            act.wait_ge(s_mg, 2)
            act.activation(merged[:, 2:4, :].rearrange("p q n -> p (q n)"), bank[3][:, :], ACT.Copy).then_inc(s_mge, 1)
            act.wait_ge(s_zz, 2 * B)
            act.dma_start(sel_sb, sel).then_inc(s_sel, 16)
            act.wait_ge(s_pool1, 1)
            act.wait_ge(s_pm, 1)
            for i in range(4):
                act.dma_start(pm_e[0:E, :, :].rearrange("p (q i) s -> p i q s", i=4)[:, i, :, :],
                              pm_pad[32 * i:32 * i + 32, :, 0:S]).then_inc(s_pme, 16)
            act.wait_ge(s_mt, 2)
            act.wait_ge(s_pool1, 2)
            act.activation(mT[:, 1, :, 0:B].rearrange("p e b -> p b e"),
                           bank[1][:, :].rearrange("p (b e) -> p b e", b=B), ACT.Copy).then_inc(s_mte, 1)
            act.sem_inc(s_gelu, GELU0)
            for g in range(2):
                act.sem_inc(s_ob[g], MOVED0)
            act.wait_ge(s_mte, 2)
            act.wait_ge(s_pool1, 4)
            for gr in range(NG):
                for n in range(2):
                    act.wait_ge(s_hid, 2 * gr + n + 1 + HID0)
                    if gr >= 1 and n == 0:
                        act.wait_ge(s_th, 2 * gr)
                    act.activation(hg[:, n * 512:(n + 1) * 512], bank[n][:, :], ACT.Gelu).then_inc(s_gelu, 1)
                if gr >= 1:
                    move_out(act, gr - 1, s_oe, o_all, o_sb, s_ob)
            move_out(act, NG - 1, s_oe, o_all, o_sb, s_ob)

        @block.tensor
        def _(pe):
            mm, tr = nc.tensor.matmul, nc.tensor.transpose
            pe.wait_ge(s_bank, 4)
            pe.wait_ge(s_pool0, 1)
            pe.wait_ge(s_wabs, 1)
            mm(bank[0][:, 0:1], ones, wsum, start=True, stop=True).then_inc(s_wsum, 1)

            def turn_x(t):
                pe.wait_ge(s_xq, t + 1)
                if t == 0:
                    pe.wait_ge(s_idb, 1)
                if t in (2, 3, 5, 6, 7):
                    pe.wait_ge(s_xte, t - 1)
                if t == 4:
                    pe.wait_ge(s_cte, 4)
                for c in range(KC):
                    last = tr(bank[4 + t % 2][:, :].bitcast(bf16)[:, c * QROWS:(c + 1) * QROWS],
                              xq[0:QROWS, t % 2, c * 128:(c + 1) * 128], ident_b[0:QROWS, 0:QROWS])
                last.then_inc(s_xt, 1)

            def project(t):
                pe.wait_ge(s_xte, t + 1)
                if t == 0:
                    pe.wait_ge(s_wq, 1)
                if t == 4:
                    pe.wait_ge(s_ce, 3)
                if t >= 2:
                    pe.wait_ge(s_h0, t - 1)
                for c in range(KC):
                    last = mm(bank[6 + t % 2][0:ROWS, 0:D], xqT[:, t % 2, c, 0:ROWS], tokw_q[:, c, :],
                              start=(c == 0), stop=(c == KC - 1))
                last.then_inc(s_proj, 1)

            def turn_z(t):
                pe.wait_ge(s_z, t + 1)
                if t == 0:
                    pe.wait_ge(s_tab, 16)
                if t % 4 == 0:
                    pe.wait_ge(s_xte, t + 4)
                if t % 4 >= 2:
                    pe.wait_ge(s_zte, 2 * (t - 1))
                for c in range(2):
                    last = tr(bank[4 + t % 2][:, c * 128:c * 128 + ROWS], z[0:ROWS, t, c * 128:(c + 1) * 128],
                              ident[0:ROWS, 0:ROWS])
                last.then_inc(s_zt, 1)

            def latents(half):
                if half == 0:
                    pe.wait_ge(s_wd, 16)
                pe.wait_ge(s_h0, 4 * half + 4)
                pe.wait_ge(s_zte, NT * (half + 1))
                for u in range(2):
                    for c in range(2):
                        last = mm(bank[6 + u][:, 0:HN], wd_sb[:, c, u * DL:(u + 1) * DL],
                                  zT[:, c, half * HN:(half + 1) * HN], start=(c == 0), stop=(c == 1))
                    last.then_inc(s_c, 1)

            def turn_ckv(half):
                pe.wait_ge(s_ce, 3 * half + 3)
                if half:
                    pe.wait_ge(s_sub, 2 * NT)
                for g in range(2):
                    for b in range(4):
                        last = tr(bank[4 + g][0:ROWS, b * 128:(b + 1) * 128], dup[:, half * HB + 4 * g + b, :], ident[:, :])
                    last.then_inc(s_ct, 1)

            def up(half, m):
                for u, w in enumerate((wuq_sb, wuk_sb)):
                    n = (half * NM + m) * 2 + u
                    if n == 0:
                        pe.wait_ge(s_wup, 16)
                        pe.wait_ge(s_wm, 1)
                    if m == 0 and u == 0:
                        pe.wait_ge(s_ce, 3 * (half + 1))
                    if n >= 2:
                        pe.wait_ge(s_prod, 2 * (n - 2) + 2)
                    rhs = cq[:, half * HN:(half + 1) * HN] if u == 0 else dup[:, half * HB:(half + 1) * HB, 0:S]
                    for j in range(2):
                        for i in range(2):
                            last = mm(bank[2 * u + j][64 * i:64 * i + 64, 0:HN], w[:, m, i, 32 * j:32 * j + 64], rhs,
                                      start=True, stop=True)
                    last.then_inc(s_up, 1)

            def scores(t):
                half = t // 4
                pe.wait_ge(s_rot, 2 * NM * (half + 1))
                pe.wait_ge(s_rotd, NM * (half + 1))
                pe.wait_ge(s_kbz, 2 * half + 2)
                if t == 0:
                    pe.wait_ge(s_zte, 2 * NT)
                if t >= 1:
                    pe.wait_ge(s_sub, 2 * t)
                for g in range(2):
                    for mq in range(4):
                        for i in range(2):
                            b = 2 * (t % 4) + i
                            m = 4 * g + mq
                            last = mm(bank[4 + g][64 * i:64 * i + S, mq * 2 * S:(mq + 1) * 2 * S],
                                      q_rot[half][:, m, b * S:(b + 1) * S], k_bd[half][:, m, :, b * S:(b + 1) * S],
                                      start=True, stop=True)
                    last.then_inc(s_sc, 1)

            def turn_probs(t):
                pe.wait_ge(s_pn, t + 1)
                if t == 0:
                    pe.wait_ge(s_gap, 1)
                    pe.wait_ge(s_ce, 6)
                if t >= 1:
                    pe.wait_ge(s_pte, 2 * t)
                for g in range(2):
                    for mq in range(4):
                        last = tr(bank[6 + g][0:ROWS, mq * 128:mq * 128 + ROWS],
                                  prob[0:ROWS, t % 2, 4 * g + mq, 0:ROWS], ident[0:ROWS, 0:ROWS])
                    last.then_inc(s_pt, 1)

            def values(half, b):
                if b == 0:
                    pe.wait_ge(s_pte, 8 * (half + 1))
                    pe.wait_ge(s_cte, 4 * (half + 1))
                    if half == 0:
                        pe.wait_ge(s_prod, 8 * NM)
                    else:
                        pe.wait_ge(s_ooe, NM)
                for par, ck in enumerate((ckv_lo, ckv_hi)):
                    if b >= 1:
                        pe.wait_ge((s_ze0, s_ze1)[par], half * HB + b)
                    mm(bank[par][:, 0:HN], ck[0:ROWS, b, :], pT[0:ROWS, :, b * S:(b + 1) * S],
                       start=True, stop=True).then_inc(s_zz, 1)

            def combine(half, m):
                pe.wait_ge(s_ooe, half * NM + m + 1)
                if m == 0 and half:
                    pe.wait_ge(s_ote, 2)
                for c in range(2):
                    last = mm(bank[2 + c][:, 0:HN], wo_sb[:, m, c * 128:(c + 1) * 128], oT[:, m % 2, :],
                              start=(m == 0), stop=(m == NM - 1))
                last.then_inc(s_otm, 1)

            def heads(half, m):
                n = half * NM + m
                if m == 0:
                    pe.wait_ge(s_ze0, HB * (half + 1))
                    pe.wait_ge(s_ze1, HB * (half + 1))
                    pe.wait_ge(s_av, 16)
                if m >= 2:
                    pe.wait_ge(s_ooe, n - 1)
                for par in range(2):
                    h = 2 * m + par
                    last = mm(bank[m % 2][64 * par:64 * par + 64, 0:HN], wuv_sb[:, h * DH:(h + 1) * DH],
                              ZT[:, par, m, :], start=True, stop=True)
                last.then_inc(s_oo, 1)
                if m >= 1:
                    combine(half, m - 1)
                if m == NM - 1:
                    combine(half, m)

            def turn_back(t):
                if t % 4 == 0:
                    pe.wait_ge(s_ote, 2 * (t // 4) + 2)
                    if t == 0:
                        pe.wait_ge(s_pte, 16)
                    else:
                        pe.wait_ge(s_rsub, 1)
                if t % 4 >= 2:
                    pe.wait_ge(s_h1, t - 1)
                for c in range(2):
                    last = tr(bank[6 + t % 2][0:ROWS, c * 128:(c + 1) * 128], aoT[:, c, (t % 4) * 128:(t % 4) * 128 + ROWS],
                              ident[:, :])
                last.then_inc(s_bk, 1)

            def turn_hn2(t):
                pe.wait_ge(s_hn2, t + 1)
                if t == 0:
                    pe.wait_ge(s_cte, 8)
                if t >= 2:
                    pe.wait_ge(s_hte, 2 * (t - 1))
                for c in range(2):
                    last = tr(bank[4 + t % 2][:, c * 128:c * 128 + ROWS], hn2[0:ROWS, t, c * 128:(c + 1) * 128],
                              ident[0:ROWS, 0:ROWS])
                last.then_inc(s_ht, 1)

            def logits(half):
                pe.wait_ge(s_tab, 16)
                pe.wait_ge(s_h1, 4 * half + 4)
                pe.wait_ge(s_hte, 8 * (half + 1))
                for q in range(2 * half, 2 * half + 2):
                    for i in range(4):
                        for c in range(2):
                            last = mm(bank[6][32 * i:32 * i + 32, q * S:(q + 1) * S], gwc[:, c, :], hn2T[:, c, 4 * q + i, :],
                                      start=(c == 0), stop=(c == 1))
                last.then_inc(s_lg, 1)

            for t in range(4):
                turn_x(t)
                if t >= 1:
                    project(t - 1)
            project(3)
            for t in range(4):
                turn_z(t)
            latents(0)
            up(0, 0)
            turn_ckv(0)
            turn_x(4)
            up(0, 1)
            turn_x(5)
            project(4)
            up(0, 2)
            project(5)
            turn_x(6)
            up(0, 3)
            turn_x(7)
            project(6)
            up(0, 4)
            project(7)
            up(0, 5)
            for t in range(4, NT):
                turn_z(t)
            up(0, 6)
            latents(1)
            up(0, 7)
            scores(0)
            up(1, 0)
            up(1, 1)
            for t in range(1, 4):
                scores(t)
                up(1, 2 * t)
                turn_probs(t - 1)
                up(1, 2 * t + 1)
            turn_probs(3)
            scores(4)
            for b in range(3):
                values(0, b)
            scores(5)
            for b in range(3, 6):
                values(0, b)
            turn_probs(4)
            scores(6)
            values(0, 6)
            values(0, 7)
            turn_probs(5)
            scores(7)
            heads(0, 0)
            heads(0, 1)
            turn_probs(6)
            for m in range(2, 5):
                heads(0, m)
            turn_probs(7)
            for m in range(5, NM):
                heads(0, m)
            for t in range(4):
                turn_back(t)
            turn_ckv(1)
            for b in range(HB):
                values(1, b)
            for t in range(4):
                turn_hn2(t)
            logits(0)
            for m in range(NM):
                heads(1, m)
            for t in range(4, NT):
                turn_back(t)
            for t in range(4, NT):
                turn_hn2(t)
            logits(1)

            pe.wait_ge(s_pm, 1)
            for q in range(4):
                last = tr(bank[7][0:ROWS, q * 128:(q + 1) * 128], pm_pad[:, q, 0:ROWS], ident[:, :])
            last.then_inc(s_pmt, 1)
            pe.wait_ge(s_pmte, 1)
            pe.wait_ge(s_ote, 4)
            for q in range(4):
                for i in range(4):
                    b, lo = 4 * q + i, 64 * (i % 2)
                    last = mm(bank[2 + q // 2][32 * i:32 * i + 32, (q % 2) * D:(q % 2 + 1) * D],
                              pmT[lo:lo + S, q, 32 * i:32 * i + 32], hn2[lo:lo + S, b // 2, :], start=True, stop=True)
                if q % 2:
                    last.then_inc(s_mg, 1)
            pe.wait_ge(s_mge, 2)
            pe.wait_ge(s_ooe, 2 * NM)
            for c in range(2):
                for q in range(4):
                    last = tr(bank[c][:, q * 128:(q + 1) * 128], merged[:, q, c:D:2], ident[:, :])
                last.then_inc(s_mt, 1)
            pe.wait_ge(s_sel, 16)
            pe.wait_ge(s_mte, 2)
            pe.sem_inc(s_hid, HID0)
            pe.sem_inc(s_o, O0)

            with pe.Fori(0, NG // 2) as it:
                for g in range(2):
                    for n in range(2):
                        if n == 0:
                            pe.wait_ge(s_b1[g], 16 * it + 16)
                            pe.wait_ge(s_stage, 2 * it + g + 1)
                        pe.wait_ge(s_gelu, 4 * it + 2 * g + n - 1 + GELU0)
                        for c in range(2):
                            for j in range(GE):
                                if n == 0 and c == 0:
                                    pe.wait_ge(s_w1[GE * g + j], 16 * it + 16)
                                last = mm(bank[n][32 * j:32 * j + 32, :], stage[:, g, c, j, :],
                                          w1_ring[:, GE * g + j, c * HID + n * 512:c * HID + (n + 1) * 512],
                                          start=(c == 0), stop=False, skip_group_check=True)
                        mm(bank[n][:, :], sel_sb[:, :], bias1[:, g, n * 512:(n + 1) * 512], start=False, stop=True,
                           skip_group_check=True).then_inc(s_hid, 1)
                    pe.wait_ge(s_gelu, 4 * it + 2 * g + 2 + GELU0)
                    pe.wait_ge(s_the, 4 * it + 2 * g + THE0)
                    for k in range(8):
                        last = tr(bank[2 + k // 4][:, (k % 4) * 128:(k % 4 + 1) * 128], hg[:, k:HID:8], ident[:, :])
                        if k % 4 == 3:
                            last.then_inc(s_th, 1)
                    pe.wait_ge(s_oe, 2 * it + g + OE0)
                    pe.wait_ge(s_b2[g], 16 * it + 16)
                    pe.wait_ge(s_the, 4 * it + 2 * g + 2 + THE0)
                    for k in range(8):
                        for j in range(GE):
                            if k == 0:
                                pe.wait_ge(s_w2[GE * g + j], 16 * it + 16)
                            last = mm(bank[4][32 * j:32 * j + 32, 0:D], hT[:, k, 32 * j:32 * j + 32],
                                      w2_ring[:, GE * g + j, k * D:(k + 1) * D], start=(k == 0), stop=False,
                                      skip_group_check=True)
                    mm(bank[4][:, 0:D], sel_sb[:, :], bias2[:, g, :], start=False, stop=True,
                       skip_group_check=True).then_inc(s_o, 1)

            pe.wait_ge(s_pme, 64)
            for g in range(2):
                pe.wait_ge(s_ob[g], 16 * GE * NG // 2 + MOVED0)
            pe.wait_ge(s_oe, NG + OE0)
            for b in range(B):
                t, i = b // 2, b % 2
                last = mm(bank[4 + t // 2][64 * i:64 * i + S, (t % 2) * D:(t % 2 + 1) * D], pm_e[:, b, :], o_all[:, b, :],
                          start=True, stop=True)
                if b % 4 == 3:
                    last.then_inc(s_fin, 1)

        @block.vector
        def _(dve):
            v = nc.vector
            count = [0]

            def link(ins):
                count[0] += 1
                ins.then_inc(s_dve, 1)
                dve.wait_ge(s_dve, count[0])

            def rsqrt(dst, src, tmp_y, tmp_a, tmp_b):
                link(v.tensor_scalar(tmp_y.bitcast(int32), src.bitcast(int32), -0.5, SEED, ALU.mult, ALU.add))
                y = tmp_y
                for step in range(3):
                    link(v.tensor_tensor(tmp_a, y, y, ALU.mult))
                    link(v.scalar_tensor_tensor(out=tmp_b, in0=tmp_a, scalar=-0.5, in1=src, op0=ALU.mult, op1=ALU.mult))
                    new = dst if step == 2 else tmp_y
                    link(v.scalar_tensor_tensor(out=new, in0=tmp_b, scalar=1.5, in1=y, op0=ALU.add, op1=ALU.mult))

            for i in range(4, 8):
                v.memset(bank[i][:, :], 0.0).then_inc(s_bank, 1)
            dve.wait_ge(s_tab, 16)
            v.tensor_copy(ident_b[:, :], ident[:, :]).then_inc(s_idb, 1)

            def ternary_weights():
                link(v.tensor_scalar(tokw_sb, tokw_sb, wscale, MAGIC, ALU.mult, ALU.add))
                link(v.tensor_scalar(tokw_sb, tokw_sb, -MAGIC, 1.0, ALU.add, ALU.min))
                v.tensor_scalar(tokw_q.rearrange("p c n -> p (c n)"), tokw_sb, -1.0, None, ALU.max).then_inc(s_wq, 1)

            def patch_scales(lo, hi):
                for t in range(lo, hi):
                    dve.wait_ge(s_x[t // 2], 16)
                    link(v.tensor_reduce(amax[0:QROWS, t:t + 1], x_sb[0:QROWS, t, :], AX.X, ALU.max, apply_absolute_value=True))
                dve.wait_ge(s_ssq, hi)
                c = lambda a: a[0:QROWS, lo:hi]
                link(v.tensor_scalar(c(nv), c(ssq), 1.0 / DIN, 1e-6, ALU.mult, ALU.add))
                rsqrt(c(xr_s), c(nv), c(ny), c(na), c(nb))
                link(v.tensor_tensor(c(na), c(amax), c(xr_s), ALU.mult))
                link(v.tensor_scalar(c(na), c(na), 1e-5, None, ALU.max))
                link(v.reciprocal(c(nb), c(na)))
                link(v.tensor_scalar(c(xscale), c(nb), 127.0, None, ALU.mult))
                if lo == 0:
                    dve.wait_ge(s_wsum, 1)
                    v.tensor_scalar(wmean, bank[0][:, 0:1], 1.0 / (DIN * D), 1e-5, ALU.mult, ALU.max).then_inc(s_wm, 1)
                    dve.wait_ge(s_wm, 1)
                    link(v.reciprocal(wscale, wmean))
                    link(v.reciprocal(wdq, wscale))
                link(v.reciprocal(c(nb), c(xscale)))
                dve.wait_ge(s_tab, 16)
                link(v.tensor_scalar(c(dq), c(nb), wdq[0:QROWS, :], maskc[0:QROWS, :], ALU.mult, ALU.mult))

            def quantise(t):
                if t >= 2:
                    dve.wait_ge(s_xt, t - 1)
                link(v.tensor_scalar(x_sb[0:QROWS, t, :], x_sb[0:QROWS, t, :], xr_s[0:QROWS, t:t + 1],
                                     xscale[0:QROWS, t:t + 1], ALU.mult, ALU.mult))
                v.tensor_scalar(xq[0:QROWS, t % 2, :], x_sb[0:QROWS, t, :], MAGIC, -MAGIC,
                                ALU.add, ALU.add).then_inc(s_xq, 1)

            def tokens(t):
                dve.wait_ge(s_proj, t + 1)
                if t == 0:
                    dve.wait_ge(s_wabs, 1)
                link(v.scalar_tensor_tensor(out=h0[0:ROWS, t, :], in0=bank[6 + t % 2][0:ROWS, 0:D],
                                            scalar=dq[0:ROWS, t:t + 1], in1=base[0:ROWS, :], op0=ALU.mult, op1=ALU.add))
                link(v.bn_stats(bst[0:ROWS, :], h0[0:ROWS, t, :]))
                v.bn_aggr(mv[0:ROWS, t, :], bst[0:ROWS, :]).then_inc(s_h0, 1)

            def norms(half):
                dve.wait_ge(s_h0, 4 * half + 4)
                var = mv[0:ROWS, 4 * half:4 * half + 4, 1]
                nv1, nv2 = nvv[0:ROWS, 0, :], nvv[0:ROWS, 1, :]
                link(v.tensor_scalar(nv1, var, LN_EPS, None, ALU.add))
                link(v.scalar_tensor_tensor(out=nv2, in0=nv1, scalar=LN_EPS, in1=var, op0=ALU.mult, op1=ALU.add))
                c = lambda a: a[0:ROWS, :]
                rsqrt(c(rr), c(nv), c(ny), c(na), c(nb))
                for t in range(4 * half, 4 * half + 4):
                    j = t % 4
                    v.tensor_scalar(z[0:ROWS, t, :], h0[0:ROWS, t, :], mv[0:ROWS, t, 0:1], rr[0:ROWS, 4 + j:5 + j],
                                    ALU.subtract, ALU.mult).then_inc(s_z, 1)
                for t in range(4 * half, 4 * half + 4):
                    j = t % 4
                    v.tensor_scalar(resid[0:ROWS, t, :], h0[0:ROWS, t, :], mv[0:ROWS, t, 0:1], rr[0:ROWS, j:j + 1],
                                    ALU.subtract, ALU.mult).then_inc(s_hn, 1)

            cos_v = rope_sb[:, 0:S].unsqueeze(1).broadcast_to([128, HB, S])
            sin_v = rope_sb[:, S:2 * S].unsqueeze(1).broadcast_to([128, HB, S])

            def rope_products(half, m):
                n = half * NM + m
                for u in range(2):
                    dve.wait_ge(s_up, 2 * n + u + 1)
                    if n >= 2:
                        dve.wait_ge(s_rot, 2 * (n - 2) + u + 1)
                    for j, (dst, table) in enumerate(((rope_a[n % 2], cos_v), (rope_b[n % 2], sin_v))):
                        v.tensor_tensor(dst[:, u, :].rearrange("p (b s) -> p b s", b=HB),
                                        bank[2 * u + j][:, 0:HN].rearrange("p (b s) -> p b s", b=HB), table,
                                        ALU.mult).then_inc(s_prod, 1)
                dve.wait_ge(s_prod, 4 * n + 4)
                v.tensor_tensor(k_bd[half][64:128, m, 1, :], rope_a[n % 2][64:128, 1, :],
                                rope_b[n % 2][64:128, 1, :], ALU.add).then_inc(s_rotd, 1)

            def shift(t):
                for g in range(2):
                    dve.wait_ge(s_sc, 2 * t + g + 1)
                    src = bank[4 + g][0:ROWS, 0:4 * 2 * S].rearrange("p (h k) -> p h k", k=S)
                    link(v.tensor_reduce(smax[0:ROWS, t % 2, 8 * g:8 * g + 8], src, AX.X, ALU.max))
                    if g == 0 and t >= 2:
                        dve.wait_ge(s_pt, 2 * (t - 2) + 2)
                    p = prob[0:ROWS, t % 2, 4 * g:4 * g + 4, :].rearrange("p m (i k) -> p (m i) k", i=2)[:, :, 0:S]
                    v.tensor_tensor(p, src, smax[0:ROWS, t % 2, 8 * g:8 * g + 8].unsqueeze(2).broadcast_to([ROWS, 8, S]),
                                    ALU.subtract).then_inc(s_sub, 1)

            def row_sums(t):
                dve.wait_ge(s_exp, t + 1)
                if t >= 2:
                    dve.wait_ge(s_pn, t - 1)
                p = prob[0:ROWS, t % 2, :, :].rearrange("p m (i k) -> p (m i) k", i=2)[:, :, 0:S]
                link(v.tensor_reduce(ssum[0:ROWS, t % 2, :], p, AX.X, ALU.add))
                v.reciprocal(ssum[0:ROWS, t % 2, :], ssum[0:ROWS, t % 2, :]).then_inc(s_rs, 1)

            def z_odd_out(half, b):
                if b == 0:
                    if half:
                        dve.wait_ge(s_oo, NM)
                    else:
                        dve.wait_ge(s_res, NT)
                dve.wait_ge(s_zz, half * B + 2 * b + 2)
                v.tensor_copy(ZT[:, 1, :, b * S:(b + 1) * S],
                              bank[1][:, 0:HN].rearrange("p (m s) -> p m s", m=NM)).then_inc(s_ze1, 1)

            def attn_out(half):
                dve.wait_ge(s_otm, NM * (half + 1))
                dve.wait_ge(s_gap, 2)
                if half:
                    dve.wait_ge(s_bk, 4)
                for c in range(2):
                    v.tensor_copy(aoT[:, c, :].rearrange("p (b s) -> p b s", b=HB)[:, :, 0:S],
                                  bank[2 + c][:, 0:HN].rearrange("p (b s) -> p b s", b=HB)).then_inc(s_ote, 1)

            def h1_and_stats(t):
                dve.wait_ge(s_bk, t + 1)
                dve.wait_ge(s_res, NT)
                v.tensor_tensor(resid[0:ROWS, t, :], bank[6 + t % 2][0:ROWS, 0:D], resid[0:ROWS, t, :],
                                ALU.add).then_inc(s_h1, 1)
                dve.wait_ge(s_h1, t + 1)
                link(v.bn_stats(bst[0:ROWS, :], resid[0:ROWS, t, :]))
                link(v.bn_aggr(mv[0:ROWS, t, :], bst[0:ROWS, :]))

            def norm3(half):
                c = lambda a: a[0:ROWS, 4 * half:4 * half + 4]
                link(v.tensor_scalar(c(nv), mv[0:ROWS, 4 * half:4 * half + 4, 1], LN_EPS, None, ALU.add))
                rsqrt(c(r1), c(nv), c(ny), c(na), c(nb))

            def hn2_out(t):
                if t == 0:
                    dve.wait_ge(s_pt, 2 * NT)
                v.tensor_scalar(hn2[0:ROWS, t, :], resid[0:ROWS, t, :], mv[0:ROWS, t, 0:1], r1[0:ROWS, t:t + 1],
                                ALU.subtract, ALU.mult).then_inc(s_hn2, 1)

            def router_shift(half):
                ex, mx = r_ex[:, 2 * half:2 * half + 2, :], rq[:, 2 * half:2 * half + 2]
                dve.wait_ge(s_lg, half + 1)
                dve.wait_ge(s_tab, 16)
                link(v.tensor_scalar(ex, bank[6][:, 2 * half * S:2 * (half + 1) * S].rearrange("p (q s) -> p q s", q=2),
                                     gbc[:, :], None, ALU.add))
                link(v.tensor_reduce(mx, ex, AX.X, ALU.max))
                v.tensor_tensor(ex, ex, mx.unsqueeze(2).broadcast_to([128, 2, S]), ALU.subtract).then_inc(s_rsub, 1)

            def router_pick(half):
                ex, sm = r_ex[:, 2 * half:2 * half + 2, :], rq[:, 2 * half:2 * half + 2]
                dve.wait_ge(s_rexp, half + 1)
                link(v.tensor_reduce(sm, ex, AX.X, ALU.add))
                link(v.reciprocal(sm, sm))
                link(v.tensor_tensor(ex, ex, sm.unsqueeze(2).broadcast_to([128, 2, S]), ALU.mult))
                for q in range(2 * half, 2 * half + 2):
                    link(v.max(top8[:, q, :], r_ex[:, q, :]))
                for q in range(2 * half, 2 * half + 2):
                    link(v.match_replace(r_keep[:, q, :], in_to_replace=top8[:, q, :], in_values=r_ex[:, q, :], imm_value=0.0))

            patch_scales(0, 4)
            quantise(0)
            ternary_weights()
            for t in range(1, 4):
                quantise(t)
            dve.wait_ge(s_base, 16)
            link(v.tensor_tensor(base[0:ROWS, :], base[0:ROWS, :], cls_sb[0:ROWS, :], ALU.add))
            for t in range(4):
                tokens(t)
            norms(0)
            patch_scales(4, 8)
            quantise(4)
            quantise(5)
            rope_products(0, 0)
            rope_products(0, 1)
            quantise(6)
            rope_products(0, 2)
            quantise(7)
            tokens(4)
            rope_products(0, 3)
            tokens(5)
            rope_products(0, 4)
            tokens(6)
            tokens(7)
            norms(1)
            rope_products(0, 5)
            rope_products(0, 6)
            rope_products(0, 7)
            for t in range(4):
                shift(t)
                rope_products(1, 2 * t)
                rope_products(1, 2 * t + 1)
                row_sums(t)
            shift(4)
            for b in range(3):
                z_odd_out(0, b)
            row_sums(4)
            shift(5)
            for b in range(3, 6):
                z_odd_out(0, b)
            row_sums(5)
            shift(6)
            z_odd_out(0, 6)
            z_odd_out(0, 7)
            row_sums(6)
            shift(7)
            row_sums(7)
            attn_out(0)
            for t in range(4):
                h1_and_stats(t)
            z_odd_out(1, 0)
            norm3(0)
            z_odd_out(1, 1)
            hn2_out(0)
            hn2_out(1)
            z_odd_out(1, 2)
            hn2_out(2)
            hn2_out(3)
            for b in range(3, HB):
                z_odd_out(1, b)
            router_shift(0)
            router_pick(0)
            attn_out(1)
            for t in range(4, NT):
                h1_and_stats(t)
            norm3(1)
            for t in range(4, NT):
                hn2_out(t)
            router_shift(1)
            router_pick(1)
            dve.wait_ge(s_pool1, 4)
            for i in range(2):
                v.tensor_tensor(pm_pad[:, :, 64 * i:64 * i + NPATCH], r_ex[:, :, 1:S], r_keep[:, :, 1:S], ALU.subtract)
                last = v.tensor_tensor(pm_pad[:, :, 64 * i + NPATCH:64 * i + S], r_ex[:, :, 0:1], r_keep[:, :, 0:1], ALU.subtract)
            last.then_inc(s_pm, 1)
            dve.wait_ge(s_mg, 1)
            v.tensor_copy(merged[:, 0:2, :].rearrange("p q n -> p (q n)"), bank[2][:, :]).then_inc(s_mge, 1)
            dve.wait_ge(s_mt, 1)
            dve.wait_ge(s_pool1, 2)
            v.tensor_copy(mT[:, 0, :, 0:B].rearrange("p e b -> p b e"),
                          bank[0][:, :].rearrange("p (b e) -> p b e", b=B)).then_inc(s_mte, 1)
            dve.wait_ge(s_mte, 2)
            dve.sem_inc(s_the, THE0)
            dve.sem_inc(s_oe, OE0)

            with dve.Fori(0, NG // 2) as it:
                for g in range(2):
                    dve.wait_ge(s_hid, 4 * it + 2 * g - 2 + HID0)
                    v.tensor_copy(stage[:, g, :, :, :], mT[:, :, bass.ds(it * SLOTS + GE * g, GE), :]).then_inc(s_stage, 1)
                    for k in range(2):
                        if k == 0:
                            dve.wait_ge(s_o, 2 * it + g + O0)
                        dve.wait_ge(s_th, 4 * it + 2 * g + k + 1)
                        v.tensor_copy(hT[:, 4 * k:4 * k + 4, :].rearrange("p k n -> p (k n)"),
                                      bank[2 + k][:, :]).then_inc(s_the, 1)
                    dve.wait_ge(s_ob[g], 16 * GE * it + MOVED0)
                    dve.wait_ge(s_o, 2 * it + g + 1 + O0)
                    v.tensor_copy(o_sb[:, g, :], bank[4][:, 0:D]).then_inc(s_oe, 1)

            for p in range(NT // 2):
                dve.wait_ge(s_fin, p + 1)
                r = resid[0:ROWS, 2 * p:2 * p + 2, :].rearrange("p t n -> p (t n)")
                v.tensor_tensor(r, bank[4 + p][0:ROWS, :], r, ALU.add).then_inc(s_fout, 1)


def move_out(act, gr, s_oe, o_all, o_sb, s_ob):
    g = gr % 2
    act.wait_ge(s_oe, gr + 1 + OE0)
    for j in range(GE):
        e = GE * gr + j
        act.dma_start(o_all[e:e + 1, :, :].rearrange("a b n -> a b n"), o_sb[32 * j:32 * j + B, g, :]).then_inc(s_ob[g], 16)


def rope_table():
    inv_freq = 1.0 / 10000.0 ** (np.arange(0, DH, 2, dtype=np.float32) / DH)
    freqs = np.outer(np.arange(S, dtype=np.float32), inv_freq)
    cos = np.concatenate([np.cos(freqs), np.cos(freqs)], -1)[:, ::2]
    sin = np.concatenate([np.sin(freqs), np.sin(freqs)], -1)[:, ::2]
    order = np.r_[1:S, 0]
    cos, sin = cos[order].T, sin[order].T
    return np.concatenate([np.tile(cos, (4, 1)), np.tile(np.concatenate([-sin, sin]), (2, 1))], 1).astype(np.float32)


def head_order():
    even, odd = np.arange(0, DH, 2), np.arange(1, DH, 2)
    one = np.concatenate([even, odd, even])
    return (np.arange(H)[:, None] * DH + one).ravel()


def kernel(**inputs):
    from concourse import bacc
    from concourse.bass_utils import run_bass_kernel_spmd

    a = {k: np.asarray(v) for k, v in inputs.items()}
    patches = a["x"].reshape(NT, 2, C, GRID, P, GRID, P).transpose(1, 3, 5, 0, 4, 6, 2).reshape(2, NPATCH, NT, DIN)
    x = np.zeros((XROWS, NT, DIN), patches.dtype)
    x[0:NPATCH], x[64:64 + NPATCH] = patches
    tokw = a["L0_tok_weight"].T.reshape(KC, 128, D).transpose(1, 0, 2).reshape(128, KC * D)
    posr = np.zeros((128, 2 * D), np.float32)
    posr[:, 0:D] = a["L0_tok_pos_embedding"].reshape(1, D)
    posr[[NPATCH, 64 + NPATCH], D:] = a["L0_tok_class_token"].reshape(D)
    wd = np.concatenate([a["L0_attn_w_down_q"], a["L0_attn_w_down_kv"]]).T.reshape(2, 128, 2 * DL).transpose(1, 0, 2)
    order = head_order()
    mask = np.zeros((128, 1), np.float32)
    mask[0:NPATCH] = mask[64:64 + NPATCH] = 1.0
    sel = np.zeros((GE, GE, 32), np.float32)
    sel[np.arange(GE), np.arange(GE), 0:B] = 1.0
    tables = np.concatenate([
        np.eye(128, dtype=np.float32), a["L0_ffn_gate_w"].T.reshape(2, 128, E).transpose(1, 0, 2).reshape(128, 2 * E),
        rope_table(), a["L0_attn_ln_scale"].reshape(2, 128).T, a["L0_attn_ln_bias"].reshape(2, 128).T,
        np.tile(a["L0_ffn_gate_b"], 4).reshape(128, 1), mask], 1)
    arrays = dict(
        x=x, tokw=tokw, tables=tables, posr=posr, wd=wd,
        wup=np.concatenate([a["L0_attn_w_up_q"][order].T, a["L0_attn_w_up_k"][order].T], 1),
        wvo=np.concatenate([a["L0_attn_w_up_v"].T,
                            a["L0_attn_w_out"].T.reshape(NM, 128, D).transpose(1, 0, 2).reshape(128, NM * D)], 1),
        w1=a["L0_ffn_w1"], w2=a["L0_ffn_w2"], sel=sel.reshape(GE, 128),
    )
    arrays = {k: np.ascontiguousarray(v) for k, v in arrays.items()}
    nc = bacc.Bacc("TRN2", target_bir_lowering=False, num_devices=1)
    args = {k: nc.dram_tensor(f"in_{k}", v.shape, mybir.dt.from_np(v.dtype), kind="ExternalInput").ap() for k, v in arrays.items()}
    out = nc.dram_tensor("out_0", (B, S, D), fp32, kind="ExternalOutput").ap()
    vit_tower(nc, out=out, **args)
    r = run_bass_kernel_spmd(nc, [{f"in_{k}": v for k, v in arrays.items()}], core_ids=[0])
    return r.results[0]["out_0"]
```

```python
from contextlib import ExitStack

import numpy as np
import concourse.bass as bass
from concourse import mybir

fp32 = mybir.dt.float32
bf16 = mybir.dt.bfloat16
int32 = mybir.dt.int32
ALU = mybir.AluOpType
ACT = mybir.ActivationFunctionType
AX = mybir.AxisListType

B, C, IMG, P = 16, 3, 96, 16
GRID = IMG // P
NPATCH = GRID * GRID
S = NPATCH + 1
D = 256
DIN = P * P * C
KC = DIN // 128
NT = B // 2
ROWS = 64 + S
QROWS = ROWS + 1
HB = B // 2
HN = HB * S
H, DH = 16, 64
NM = H // 2
DL = 128
E, HID, K = 32, 1024, 8
GE = 4
NG = E // GE
SLOTS = 2 * GE
W1N, W2N = 2 * HID, 8 * D
TABLES = 128 + 2 * E + 2 * S + 7
XROWS = 112
SELS = 384 + B
SCRATCH = 3
MAGIC = 12582912.0
SEED = 1597463007.0
LN_EPS = 1e-5
HID0, GELU0, THE0, O0, OE0, MOVED0 = 3, 2, 2, 1, 1, 16
FIRST = (32, 16)


def vit_tower(nc, x, tokw, tables, posr, wd, wup, wvo, w1, w2, sel, out):
    ctx = ExitStack()
    with ctx:
        def sb(name, shape, dt=fp32):
            return ctx.enter_context(nc.sbuf_tensor(name, shape, dt))

        def sem(name):
            return ctx.enter_context(nc.semaphore(name))

        def sems(name, n):
            return [sem(f"{name}{i}") for i in range(n)]

        w1_ring = sb("w1_ring", [128, SLOTS, W1N])
        w2_ring = sb("w2_ring", [128, SLOTS, W2N])
        scr1 = w1_ring[:, SCRATCH:SLOTS, :].rearrange("p a n -> p (a n)")
        scr2 = w2_ring[:, SCRATCH:SLOTS, :].rearrange("p a n -> p (a n)")
        r_av = sb("r_av", [128, 1024 + 2048])
        resid = sb("resid", [128, NT, D])
        ckv_dup = sb("ckv_dup", [128, B * ROWS])
        r_lo = sb("r_lo", [128, 2 * HB * 128])
        ckv_hi = sb("ckv_hi", [128, HB, 128])
        r_p = sb("r_p", [128, 2048])
        r_pt = sb("r_pt", [128, NM * HN])
        r_z = sb("r_z", [128, 2 * NM * HN])
        r_ot = sb("r_ot", [128, 2 * HN])
        ckv_lo = r_lo[:, 0:HB * 128].rearrange("p (a n) -> p a n", a=HB)
        r_ao = r_lo[:, HB * 128:2 * HB * 128].rearrange("p (c n) -> p c n", c=2)
        tab = sb("tab", [128, TABLES])
        ident = tab[:, 0:128]
        gwc = tab[:, 128:128 + 2 * E].rearrange("p (c e) -> p c e", c=2)
        rope_sb = tab[:, 192:192 + 2 * S]
        lnc = tab[:, 192 + 2 * S:196 + 2 * S]
        gbc = tab[:, 196 + 2 * S:197 + 2 * S]
        maskc = tab[:, 197 + 2 * S:198 + 2 * S]
        magicc = tab[:, 198 + 2 * S:199 + 2 * S]
        ident_b = sb("ident_b", [128, 128], bf16)
        small = sb("small", [128, 256])

        k_bd = [scr1[:, 4736 * h:4736 * (h + 1)].rearrange("p (m i n) -> p m i n", m=NM, i=2) for h in range(2)]
        x_sb = scr1[:, 4096:4096 + NT * DIN].rearrange("p (t n) -> p t n", t=NT)
        wuq_sb = scr2[:, 0:H * 96].rearrange("p (m i n) -> p m i n", m=NM, i=2)
        wuk_sb = scr2[:, 1536:1536 + H * 96].rearrange("p (m i n) -> p m i n", m=NM, i=2)
        q_rot = [scr2[:, 3072 + 2368 * h:3072 + 2368 * (h + 1)].rearrange("p (m n) -> p m n", m=NM) for h in range(2)]
        tokw_sb = scr2[:, 5440:5440 + KC * D]
        tokw_q = scr2[:, 6976:6976 + KC * D // 2].bitcast(bf16).rearrange("p (c n) -> p c n", c=KC)
        products = [scr2[:, 7808:7808 + 2 * HN], scr2[:, 8400:8400 + 2 * HN], scr2[:, 9584:9584 + 2 * HN], r_ot[:, :]]
        products = [a.rearrange("p (i n) -> p i n", i=2) for a in products]
        rope_a, rope_b = products[0:2], products[2:4]
        cq = scr2[:, 8992:8992 + B * S]
        wuv_sb = r_av[:, 0:H * DH]
        wo_sb = r_av[:, 1024:3072].rearrange("p (m n) -> p m n", m=NM)
        base = r_p[:, 0:D]
        cls_sb = r_p[:, D:2 * D]
        ones = r_p[:, 2 * D:2 * D + 128]
        junk = r_p[:, 1024:1024 + DIN]
        prob = r_p[:, :].rearrange("p (i m n) -> p i m n", i=2, m=NM)
        xq = r_pt[:, 0:DIN].bitcast(bf16).rearrange("p (i n) -> p i n", i=2)
        zT = r_pt[:, 768:768 + 2 * B * S].rearrange("p (c n) -> p c n", c=2)
        pT = r_pt[:, :].rearrange("p (m n) -> p m n", m=NM)
        h0 = r_z[:, 0:2048].rearrange("p (t n) -> p t n", t=NT)
        z = r_z[:, 2048:4096].rearrange("p (t n) -> p t n", t=NT)
        xqT = r_z[:, 4096:4096 + KC * QROWS].bitcast(bf16).rearrange("p (i c n) -> p i c n", i=2, c=KC)
        wjunk = r_z[:, 0:KC * D]
        ZT = r_z[:, :].rearrange("p (i m n) -> p i m n", i=2, m=NM)
        dup = ckv_dup[:, :].rearrange("p (b n) -> p b n", b=B)
        oT = r_ot[:, :].rearrange("p (i n) -> p i n", i=2)
        wd_sb = r_ao[:, :, 0:256]
        aoT = r_ao
        hn2 = r_p[:, :].rearrange("p (t n) -> p t n", t=NT)
        hn2T = ckv_dup[:, 0:2 * B * S].rearrange("p (c b s) -> p c b s", c=2, b=B)
        r_ex = ckv_dup[:, 1184:1184 + 4 * S].rearrange("p (q s) -> p q s", q=4)
        r_keep = ckv_dup[:, 1332:1332 + 4 * S].rearrange("p (q s) -> p q s", q=4)
        pm_pad = [a.rearrange("p (q n) -> p q n", q=2) for a in (r_pt[:, 2048:2304], r_ao[:, 0, 0:256])]
        pmT = [a.rearrange("p (q n) -> p q n", q=2) for a in (ckv_dup[:, 0:256], r_ao[:, 1, 0:256])]
        merged = r_lo[:, 0:HB * 128].rearrange("p (q n) -> p q n", q=4)
        mT = r_pt[:, 0:2048].rearrange("p (c e b) -> p c e b", c=2, e=E)
        hi_flat = ckv_hi[:, :, :].rearrange("p a n -> p (a n)")
        pm_e = hi_flat[:, 0:B * S].rearrange("p (b s) -> p b s", b=B)
        sel_sb = hi_flat[0:GE, B * S:B * S + 128]
        last_sel = [hi_flat[:, B * S + 128 * (k + 1):B * S + 128 * (k + 2)] for k in range(2)]
        image_mask = hi_flat[:, B * S + 384:B * S + SELS]
        pm_last = ckv_dup[:, 0:2 * B * S].rearrange("p (k b s) -> p k b s", k=2, b=B)
        bias1 = r_av[0:GE, 0:2 * HID].rearrange("p (g n) -> p g n", g=2)
        bias2 = r_av[0:GE, 2048:2048 + 2 * D].rearrange("p (g n) -> p g n", g=2)
        stage = r_av[:, 2560:3072].rearrange("p (g c e b) -> p g c e b", g=2, c=2, e=GE)
        hg = r_p[:, 0:HID]
        hT = r_p[:, 1024:2048].rearrange("p (k n) -> p k n", k=8)
        o_sb = r_ot[:, 0:2 * D].rearrange("p (g n) -> p g n", g=2)
        o_all = r_lo[:, :].rearrange("p (b n) -> p b n", b=HB)
        ahead = r_z[:, 0:GE * HID].rearrange("p (e n) -> p e n", e=GE)

        at = [0]

        def few(n):
            at[0] += n
            assert at[0] <= 256
            return small[:, at[0] - n:at[0]]

        wsum, wmean, wscale, wdq = few(1), few(1), few(1), few(1)
        ssq, amax, xr_s, xscale, dq = few(NT), few(NT), few(NT), few(NT), few(NT)
        nv, ny, na, nb = few(NT), few(NT), few(NT), few(NT)
        r1, rr = few(NT), few(NT)
        fac = few(8).rearrange("p (k t) -> p k t", k=2)
        nvv = nv.rearrange("p (k t) -> p k t", k=2)
        mv = few(2 * NT).rearrange("p (t k) -> p t k", k=2)
        bst = few(24).rearrange("p (t n) -> p t n", t=4)
        smax = few(2 * H).rearrange("p (i h) -> p i h", i=2)
        ssum = few(2 * H).rearrange("p (i h) -> p i h", i=2)
        top8 = few(32).rearrange("p (q k) -> p q k", q=4)
        rq = few(4)

        bank = [ctx.enter_context(nc.psum_tensor(f"bank{i}", [128, 512], fp32)) for i in range(8)]

        s_x = sems("x_in", NT // 2)
        s_tokw, s_base, s_wd, s_tab, s_wup, s_av, s_sel = (
            sem(n) for n in ("tokw_in", "base_in", "wd_in", "tables_in", "wup_in", "av_in", "sel_in"))
        s_w1 = [sems(f"w1_in{g}_", 2) for g in range(2)]
        s_w2 = [sems(f"w2_in{g}_", 2) for g in range(2)]
        s_b1 = sems("b1_in", 2)
        s_b2 = sems("b2_in", 2)
        s_bank = sem("banks_zeroed")
        s_pool0 = sem("pool_constants")
        s_dve = sem("dve_chain")
        s_wabs, s_wsum, s_wm, s_wq = (sem(n) for n in ("w_abs", "w_sum", "w_mean", "w_ternary"))
        s_ssq, s_xq, s_xt, s_xte, s_proj, s_h0, s_hn, s_z, s_res = (sem(n) for n in (
            "sum_sq", "x_rounded", "x_turned", "x_turned_out", "projected", "h0_ready",
            "hn_ready", "z_ready", "resid_ready"))
        s_zt, s_zte, s_c, s_ce, s_ct, s_cte = (sem(n) for n in (
            "z_turned", "z_turned_out", "latents", "latents_out", "ckv_turned", "ckv_turned_out"))
        s_up, s_prod, s_rot, s_rotd, s_kbz = (sem(n) for n in (
            "up_done", "rope_products", "rotated", "rotated_second", "k_bd_zeroed"))
        s_sc, s_sub, s_exp, s_rs, s_pn, s_pt, s_pte = (sem(n) for n in (
            "scores", "shifted", "exps", "row_sums", "probs", "probs_turned", "probs_turned_out"))
        s_gap = sem("gaps_zeroed")
        s_zz, s_ze0, s_ze1, s_oo, s_ooe, s_ote, s_bk, s_h1 = (sem(n) for n in (
            "z_done", "z_out_even", "z_out_odd", "heads_done", "heads_out", "attn_out",
            "attn_turned", "h1_ready"))
        s_hn2, s_ht, s_hte, s_lg, s_rsub, s_rexp, s_pm, s_pmt, s_pmte, s_mg, s_mge, s_mt, s_mte, s_pme = (
            sem(n) for n in (
                "hn2_ready", "hn2_turned", "hn2_turned_out", "logits", "logits_shifted", "router_exps",
                "pm_ready", "pm_turned", "pm_turned_out", "merged_done", "merged_out", "merged_turned",
                "merged_turned_out", "pm_e_in"))
        s_pool1 = sem("expert_zeros")
        s_w1a, s_w2a, s_rep, s_pml = (sem(n) for n in (
            "w1_half_used", "w2_half_used", "pm_repeated", "pm_last_ready"))
        s_stage, s_hid, s_gelu, s_th, s_the, s_o, s_oe, s_fin, s_fout, s_out = (sem(n) for n in (
            "staged", "hidden", "gelus", "hidden_turned", "hidden_turned_out", "expert_out",
            "expert_out_kept", "scattered", "result", "stored"))
        s_ob = sems("expert_out_moved", 2)
        s_idb = sem("ident_b_ready")
        s_ahead = sem("w1_ahead_in")
        s_rz = sem("resid_rows_zeroed")
        s_tok = sem("tokens_out")
        s_wr, s_xr, s_xs, s_xm = (sem(n) for n in ("w_rounded", "rms_ready", "x_scaled", "x_shifted"))
        s_nm = sem("norm_factors")
        s_otm = sem("attn_sums")

        def turned_out(copy, half, c):
            src = bank[4 + c][:, :].rearrange("p (b s) -> p b s", b=HB)
            dst = hn2T[:, c, HB * half:HB * (half + 1), :]
            more = (ACT.Copy,) if c == 0 else ()
            copy(dst[:, :, 1:S], src[:, :, 0:NPATCH], *more).then_inc(s_hte, 1)
            copy(dst[:, :, 0:1], src[:, :, NPATCH:S], *more).then_inc(s_hte, 1)

        BACK = (6, 7, 6, 7, 6, 7, 4, 5)

        def rotated(n):
            late = max(n + 1 - NM, 0)
            return 3 * min(n + 1, NM) + 5 * (late // 2) + 3 * (late % 2)

        def rotated_q(n):
            return rotated(n - 1) + 1

        block = ctx.enter_context(nc.Block())

        @block.sync
        def _(sp):
            def load_x(p):
                sp.dma_start(x_sb[0:XROWS, 2 * p:2 * p + 2, :], x[:, 2 * p:2 * p + 2, :]).then_inc(s_x[p], 16)

            load_x(0)
            load_x(1)
            sp.dma_start(tokw_sb, tokw).then_inc(s_tokw, 16)
            sp.dma_start(tab[:, :], tables).then_inc(s_tab, 16)
            sp.dma_start(r_p[:, 0:2 * D], posr).then_inc(s_base, 16)
            sp.dma_start(wd_sb, wd).then_inc(s_wd, 16)
            sp.dma_start(scr2[:, 0:3072], wup).then_inc(s_wup, 16)
            load_x(2)
            load_x(3)
            sp.dma_start(r_av[:, :], wvo).then_inc(s_av, 16)

            def load_w1(e, g, c, lo=0, hi=GE):
                sp.dma_start(w1_ring[:, GE * g + lo:GE * g + hi, c * HID:(c + 1) * HID],
                             w1[bass.ds(e + lo, hi - lo), 0:D, :].rearrange("e (p c) h -> c p e h", c=2)[c]
                             ).then_inc(s_w1[g][c], 16)

            def load_w2(e, g, kk, lo=0, hi=GE):
                sp.dma_start(w2_ring[:, GE * g + lo:GE * g + hi, kk * 4 * D:(kk + 1) * 4 * D],
                             w2[bass.ds(e + lo, hi - lo), 0:HID, :].rearrange("e (p k) d -> p e (k d)", k=8)[:, :, kk * 4 * D:(kk + 1) * 4 * D]
                             ).then_inc(s_w2[g][kk], 16)

            def load_b1(e, g):
                sp.dma_start(bias1[:, g, :], w1[bass.ds(e, GE), D:D + 1, :].rearrange("e a h -> e (a h)")).then_inc(s_b1[g], 16)

            def load_b2(e, g):
                sp.dma_start(bias2[:, g, :], w2[bass.ds(e, GE), HID:HID + 1, :].rearrange("e a h -> e (a h)")).then_inc(s_b2[g], 16)

            for load in (load_w1, load_w2):
                for c in range(2):
                    load(0, 0, c, 0, SCRATCH)
            sp.wait_ge(s_sc, 2 * NT)
            for load in (load_w1, load_w2):
                for c in range(2):
                    load(0, 0, c, SCRATCH, GE)
                for c in range(2):
                    load(GE, 1, c)
            sp.wait_ge(s_zz, 2 * B)
            sp.dma_start(hi_flat[:, B * S:B * S + SELS], sel).then_inc(s_sel, 16)
            sp.wait_ge(s_otm, 2 * NM)
            for g in range(2):
                load_b1(GE * g, g)
                load_b2(GE * g, g)
            sp.wait_ge(s_oo, 2 * NM)
            sp.dma_start(ahead, w1[SLOTS:SLOTS + GE, 0:D, :].rearrange("e (p c) h -> c p e h", c=2)[0]).then_inc(s_ahead, 16)

            def refill(it, g, paced=False, last=False):
                e = it * SLOTS + GE * g
                sp.wait_ge(s_hid, 4 * it + 2 * g - 2 + HID0)
                if paced:
                    sp.wait_ge(s_w2[1 - g][1], 16 * (it - 1 + g) + FIRST[1 - g])
                load_w1(e, g, 1)
                sp.wait_ge(s_w2a, 2 * it + g - 1)
                if paced:
                    sp.wait_ge(s_w1[g][0], 16 * it + FIRST[g])
                load_b2(e, g)
                load_w2(e, g, 0)
                sp.wait_ge(s_o, 2 * it + g - 1 + O0)
                if paced:
                    sp.wait_ge(s_w1[g][1], 16 * it + FIRST[g])
                load_w2(e, g, 1)
                if last:
                    return
                sp.wait_ge(s_w1a, 2 * it + g)
                if paced:
                    sp.wait_ge(s_w2[g][0], 16 * it + FIRST[g])
                load_b1(e + GE, 1 - g)
                load_w1(e + GE, 1 - g, 0)

            sp.wait_ge(s_w1a, 1)
            load_b1(SLOTS, 0)
            with sp.Fori(1, NG // 2 - 1) as it:
                for g in range(2):
                    refill(it, g)
            for g in range(2):
                refill(NG // 2 - 1, g, paced=True, last=(g == 1))
            for p in range(NT // 2):
                sp.wait_ge(s_fout, p + 1)
                sp.dma_start(out[:, 2 * p:2 * p + 2, :], resid[0:XROWS, 2 * p:2 * p + 2, :]).then_inc(s_out, 16)
            sp.wait_ge(s_out, 16 * (NT // 2))

        @block.gpsimd
        def _(pool):
            pool.memset(resid[96:XROWS, :, :], 0.0).then_inc(s_rz, 1)
            pool.wait_ge(s_rz, 1)
            pool.memset(ones, 1.0).then_inc(s_pool0, 1)
            pool.memset(ckv_dup[:, :], 0.0).then_inc(s_pool0, 1)
            pool.memset(ckv_lo[:, :, :], 0.0).then_inc(s_pool0, 1)
            pool.memset(ckv_hi[:, :, :], 0.0).then_inc(s_pool0, 1)
            def zero_k(half):
                pool.wait_ge(s_xq, NT if half else 1)
                pool.memset(k_bd[half][0:64, :, 1, :], 0.0).then_inc(s_kbz, 1)
                pool.wait_ge(s_kbz, 2 * half + 1)
                pool.memset(k_bd[half][64:128, :, 0, :], 0.0).then_inc(s_kbz, 1)
                pool.wait_ge(s_kbz, 2 * half + 2)

            def residual(t):
                pool.wait_ge(s_hn, t + 1)
                pool.tensor_tensor(resid[0:ROWS, t, :], h0[0:ROWS, t, :], resid[0:ROWS, t, :], ALU.add).then_inc(s_res, 1)

            def rotate(half, m):
                n = half * NM + m
                if n == NM:
                    pool.wait_ge(s_proj, NT)
                if n:
                    pool.wait_ge(s_rot, rotated(n - 1))
                pool.wait_ge(s_prod, 4 * n + 2)
                pool.tensor_tensor(q_rot[half][:, m, :], rope_a[n % 2][:, 0, :], rope_b[n % 2][:, 0, :], ALU.add).then_inc(s_rot, 1)
                pool.wait_ge(s_prod, 4 * n + 4)
                for i in range(2 - half * (m % 2)):
                    if i:
                        pool.wait_ge(s_rot, rotated(n) - 1)
                    p = slice(64 * i, 64 * i + 64)
                    pool.tensor_tensor(k_bd[half][p, m, i, :], rope_a[n % 2][p, 1, :], rope_b[n % 2][p, 1, :],
                                       ALU.add).then_inc(s_rot, 1)
                if half == 0 and m in (4, 6, 7):
                    pool.wait_ge(s_rot, rotated(n))

            def normalise(t):
                pool.wait_ge(s_rs, t + 1)
                p = prob[0:ROWS, t % 2, :, :].rearrange("p m (i k) -> p (m i) k", i=2)[:, :, 0:S]
                pool.tensor_tensor(p, p, ssum[0:ROWS, t % 2, :].unsqueeze(2).broadcast_to([ROWS, H, S]),
                                   ALU.mult).then_inc(s_pn, 1)
                pool.wait_ge(s_pn, t + 1)

            zero_k(0)
            for t in range(4):
                residual(t)
            for m in range(NM):
                rotate(0, m)
                if m == 4:
                    zero_k(1)
                if m == 6:
                    pool.wait_ge(s_h0, NT)
                    pool.wait_ge(s_wm, 1)
                    pool.memset(prob[:, :, :, 37:64], 0.0).then_inc(s_gap, 1)
            rotate(1, 0)
            for t in range(4):
                rotate(1, 2 * t + 1)
                normalise(t)
                residual(4 + t)
                if t < 3:
                    rotate(1, 2 * t + 2)
            pool.wait_ge(s_c, 4)
            pool.memset(aoT[:, :, :], 0.0).then_inc(s_gap, 1)
            for t in range(4, NT):
                normalise(t)
            pool.wait_ge(s_zz, 2 * B)
            pool.memset(hi_flat[:, 0:B * S], 0.0).then_inc(s_pool1, 1)
            pool.memset(r_pt[:, 0:2304], 0.0).then_inc(s_pool1, 1)
            pool.wait_ge(s_bk, NT)
            pool.memset(pm_pad[1], 0.0).then_inc(s_pool1, 1)
            pool.wait_ge(s_mt, 2)
            pool.wait_ge(s_pme, 128)
            pool.memset(r_lo[:, :], 0.0).then_inc(s_pool1, 1)
            pool.wait_ge(s_ahead, 16)
            pool.wait_ge(s_w1a, 1)
            for j in range(GE):
                pool.tensor_copy(w1_ring[:, j, 0:HID], ahead[:, j, :]).then_inc(s_w1[0][0], 16 // GE)

        @block.scalar
        def _(act):
            def square_sum(t):
                act.wait_ge(s_x[t // 2], 16)
                if t >= 1:
                    act.wait_ge(s_ssq, t)
                act.activation(junk[0:QROWS, :], x_sb[0:QROWS, t, :], ACT.Square,
                               accum_out=ssq[0:QROWS, t:t + 1]).then_inc(s_ssq, 1)

            def xq_out(t):
                act.wait_ge(s_xt, t + 1)
                if t >= 2:
                    act.wait_ge(s_proj, t - 1)
                act.activation(xqT[:, t % 2, :, :].rearrange("p c n -> p (c n)"),
                               bank[4 + t % 2][:, :].bitcast(bf16)[:, 0:KC * QROWS], ACT.Copy).then_inc(s_xte, 1)

            def scale_x(t):
                act.wait_ge(s_xr, 1 + t // 4)
                act.activation(x_sb[0:QROWS, t, :], x_sb[0:QROWS, t, :], ACT.Copy, scale=xr_s[0:QROWS, t:t + 1]).then_inc(s_xs, 1)

            def round_x(t):
                act.wait_ge(s_xm, t - 2)
                act.wait_ge(s_xt, t - 1)
                act.activation(xq[0:QROWS, t % 2, :], x_sb[0:QROWS, t, :], ACT.Identity,
                               bias=magicc[0:QROWS, :]).then_inc(s_xq, 1)

            act.sem_inc(s_gelu, GELU0)
            for g in range(2):
                act.sem_inc(s_ob[g], MOVED0)
            for t in range(4):
                square_sum(t)
            act.wait_ge(s_tokw, 16)
            act.activation(wjunk, tokw_sb, ACT.Abs, accum_out=wsum).then_inc(s_wabs, 1)
            scale_x(3)
            act.wait_ge(s_tab, 16)
            act.wait_ge(s_wr, 1)
            act.activation(tokw_q.rearrange("p c n -> p (c n)"), tokw_sb, ACT.Identity, bias=magicc).then_inc(s_wq, 1)
            xq_out(0)
            xq_out(1)
            round_x(3)
            xq_out(2)
            xq_out(3)
            for t in range(4, NT):
                square_sum(t)

            def z_out(half):
                act.wait_ge(s_zt, 4 * half + 4)
                act.wait_ge(s_tab, 16)
                for c in range(2):
                    act.activation(zT[:, c, half * HN:(half + 1) * HN].rearrange("p (i s) -> p i s", i=HB),
                                   bank[4 + c][:, :].rearrange("p (i s) -> p i s", i=HB)[:, :, 0:S],
                                   ACT.Identity, bias=lnc[:, 2 + c:3 + c], scale=lnc[:, c:c + 1]).then_inc(s_zte, 1)

            def latents_out(half):
                act.wait_ge(s_c, 2 * half + 1)
                act.activation(cq[:, half * HN:(half + 1) * HN], bank[6][:, 0:HN], ACT.Copy).then_inc(s_ce, 1)
                act.wait_ge(s_c, 2 * half + 2)
                act.wait_ge(s_pool0, 2)
                for i in range(2):
                    act.activation(dup[:, half * HB:(half + 1) * HB, 64 * i:64 * i + S],
                                   bank[7][:, 0:HN].rearrange("p (b s) -> p b s", b=HB),
                                   ACT.Copy).then_inc(s_ce, 1)

            def ckv_out(half):
                act.wait_ge(s_pool0, 4)
                if half:
                    act.wait_ge(s_zz, B)
                for g in range(2):
                    act.wait_ge(s_ct, 2 * half + g + 1)
                    src = bank[4 + g][:, :].rearrange("p (b n) -> p b n", b=4)
                    act.activation(ckv_lo[0:S, 4 * g:4 * g + 4, :], src[0:S, :, :], ACT.Copy).then_inc(s_cte, 1)
                    act.activation(ckv_hi[64:64 + S, 4 * g:4 * g + 4, :], src[64:64 + S, :, :], ACT.Copy).then_inc(s_cte, 1)

            def exps(t):
                act.wait_ge(s_sub, 2 * t + 2)
                p = prob[0:ROWS, t % 2, :, :].rearrange("p m (i k) -> p (m i) k", i=2)[:, :, 0:S]
                act.activation(p, p, ACT.Exp, scale=DH ** -0.5).then_inc(s_exp, 1)

            def probs_out(t):
                if t == 0:
                    act.wait_ge(s_ce, 6)
                if t >= 4:
                    act.wait_ge(s_zz, 4 * (t - 4) + 4)
                for g in range(2):
                    act.wait_ge(s_pt, 2 * t + g + 1)
                    act.activation(
                        pT[0:ROWS, 4 * g:4 * g + 4, 2 * (t % 4) * S:2 * (t % 4) * S + 2 * S].rearrange("p m (i q) -> p m i q", i=2),
                        bank[6 + g][0:ROWS, :].rearrange("p (m i q) -> p m i q", m=4, i=2)[:, :, :, 0:S],
                        ACT.Copy).then_inc(s_pte, 1)

            def z_even_out(half, b):
                if b == 0:
                    if half:
                        act.wait_ge(s_oo, NM)
                    else:
                        act.wait_ge(s_res, NT)
                act.wait_ge(s_zz, half * B + 2 * b + 1)
                act.activation(ZT[:, 0, :, b * S:(b + 1) * S],
                               bank[2 * (b % 2)][:, 0:HN].rearrange("p (m s) -> p m s", m=NM), ACT.Copy).then_inc(s_ze0, 1)

            def heads_out(half, m):
                n = half * NM + m
                act.wait_ge(s_oo, n + 1)
                if n >= 2:
                    act.wait_ge(s_otm, n - 1)
                act.activation(oT[:, m % 2, :], bank[m % 2][:, 0:HN], ACT.Copy).then_inc(s_ooe, 1)

            def attn_out(half):
                act.wait_ge(s_otm, NM * (half + 1))
                act.wait_ge(s_gap, 2)
                if half:
                    act.wait_ge(s_bk, 4)
                act.activation(aoT[:, 1, :].rearrange("p (b s) -> p b s", b=HB)[:, :, 0:S],
                               bank[3][:, 0:HN].rearrange("p (b s) -> p b s", b=HB), ACT.Copy).then_inc(s_ote, 1)

            def hn2_turned_out(half):
                act.wait_ge(s_ct, 4)
                act.wait_ge(s_ht, 4 * half + 4)
                turned_out(act.activation, half, 0)

            def router_exps(half):
                act.wait_ge(s_rsub, half + 1)
                ex = r_ex[:, 2 * half:2 * half + 2, :]
                act.activation(ex, ex, ACT.Exp).then_inc(s_rexp, 1)

            def norm_out(half):
                act.wait_ge(s_nm, 2 * half + 2)
                act.wait_ge(s_rz, 1)
                for t in range(4 * half, 4 * half + 4):
                    j = t % 4
                    act.activation(resid[0:ROWS, t, :], h0[0:ROWS, t, :], ACT.Identity, bias=fac[0:ROWS, 1, j:j + 1],
                                   scale=fac[0:ROWS, 0, j:j + 1]).then_inc(s_hn, 1)

            z_out(0)
            norm_out(0)
            latents_out(0)
            scale_x(4)
            scale_x(5)
            round_x(4)
            xq_out(4)
            round_x(5)
            xq_out(5)
            scale_x(6)
            scale_x(7)
            round_x(6)
            xq_out(6)
            round_x(7)
            xq_out(7)
            ckv_out(0)
            z_out(1)
            latents_out(1)
            norm_out(1)
            exps(0)
            exps(1)
            probs_out(0)
            exps(2)
            probs_out(1)
            exps(3)
            probs_out(2)
            probs_out(3)
            z_even_out(0, 0)
            exps(4)
            z_even_out(0, 1)
            z_even_out(0, 2)
            exps(5)
            for b in range(3, 6):
                z_even_out(0, b)
            probs_out(4)
            exps(6)
            z_even_out(0, 6)
            z_even_out(0, 7)
            probs_out(5)
            exps(7)
            heads_out(0, 0)
            heads_out(0, 1)
            probs_out(6)
            for m in range(2, 5):
                heads_out(0, m)
            probs_out(7)
            ckv_out(1)
            for m in range(5, NM):
                heads_out(0, m)
            attn_out(0)
            for b in range(HB):
                z_even_out(1, b)
            hn2_turned_out(0)
            def pm_turned_out(half):
                act.wait_ge(s_pmt, half + 1)
                act.activation(pmT[half][0:ROWS, :, :].rearrange("p q n -> p (q n)"), bank[(4, 7)[half]][0:ROWS, 0:256],
                               ACT.Copy).then_inc(s_pmte, 1)

            def pm_by_expert(half):
                act.wait_ge(s_pool1, 1)
                act.wait_ge(s_pm, half + 1)
                for i in range(4):
                    act.dma_start(pm_e[64 * half:64 * half + E, HB * half:HB * (half + 1), :].rearrange("p (q i) s -> p i q s", i=4)[:, i, :, :],
                                  pm_pad[half][32 * i:32 * i + 32, :, 0:S]).then_inc(s_pme, 16)

            def merged_out(half):
                act.wait_ge(s_mg, half + 1)
                act.activation(merged[:, 2 * half, :], bank[(4, 2)[half]][:, 0:D], ACT.Copy).then_inc(s_mge, 1)

            def merged_turned_out(half):
                act.wait_ge(s_mt, half + 1)
                act.wait_ge(s_pool1, 2)
                act.activation(mT[:, 1, :, HB * half:HB * (half + 1)].rearrange("p e b -> p b e"),
                               bank[5][:, 0:256].rearrange("p (b e) -> p b e", b=HB), ACT.Copy).then_inc(s_mte, 1)

            heads_out(1, 0)
            heads_out(1, 1)
            router_exps(0)
            heads_out(1, 2)
            heads_out(1, 3)
            pm_turned_out(0)
            pm_by_expert(0)
            heads_out(1, 4)
            merged_out(0)
            heads_out(1, 5)
            heads_out(1, 6)
            merged_turned_out(0)
            heads_out(1, 7)
            attn_out(1)
            hn2_turned_out(1)
            router_exps(1)
            pm_turned_out(1)
            pm_by_expert(1)
            merged_out(1)
            merged_turned_out(1)
            act.wait_ge(s_mte, 4)
            act.wait_ge(s_pool1, 4)
            for gr in range(NG):
                if 1 <= gr <= NG - 2:
                    move_out(act, gr - 1, s_oe, o_all, o_sb, s_ob)
                for n in range(2):
                    act.wait_ge(s_hid, 2 * gr + n + 1 + HID0)
                    if gr >= 1 and n == 0:
                        act.wait_ge(s_th, 2 * gr)
                    act.activation(hg[:, n * 512:(n + 1) * 512], bank[n][:, :], ACT.Gelu).then_inc(s_gelu, 1)

        @block.tensor
        def _(pe):
            mm, tr = nc.tensor.matmul, nc.tensor.transpose
            pe.sem_inc(s_hid, HID0)
            pe.sem_inc(s_o, O0)
            pe.wait_ge(s_bank, 4)
            pe.wait_ge(s_pool0, 1)
            pe.wait_ge(s_wabs, 1)
            mm(bank[0][:, 0:1], ones, wsum, start=True, stop=True).then_inc(s_wsum, 1)

            def keep_warm(n, b):
                for _ in range(n):
                    mm(bank[b][:, 0:128], ident[:, :], ident[:, :], start=True, stop=True)

            def turn_x(t):
                pe.wait_ge(s_xq, t + 1)
                if t == 0:
                    pe.wait_ge(s_idb, 1)
                if t in (2, 3, 5, 6, 7):
                    pe.wait_ge(s_xte, t - 1)
                if t == 4:
                    pe.wait_ge(s_zte, 2)
                for c in range(KC):
                    last = tr(bank[4 + t % 2][:, :].bitcast(bf16)[:, c * QROWS:(c + 1) * QROWS],
                              xq[0:QROWS, t % 2, c * 128:(c + 1) * 128], ident_b[0:QROWS, 0:QROWS])
                last.then_inc(s_xt, 1)

            def project(t):
                pe.wait_ge(s_xte, t + 1)
                if t == 0:
                    pe.wait_ge(s_wq, 1)
                if t == 4:
                    pe.wait_ge(s_ce, 3)
                if t >= 2:
                    pe.wait_ge(s_tok, t - 1)
                for c in range(KC):
                    last = mm(bank[6 + t % 2][0:ROWS, 0:D], xqT[:, t % 2, c, 0:ROWS], tokw_q[:, c, :],
                              start=(c == 0), stop=(c == KC - 1))
                last.then_inc(s_proj, 1)

            def turn_z(t):
                pe.wait_ge(s_z, t + 1)
                if t == 0:
                    pe.wait_ge(s_tab, 16)
                if t == 0:
                    pe.wait_ge(s_xte, 4)
                if t == 4:
                    pe.wait_ge(s_cte, 4)
                for c in range(2):
                    last = tr(bank[4 + c][:, (t % 4) * 128:(t % 4) * 128 + ROWS], z[0:ROWS, t, c * 128:(c + 1) * 128],
                              ident[0:ROWS, 0:ROWS])
                last.then_inc(s_zt, 1)

            def latents(half):
                if half == 0:
                    pe.wait_ge(s_wd, 16)
                pe.wait_ge(s_h0, 4 * half + 4)
                pe.wait_ge(s_zte, 2 * (half + 1))
                for u in range(2):
                    for c in range(2):
                        last = mm(bank[6 + u][:, 0:HN], wd_sb[:, c, u * DL:(u + 1) * DL],
                                  zT[:, c, half * HN:(half + 1) * HN], start=(c == 0), stop=(c == 1))
                    last.then_inc(s_c, 1)

            def turn_ckv(half):
                pe.wait_ge(s_ce, 3 * half + 3)
                if half:
                    pe.wait_ge(s_sub, 2 * NT)
                else:
                    pe.wait_ge(s_xte, NT)
                for g in range(2):
                    for b in range(4):
                        last = tr(bank[4 + g][0:ROWS, b * 128:(b + 1) * 128], dup[:, half * HB + 4 * g + b, :], ident[:, :])
                    last.then_inc(s_ct, 1)

            def up(half, m):
                for u, w in enumerate((wuq_sb, wuk_sb)):
                    n = (half * NM + m) * 2 + u
                    if n == 0:
                        pe.wait_ge(s_wup, 16)
                        pe.wait_ge(s_wm, 1)
                    if m == 0 and u == 0:
                        pe.wait_ge(s_ce, 3 * (half + 1))
                    if n >= 2:
                        pe.wait_ge(s_prod, 2 * (n - 2) + 2)
                    rhs = cq[:, half * HN:(half + 1) * HN] if u == 0 else dup[:, half * HB:(half + 1) * HB, 0:S]
                    for j in range(2):
                        for i in range(2):
                            last = mm(bank[2 * u + j][64 * i:64 * i + 64, 0:HN], w[:, m, i, 32 * j:32 * j + 64], rhs,
                                      start=True, stop=True)
                    last.then_inc(s_up, 1)

            def scores(t):
                half = t // 4
                pe.wait_ge(s_rot, rotated((half + 1) * NM - 1))
                if half:
                    pe.wait_ge(s_rotd, NM // 2)
                pe.wait_ge(s_kbz, 2 * half + 2)
                if t == 0:
                    pe.wait_ge(s_zte, 4)
                if t >= 1:
                    pe.wait_ge(s_sub, 2 * t)
                for g in range(2):
                    for mq in range(4):
                        for i in range(2):
                            b = 2 * (t % 4) + i
                            m = 4 * g + mq
                            last = mm(bank[4 + g][64 * i:64 * i + S, mq * 2 * S:(mq + 1) * 2 * S],
                                      q_rot[half][:, m, b * S:(b + 1) * S], k_bd[half][:, m, :, b * S:(b + 1) * S],
                                      start=True, stop=True)
                    last.then_inc(s_sc, 1)

            def turn_probs(t):
                pe.wait_ge(s_pn, t + 1)
                if t == 0:
                    pe.wait_ge(s_gap, 1)
                    pe.wait_ge(s_ce, 6)
                if t >= 1:
                    pe.wait_ge(s_pte, 2 * t)
                for g in range(2):
                    for mq in range(4):
                        last = tr(bank[6 + g][0:ROWS, mq * 128:mq * 128 + ROWS],
                                  prob[0:ROWS, t % 2, 4 * g + mq, 0:ROWS], ident[0:ROWS, 0:ROWS])
                    last.then_inc(s_pt, 1)

            def values(half, b):
                if b == 0:
                    pe.wait_ge(s_pte, 8 * (half + 1))
                    pe.wait_ge(s_cte, 4 * (half + 1))
                    if half == 0:
                        pe.wait_ge(s_prod, 8 * NM)
                    else:
                        pe.wait_ge(s_ooe, NM)
                if b == 1 and half:
                    pe.wait_ge(s_ote, 2)
                for par, ck in enumerate((ckv_lo, ckv_hi)):
                    if b >= 2:
                        pe.wait_ge((s_ze0, s_ze1)[par], half * HB + b - 1)
                    mm(bank[par + 2 * (b % 2)][:, 0:HN], ck[0:ROWS, b, :], pT[0:ROWS, :, b * S:(b + 1) * S],
                       start=True, stop=True).then_inc(s_zz, 1)

            def combine(half, m):
                pe.wait_ge(s_ooe, half * NM + m + 1)
                if m == 0 and half:
                    pe.wait_ge(s_ote, 2)
                for c in range(2):
                    last = mm(bank[2 + c][:, 0:HN], wo_sb[:, m, c * 128:(c + 1) * 128], oT[:, m % 2, :],
                              start=(m == 0), stop=(m == NM - 1))
                last.then_inc(s_otm, 1)

            def heads(half, m):
                n = half * NM + m
                if m == 0:
                    pe.wait_ge(s_ze0, HB * (half + 1))
                    pe.wait_ge(s_ze1, HB * (half + 1))
                    pe.wait_ge(s_av, 16)
                if m >= 2:
                    pe.wait_ge(s_ooe, n - 1)
                for par in range(2):
                    h = 2 * m + par
                    last = mm(bank[m % 2][64 * par:64 * par + 64, 0:HN], wuv_sb[:, h * DH:(h + 1) * DH],
                              ZT[:, par, m, :], start=True, stop=True)
                last.then_inc(s_oo, 1)
                if m >= 1:
                    combine(half, m - 1)
                if m == NM - 1:
                    combine(half, m)

            def turn_back(t):
                if t % 4 == 0:
                    pe.wait_ge(s_ote, 2 * (t // 4) + 2)
                    if t == 0:
                        pe.wait_ge(s_pte, 16)
                    else:
                        pe.wait_ge(s_rsub, 1)
                if t in (2, 3):
                    pe.wait_ge(s_h1, t - 1)
                if t == 6:
                    pe.wait_ge(s_mte, 2)
                for c in range(2):
                    last = tr(bank[BACK[t]][0:ROWS, c * 128:(c + 1) * 128], aoT[:, c, (t % 4) * 128:(t % 4) * 128 + ROWS],
                              ident[:, :])
                last.then_inc(s_bk, 1)

            def turn_hn2(t):
                pe.wait_ge(s_hn2, t + 1)
                if t == 0:
                    pe.wait_ge(s_cte, 8)
                if t == 4:
                    pe.wait_ge(s_h1, NT)
                for c in range(2):
                    last = tr(bank[4 + c][:, (t % 4) * 128:(t % 4) * 128 + ROWS], hn2[0:ROWS, t, c * 128:(c + 1) * 128],
                              ident[0:ROWS, 0:ROWS])
                last.then_inc(s_ht, 1)

            def logits(half):
                pe.wait_ge(s_tab, 16)
                pe.wait_ge(s_h1, 4 * half + 4)
                pe.wait_ge(s_hte, 4 * (half + 1))
                for q in range(2 * half, 2 * half + 2):
                    for i in range(4):
                        for c in range(2):
                            last = mm(bank[6][32 * i:32 * i + 32, q * S:(q + 1) * S], gwc[:, c, :], hn2T[:, c, 4 * q + i, :],
                                      start=(c == 0), stop=(c == 1))
                last.then_inc(s_lg, 1)

            pe.wait_ge(s_tab, 16)
            pe.wait_ge(s_wm, 1)
            keep_warm(14, 0)
            for t in range(4):
                turn_x(t)
                if t >= 1:
                    project(t - 1)
            project(3)
            keep_warm(12, 0)
            for t in range(4):
                turn_z(t)
            keep_warm(4, 0)
            latents(0)
            keep_warm(2, 0)
            up(0, 0)
            turn_x(4)
            up(0, 1)
            turn_x(5)
            project(4)
            up(0, 2)
            project(5)
            turn_x(6)
            up(0, 3)
            turn_x(7)
            project(6)
            up(0, 4)
            project(7)
            turn_ckv(0)
            up(0, 5)
            up(0, 6)
            for t in range(4, NT):
                turn_z(t)
            up(0, 7)
            latents(1)
            up(1, 0)
            for t in range(4):
                scores(t)
                up(1, 2 * t + 1)
                if t >= 1:
                    turn_probs(t - 1)
                if t < 3:
                    up(1, 2 * t + 2)
            scores(4)
            turn_probs(3)
            for b in range(3):
                values(0, b)
            scores(5)
            for b in range(3, 6):
                values(0, b)
            turn_probs(4)
            scores(6)
            values(0, 6)
            values(0, 7)
            turn_probs(5)
            scores(7)
            heads(0, 0)
            heads(0, 1)
            turn_probs(6)
            for m in range(2, 5):
                heads(0, m)
            turn_probs(7)
            turn_ckv(1)
            for m in range(5, NM):
                heads(0, m)
            values(1, 0)
            turn_back(0)
            turn_back(1)
            values(1, 1)
            turn_back(2)
            turn_back(3)
            for b in range(2, HB):
                values(1, b)
            for t in range(4):
                turn_hn2(t)
            logits(0)
            def turn_pm(half):
                pe.wait_ge(s_pm, half + 1)
                for q in range(2):
                    last = tr(bank[(4, 7)[half]][0:ROWS, q * 128:(q + 1) * 128], pm_pad[half][:, q, 0:ROWS], ident[:, :])
                last.then_inc(s_pmt, 1)

            def merge(half):
                pe.wait_ge(s_pmte, half + 1)
                for q in range(2):
                    for i in range(4):
                        b, lo = HB * half + 4 * q + i, 64 * (i % 2)
                        last = mm(bank[(4, 2)[half] + q][32 * i:32 * i + 32, 0:D],
                                  pmT[half][lo:lo + S, q, 32 * i:32 * i + 32], hn2[lo:lo + S, b // 2, :], start=True, stop=True)
                last.then_inc(s_mg, 1)

            def turn_merged(half):
                pe.wait_ge(s_mge, 2 * half + 2)
                for c in range(2):
                    for q in range(2):
                        last = tr(bank[4 + c][:, q * 128:(q + 1) * 128],
                                  merged[:, 2 * half + q, c:D:2], ident[:, :])
                last.then_inc(s_mt, 1)

            def bias(it, g):
                pe.wait_ge(s_b1[g], 16 * it + 16)
                for n in range(2):
                    mm(bank[n][:, :], sel_sb[:, :], bias1[:, g, n * 512:(n + 1) * 512], start=True, stop=False,
                       skip_group_check=True)

            for m in range(4):
                heads(1, m)
            turn_pm(0)
            heads(1, 4)
            merge(0)
            heads(1, 5)
            heads(1, 6)
            turn_merged(0)
            heads(1, 7)
            for t in range(4, NT):
                turn_back(t)
            pe.wait_ge(s_sel, 16)
            bias(0, 0)
            keep_warm(6, 2)
            for t in range(4, NT):
                turn_hn2(t)
            logits(1)
            keep_warm(12, 2)
            turn_pm(1)
            keep_warm(2, 2)
            merge(1)
            keep_warm(2, 7)
            turn_merged(1)
            keep_warm(2, 7)

            def scatter(b, pm, o, start, stop):
                t, i = b // 2, b % 2
                return mm(bank[4 + t // 2][64 * i:64 * i + S, (t % 2) * D:(t % 2 + 1) * D], pm, o,
                          start=start, stop=stop, skip_group_check=True)

            def scatter_moved():
                for b in range(B):
                    scatter(b, pm_e[:, b, :], o_all[:, b % HB, :], b // 2 % 2 == 0, False)

            def scatter_direct(g, stop):
                pe.wait_ge(s_oe, NG - 1 + g + OE0)
                for b in range(B):
                    last = scatter(b, pm_last[:, g, b, :], o_sb[:, g, :], False, stop)
                    if stop and b % 4 == 3:
                        last.then_inc(s_fin, 1)

            def group(it, g, turn=None):
                if turn == 6:
                    pe.wait_ge(s_pme, 128)
                    for k in range(4):
                        half = k % 2
                        mm(bank[4 + k][:, 0:HN], last_sel[k // 2],
                           pm_e[:, HB * half:HB * (half + 1), :].rearrange("p b s -> p (b s)"),
                           start=True, stop=True).then_inc(s_rep, 1)
                pe.wait_ge(s_stage, 2 * it + g + 1)
                for c in range(2):
                    pe.wait_ge(s_w1[g][c], 16 * it + FIRST[g])
                    for n in range(2):
                        for j in range(GE):
                            last = mm(bank[n][32 * j:32 * j + 32, :], stage[:, g, c, j, :],
                                      w1_ring[:, GE * g + j, c * HID + n * 512:c * HID + (n + 1) * 512],
                                      start=False, stop=(c == 1), skip_group_check=True)
                        if c == 1:
                            last.then_inc(s_hid, 1)
                    if c == 0:
                        last.then_inc(s_w1a, 1)
                        if turn == 7:
                            scatter_direct(0, stop=False)
                pe.wait_ge(s_oe, 2 * it + g + OE0)
                keep_warm(6, 3)
                for kk in range(2):
                    if kk == 0:
                        pe.wait_ge(s_gelu, 4 * it + 2 * g + 2 + GELU0)
                    pe.wait_ge(s_the, 4 * it + 2 * g + kk + THE0)
                    for k in range(4 * kk, 4 * kk + 4):
                        last = tr(bank[2][:, (k % 4) * 128:(k % 4 + 1) * 128], hg[:, k:HID:8], ident[:, :])
                    last.then_inc(s_th, 1)
                pe.wait_ge(s_b2[g], 16 * it + 16)
                mm(bank[3][:, 0:D], sel_sb[:, :], bias2[:, g, :], start=True, stop=False, skip_group_check=True)
                for kk in range(2):
                    pe.wait_ge(s_the, 4 * it + 2 * g + kk + 1 + THE0)
                    pe.wait_ge(s_w2[g][kk], 16 * it + FIRST[g])
                    for k in range(4 * kk, 4 * kk + 4):
                        for j in range(GE):
                            last = mm(bank[3][32 * j:32 * j + 32, 0:D], hT[:, k, 32 * j:32 * j + 32],
                                      w2_ring[:, GE * g + j, k * D:(k + 1) * D], start=False, stop=(k == 7),
                                      skip_group_check=True)
                    last.then_inc((s_w2a, s_o)[kk], 1)
                    if kk == 0 and turn == 6:
                        for k in range(2):
                            pe.wait_ge(s_ob[k], 32 * GE * (NG // 2 - 1) + MOVED0)
                        pe.wait_ge(s_pml, 4)
                        scatter_moved()
                if turn != 7:
                    bias(it + g, 1 - g)

            with pe.Fori(0, NG // 2 - 1) as it:
                for g in range(2):
                    group(it, g)
            group(NG // 2 - 1, 0, turn=6)
            group(NG // 2 - 1, 1, turn=7)
            scatter_direct(1, stop=True)

        @block.vector
        def _(dve):
            v = nc.vector
            count = [0]

            def link(ins):
                count[0] += 1
                ins.then_inc(s_dve, 1)
                dve.wait_ge(s_dve, count[0])

            def mark(ins):
                count[0] += 1
                ins.then_inc(s_dve, 1)
                return count[0]

            def rsqrt(dst, src, tmp_y, tmp_a, tmp_b):
                link(v.tensor_scalar(tmp_y.bitcast(int32), src.bitcast(int32), -0.5, SEED, ALU.mult, ALU.add))
                y = tmp_y
                for step in range(3):
                    link(v.tensor_tensor(tmp_a, y, y, ALU.mult))
                    link(v.scalar_tensor_tensor(out=tmp_b, in0=tmp_a, scalar=-0.5, in1=src, op0=ALU.mult, op1=ALU.mult))
                    new = dst if step == 2 else tmp_y
                    link(v.scalar_tensor_tensor(out=new, in0=tmp_b, scalar=1.5, in1=y, op0=ALU.add, op1=ALU.mult))

            dve.sem_inc(s_the, THE0)
            dve.sem_inc(s_oe, OE0)
            for i in range(4, 8):
                v.memset(bank[i][:, :], 0.0).then_inc(s_bank, 1)
            def ternary_weights():
                link(v.tensor_scalar(tokw_sb, tokw_sb, wscale, MAGIC, ALU.mult, ALU.add))
                v.tensor_scalar(tokw_sb, tokw_sb, MAGIC + 1.0, MAGIC - 1.0, ALU.min, ALU.max).then_inc(s_wr, 1)

            def patch_scales(lo, hi):
                for t in range(lo, hi):
                    dve.wait_ge(s_x[t // 2], 16)
                    link(v.tensor_reduce(amax[0:QROWS, t:t + 1], x_sb[0:QROWS, t, :], AX.X, ALU.max, apply_absolute_value=True))
                if lo == 0:
                    dve.wait_ge(s_tab, 16)
                    v.tensor_copy(ident_b[:, :], ident[:, :]).then_inc(s_idb, 1)
                dve.wait_ge(s_ssq, hi)
                c = lambda a: a[0:QROWS, lo:hi]
                link(v.tensor_scalar(c(nv), c(ssq), 1.0 / DIN, 1e-6, ALU.mult, ALU.add))
                rsqrt(c(xr_s), c(nv), c(ny), c(na), c(nb))
                dve.sem_inc(s_xr, 1)
                link(v.tensor_tensor(c(na), c(amax), c(xr_s), ALU.mult))
                link(v.tensor_scalar(c(na), c(na), 1e-5, None, ALU.max))
                link(v.reciprocal(c(nb), c(na)))
                link(v.tensor_scalar(c(xscale), c(nb), 127.0, None, ALU.mult))
                if lo == 0:
                    dve.wait_ge(s_wsum, 1)
                    v.tensor_scalar(wmean, bank[0][:, 0:1], 1.0 / (DIN * D), 1e-5, ALU.mult, ALU.max).then_inc(s_wm, 1)
                    dve.wait_ge(s_wm, 1)
                    link(v.reciprocal(wscale, wmean))
                    link(v.reciprocal(wdq, wscale))
                link(v.reciprocal(c(nb), c(xscale)))
                link(v.tensor_scalar(c(dq), c(nb), wdq[0:QROWS, :], maskc[0:QROWS, :], ALU.mult, ALU.mult))

            def quantise(t):
                if t >= 2:
                    dve.wait_ge(s_xt, t - 1)
                link(v.tensor_scalar(x_sb[0:QROWS, t, :], x_sb[0:QROWS, t, :], xr_s[0:QROWS, t:t + 1],
                                     xscale[0:QROWS, t:t + 1], ALU.mult, ALU.mult))
                v.tensor_scalar(xq[0:QROWS, t % 2, :], x_sb[0:QROWS, t, :], MAGIC, -MAGIC,
                                ALU.add, ALU.add).then_inc(s_xq, 1)

            def shift_x(t):
                dve.wait_ge(s_xs, t - 2)
                v.tensor_scalar(x_sb[0:QROWS, t, :], x_sb[0:QROWS, t, :], xscale[0:QROWS, t:t + 1], MAGIC,
                                ALU.mult, ALU.add).then_inc(s_xm, 1)

            def tokens(lo, hi):
                for t in range(lo, hi + 1):
                    if t < hi:
                        dve.wait_ge(s_proj, t + 1)
                        if t == 0:
                            dve.wait_ge(s_wabs, 1)
                        v.scalar_tensor_tensor(out=h0[0:ROWS, t, :], in0=bank[6 + t % 2][0:ROWS, 0:D],
                                               scalar=dq[0:ROWS, t:t + 1], in1=base[0:ROWS, :],
                                               op0=ALU.mult, op1=ALU.add).then_inc(s_tok, 1)
                    if t > lo:
                        dve.wait_ge(s_tok, t)
                        link(v.bn_stats(bst[0:ROWS, t % 4, :], h0[0:ROWS, t - 1, :]))
                        v.bn_aggr(mv[0:ROWS, t - 1, :], bst[0:ROWS, t % 4, :]).then_inc(s_h0, 1)

            def norms(half):
                dve.wait_ge(s_h0, 4 * half + 4)
                var = mv[0:ROWS, 4 * half:4 * half + 4, 1]
                nv1, nv2 = nvv[0:ROWS, 0, :], nvv[0:ROWS, 1, :]
                link(v.tensor_scalar(nv1, var, LN_EPS, None, ALU.add))
                link(v.scalar_tensor_tensor(out=nv2, in0=nv1, scalar=LN_EPS, in1=var, op0=ALU.mult, op1=ALU.add))
                c = lambda a: a[0:ROWS, :]
                rsqrt(c(rr), c(nv), c(ny), c(na), c(nb))
                if half:
                    dve.wait_ge(s_hn, 4)
                v.tensor_copy(fac[0:ROWS, 0, :], rr[0:ROWS, 0:4]).then_inc(s_nm, 1)
                v.scalar_tensor_tensor(out=fac[0:ROWS, 1, :], in0=mv[0:ROWS, 4 * half:4 * half + 4, 0], scalar=-1.0,
                                       in1=rr[0:ROWS, 0:4], op0=ALU.mult, op1=ALU.mult).then_inc(s_nm, 1)
                for t in range(4 * half, 4 * half + 4):
                    j = t % 4
                    v.tensor_scalar(z[0:ROWS, t, :], h0[0:ROWS, t, :], mv[0:ROWS, t, 0:1], rr[0:ROWS, 4 + j:5 + j],
                                    ALU.subtract, ALU.mult).then_inc(s_z, 1)

            cos_v = rope_sb[:, 0:S].unsqueeze(1).broadcast_to([128, HB, S])
            sin_v = rope_sb[:, S:2 * S].unsqueeze(1).broadcast_to([128, HB, S])

            def rope_products(half, m):
                n = half * NM + m
                for u in range(2):
                    dve.wait_ge(s_up, 2 * n + u + 1)
                    if n >= 2:
                        dve.wait_ge(s_rot, rotated(n - 2) if u else rotated_q(n - 2))
                    for j, (dst, table) in enumerate(((rope_a[n % 2], cos_v), (rope_b[n % 2], sin_v))):
                        v.tensor_tensor(dst[:, u, :].rearrange("p (b s) -> p b s", b=HB),
                                        bank[2 * u + j][:, 0:HN].rearrange("p (b s) -> p b s", b=HB), table,
                                        ALU.mult).then_inc(s_prod, 1)

            def rotate_second(m):
                n = NM + m
                dve.wait_ge(s_prod, 4 * n + 4)
                v.tensor_tensor(k_bd[1][64:128, m, 1, :], rope_a[n % 2][64:128, 1, :],
                                rope_b[n % 2][64:128, 1, :], ALU.add).then_inc(s_rotd, 1)

            def shift(t):
                for g in range(2):
                    dve.wait_ge(s_sc, 2 * t + g + 1)
                    src = bank[4 + g][0:ROWS, 0:4 * 2 * S].rearrange("p (h k) -> p h k", k=S)
                    link(v.tensor_reduce(smax[0:ROWS, t % 2, 8 * g:8 * g + 8], src, AX.X, ALU.max))
                    if g == 0 and t >= 2:
                        dve.wait_ge(s_pt, 2 * (t - 2) + 2)
                    p = prob[0:ROWS, t % 2, 4 * g:4 * g + 4, :].rearrange("p m (i k) -> p (m i) k", i=2)[:, :, 0:S]
                    v.tensor_tensor(p, src, smax[0:ROWS, t % 2, 8 * g:8 * g + 8].unsqueeze(2).broadcast_to([ROWS, 8, S]),
                                    ALU.subtract).then_inc(s_sub, 1)

            def row_sums(t):
                dve.wait_ge(s_exp, t + 1)
                if t >= 2:
                    dve.wait_ge(s_pn, t - 1)
                p = prob[0:ROWS, t % 2, :, :].rearrange("p m (i k) -> p (m i) k", i=2)[:, :, 0:S]
                link(v.tensor_reduce(ssum[0:ROWS, t % 2, :], p, AX.X, ALU.add))
                v.reciprocal(ssum[0:ROWS, t % 2, :], ssum[0:ROWS, t % 2, :]).then_inc(s_rs, 1)

            def z_odd_out(half, b):
                if b == 0:
                    if half:
                        dve.wait_ge(s_oo, NM)
                    else:
                        dve.wait_ge(s_res, NT)
                dve.wait_ge(s_zz, half * B + 2 * b + 2)
                v.tensor_copy(ZT[:, 1, :, b * S:(b + 1) * S],
                              bank[1 + 2 * (b % 2)][:, 0:HN].rearrange("p (m s) -> p m s", m=NM)).then_inc(s_ze1, 1)

            def attn_out(half):
                dve.wait_ge(s_otm, NM * (half + 1))
                dve.wait_ge(s_gap, 2)
                if half:
                    dve.wait_ge(s_bk, 4)
                v.tensor_copy(aoT[:, 0, :].rearrange("p (b s) -> p b s", b=HB)[:, :, 0:S],
                              bank[2][:, 0:HN].rearrange("p (b s) -> p b s", b=HB)).then_inc(s_ote, 1)

            def h1_out(t):
                dve.wait_ge(s_bk, t + 1)
                dve.wait_ge(s_res, NT)
                v.tensor_tensor(resid[0:ROWS, t, :], bank[BACK[t]][0:ROWS, 0:D], resid[0:ROWS, t, :],
                                ALU.add).then_inc(s_h1, 1)

            def h1_stats(half):
                for t in range(4 * half, 4 * half + 4):
                    dve.wait_ge(s_h1, t + 1)
                    last = mark(v.bn_stats(bst[0:ROWS, t % 4, :], resid[0:ROWS, t, :]))
                for t in range(4 * half, 4 * half + 4):
                    dve.wait_ge(s_dve, last - 3 + t % 4)
                    end = mark(v.bn_aggr(mv[0:ROWS, t, :], bst[0:ROWS, t % 4, :]))
                dve.wait_ge(s_dve, end)

            def norm3(half):
                c = lambda a: a[0:ROWS, 4 * half:4 * half + 4]
                link(v.tensor_scalar(c(nv), mv[0:ROWS, 4 * half:4 * half + 4, 1], LN_EPS, None, ALU.add))
                rsqrt(c(r1), c(nv), c(ny), c(na), c(nb))

            def hn2_out(t):
                if t == 0:
                    dve.wait_ge(s_pt, 2 * NT)
                v.tensor_scalar(hn2[0:ROWS, t, :], resid[0:ROWS, t, :], mv[0:ROWS, t, 0:1], r1[0:ROWS, t:t + 1],
                                ALU.subtract, ALU.mult).then_inc(s_hn2, 1)

            def hn2_turned_out(half):
                dve.wait_ge(s_ct, 4)
                dve.wait_ge(s_ht, 4 * half + 4)
                turned_out(v.tensor_copy, half, 1)

            def router_shift(half):
                ex, mx = r_ex[:, 2 * half:2 * half + 2, :], rq[:, 2 * half:2 * half + 2]
                dve.wait_ge(s_lg, half + 1)
                dve.wait_ge(s_tab, 16)
                link(v.tensor_scalar(ex, bank[6][:, 2 * half * S:2 * (half + 1) * S].rearrange("p (q s) -> p q s", q=2),
                                     gbc[:, :], None, ALU.add))
                link(v.tensor_reduce(mx, ex, AX.X, ALU.max))
                v.tensor_tensor(ex, ex, mx.unsqueeze(2).broadcast_to([128, 2, S]), ALU.subtract).then_inc(s_rsub, 1)

            def router_pick(half):
                ex, sm = r_ex[:, 2 * half:2 * half + 2, :], rq[:, 2 * half:2 * half + 2]
                dve.wait_ge(s_rexp, half + 1)
                link(v.tensor_reduce(sm, ex, AX.X, ALU.add))
                link(v.reciprocal(sm, sm))
                link(v.tensor_tensor(ex, ex, sm.unsqueeze(2).broadcast_to([128, 2, S]), ALU.mult))
                for q in range(2 * half, 2 * half + 2):
                    link(v.max(top8[:, q, :], r_ex[:, q, :]))
                for q in range(2 * half, 2 * half + 2):
                    link(v.match_replace(r_keep[:, q, :], in_to_replace=top8[:, q, :], in_values=r_ex[:, q, :], imm_value=0.0))

            def pm_out(half):
                dve.wait_ge(s_pool1, (2, 3)[half])
                r = slice(2 * half, 2 * half + 2)
                for i in range(2):
                    v.tensor_tensor(pm_pad[half][:, :, 64 * i:64 * i + NPATCH], r_ex[:, r, 1:S], r_keep[:, r, 1:S], ALU.subtract)
                    last = v.tensor_tensor(pm_pad[half][:, :, 64 * i + NPATCH:64 * i + S], r_ex[:, r, 0:1], r_keep[:, r, 0:1],
                                           ALU.subtract)
                last.then_inc(s_pm, 1)

            def merged_out(half):
                dve.wait_ge(s_mg, half + 1)
                v.tensor_copy(merged[:, 2 * half + 1, :], bank[(5, 3)[half]][:, 0:D]).then_inc(s_mge, 1)

            def merged_turned_out(half):
                dve.wait_ge(s_mt, half + 1)
                dve.wait_ge(s_pool1, 2)
                v.tensor_copy(mT[:, 0, :, HB * half:HB * (half + 1)].rearrange("p e b -> p b e"),
                              bank[4][:, 0:256].rearrange("p (b e) -> p b e", b=HB)).then_inc(s_mte, 1)

            patch_scales(0, 4)
            ternary_weights()
            quantise(0)
            quantise(1)
            quantise(2)
            shift_x(3)
            dve.wait_ge(s_base, 16)
            link(v.tensor_tensor(base[0:ROWS, :], base[0:ROWS, :], cls_sb[0:ROWS, :], ALU.add))
            tokens(0, 4)
            norms(0)
            patch_scales(4, 8)
            shift_x(4)
            shift_x(5)
            rope_products(0, 0)
            rope_products(0, 1)
            shift_x(6)
            rope_products(0, 2)
            shift_x(7)
            tokens(4, 5)
            rope_products(0, 3)
            tokens(5, 6)
            rope_products(0, 4)
            tokens(6, 8)
            rope_products(0, 5)
            norms(1)
            rope_products(0, 6)
            rope_products(0, 7)
            rope_products(1, 0)
            for t in range(4):
                shift(t)
                rope_products(1, 2 * t + 1)
                row_sums(t)
                rotate_second(2 * t + 1)
                if t < 3:
                    rope_products(1, 2 * t + 2)
            shift(4)
            for b in range(3):
                z_odd_out(0, b)
            row_sums(4)
            shift(5)
            for b in range(3, 6):
                z_odd_out(0, b)
            row_sums(5)
            shift(6)
            z_odd_out(0, 6)
            z_odd_out(0, 7)
            row_sums(6)
            shift(7)
            row_sums(7)
            attn_out(0)
            z_odd_out(1, 0)
            h1_out(0)
            h1_out(1)
            z_odd_out(1, 1)
            h1_out(2)
            h1_out(3)
            h1_stats(0)
            z_odd_out(1, 2)
            norm3(0)
            z_odd_out(1, 3)
            hn2_out(0)
            hn2_out(1)
            z_odd_out(1, 4)
            hn2_out(2)
            hn2_out(3)
            for b in range(5, HB):
                z_odd_out(1, b)
            hn2_turned_out(0)
            router_shift(0)
            router_pick(0)
            pm_out(0)
            merged_out(0)
            merged_turned_out(0)
            attn_out(1)
            for t in range(4, NT):
                h1_out(t)
            h1_stats(1)
            norm3(1)
            for t in range(4, NT):
                hn2_out(t)
            hn2_turned_out(1)
            router_shift(1)
            router_pick(1)
            pm_out(1)
            merged_out(1)
            merged_turned_out(1)
            dve.wait_ge(s_mte, 4)

            def stage_tokens(it, g):
                dve.wait_ge(s_hid, 4 * it + 2 * g - 2 + HID0)
                v.tensor_copy(stage[:, g, :, :, :], mT[:, :, bass.ds(it * SLOTS + GE * g, GE), :]).then_inc(s_stage, 1)

            def group(it, g, turn=None):
                if turn == 6:
                    for k in range(4):
                        half = k % 2
                        dve.wait_ge(s_rep, k + 1)
                        v.tensor_tensor(pm_last[:, k // 2, HB * half:HB * (half + 1), :],
                                        bank[4 + k][:, 0:HN].rearrange("p (b s) -> p b s", b=HB),
                                        image_mask[:, HB * half:HB * (half + 1)].unsqueeze(2).broadcast_to([128, HB, S]),
                                        ALU.mult).then_inc(s_pml, 1)
                for k in range(2):
                    if k == 0:
                        dve.wait_ge(s_o, 2 * it + g + O0)
                    dve.wait_ge(s_th, 4 * it + 2 * g + k + 1)
                    v.tensor_copy(hT[:, 4 * k:4 * k + 4, :].rearrange("p k n -> p (k n)"),
                                  bank[2][:, :]).then_inc(s_the, 1)
                if turn != 7:
                    stage_tokens(it + g, 1 - g)
                dve.wait_ge(s_ob[g], 32 * GE * it + MOVED0)
                dve.wait_ge(s_o, 2 * it + g + 1 + O0)
                v.tensor_copy(o_sb[:, g, :], bank[3][:, 0:D]).then_inc(s_oe, 1)

            stage_tokens(0, 0)
            with dve.Fori(0, NG // 2 - 1) as it:
                for g in range(2):
                    group(it, g)
            group(NG // 2 - 1, 0, turn=6)
            group(NG // 2 - 1, 1, turn=7)

            for p in range(NT // 2):
                dve.wait_ge(s_fin, p + 1)
                r = resid[0:ROWS, 2 * p:2 * p + 2, :].rearrange("p t n -> p (t n)")
                v.tensor_tensor(r, bank[4 + p][0:ROWS, :], r, ALU.add).then_inc(s_fout, 1)


def move_out(act, gr, s_oe, o_all, o_sb, s_ob):
    g = gr % 2
    act.wait_ge(s_oe, gr + 1 + OE0)
    for j in range(GE):
        for half in range(2):
            row = 64 * half + GE * gr + j
            act.dma_start(o_all[row:row + 1, :, :],
                          o_sb[32 * j + HB * half:32 * j + HB * (half + 1), g, :]).then_inc(s_ob[g], 16)


def rope_table():
    inv_freq = 1.0 / 10000.0 ** (np.arange(0, DH, 2, dtype=np.float32) / DH)
    freqs = np.outer(np.arange(S, dtype=np.float32), inv_freq)
    cos = np.concatenate([np.cos(freqs), np.cos(freqs)], -1)[:, ::2]
    sin = np.concatenate([np.sin(freqs), np.sin(freqs)], -1)[:, ::2]
    order = np.r_[1:S, 0]
    cos, sin = cos[order].T, sin[order].T
    return np.concatenate([np.tile(cos, (4, 1)), np.tile(np.concatenate([-sin, sin]), (2, 1))], 1).astype(np.float32)


def head_order():
    even, odd = np.arange(0, DH, 2), np.arange(1, DH, 2)
    one = np.concatenate([even, odd, even])
    return (np.arange(H)[:, None] * DH + one).ravel()


def kernel(**inputs):
    from concourse import bacc
    from concourse.bass_utils import run_bass_kernel_spmd

    a = {k: np.asarray(v) for k, v in inputs.items()}
    patches = a["x"].reshape(NT, 2, C, GRID, P, GRID, P).transpose(1, 3, 5, 0, 4, 6, 2).reshape(2, NPATCH, NT, DIN)
    x = np.zeros((XROWS, NT, DIN), patches.dtype)
    x[0:NPATCH], x[64:64 + NPATCH] = patches
    tokw = a["L0_tok_weight"].T.reshape(KC, 128, D).transpose(1, 0, 2).reshape(128, KC * D)
    posr = np.zeros((128, 2 * D), np.float32)
    posr[:, 0:D] = a["L0_tok_pos_embedding"].reshape(1, D)
    posr[[NPATCH, 64 + NPATCH], D:] = a["L0_tok_class_token"].reshape(D)
    wd = np.concatenate([a["L0_attn_w_down_q"], a["L0_attn_w_down_kv"]]).T.reshape(2, 128, 2 * DL).transpose(1, 0, 2)
    order = head_order()
    mask = np.zeros((128, 1), np.float32)
    mask[0:NPATCH] = mask[64:64 + NPATCH] = 1.0
    sel = np.zeros((128, SELS), np.float32)
    for j in range(GE):
        sel[j, 32 * j:32 * j + B] = 1.0
        for k in range(2):
            e = E - (2 - k) * GE + j
            sel[[[e], [64 + e]], 128 * (k + 1) + 32 * j + np.arange(B)] = 1.0
        sel[32 * j + np.arange(B), 384 + np.arange(B)] = 1.0
    tables = np.concatenate([
        np.eye(128, dtype=np.float32), a["L0_ffn_gate_w"].T.reshape(2, 128, E).transpose(1, 0, 2).reshape(128, 2 * E),
        rope_table(), a["L0_attn_ln_scale"].reshape(2, 128).T, a["L0_attn_ln_bias"].reshape(2, 128).T,
        np.tile(a["L0_ffn_gate_b"], 4).reshape(128, 1), mask, np.full((128, 1), -MAGIC, np.float32)], 1)
    arrays = dict(
        x=x, tokw=tokw, tables=tables, posr=posr, wd=wd,
        wup=np.concatenate([a["L0_attn_w_up_q"][order].T, a["L0_attn_w_up_k"][order].T], 1),
        wvo=np.concatenate([a["L0_attn_w_up_v"].T,
                            a["L0_attn_w_out"].T.reshape(NM, 128, D).transpose(1, 0, 2).reshape(128, NM * D)], 1),
        w1=a["L0_ffn_w1"], w2=a["L0_ffn_w2"], sel=sel,
    )
    arrays = {k: np.ascontiguousarray(v) for k, v in arrays.items()}
    nc = bacc.Bacc("TRN2", target_bir_lowering=False, num_devices=1)
    args = {k: nc.dram_tensor(f"in_{k}", v.shape, mybir.dt.from_np(v.dtype), kind="ExternalInput").ap() for k, v in arrays.items()}
    out = nc.dram_tensor("out_0", (XROWS, NT, D), fp32, kind="ExternalOutput").ap()
    vit_tower(nc, out=out, **args)
    r = run_bass_kernel_spmd(nc, [{f"in_{k}": v for k, v in arrays.items()}], core_ids=[0])
    o = r.results[0]["out_0"]
    o = np.stack([o[0:S], o[64:64 + S]]).transpose(2, 0, 1, 3).reshape(B, S, D)
    return np.concatenate([o[:, NPATCH:], o[:, :NPATCH]], 1)
```
